# Optimizing a Trainium2 kernel written in Bass

```python
import numpy as np
import jax
import jax.numpy as jnp

def _softmax(x, axis=-1):
    return jax.nn.softmax(x, axis=axis)

def _gelu(x):
    return jax.nn.gelu(x, approximate=True)

def _silu(x):
    return jax.nn.silu(x)

def _sigmoid(x):
    return jax.nn.sigmoid(x)

def _layernorm(x, axis=-1, eps=1e-05):
    m = jnp.mean(x, axis=axis, keepdims=True)
    v = jnp.var(x, axis=axis, keepdims=True)
    return (x - m) / jnp.sqrt(v + eps)

def _scatter_add(tgt, idx, src, axis=0):
    return tgt.at[idx].add(src)

def _segment_sum(src, seg, n):
    return jax.ops.segment_sum(src, seg, n)
kernel_name = 'mk_macaron_d1_jaxref_r8_8ca1bd'

def setup_inputs(seed: int=0):
    np.random.seed(seed)
    _w = jnp.asarray

    def _L0_attn_setup():
        import jax, jax.numpy as jnp
        import numpy as np
        B, T, HID = (2, 512, 256)
        H, K = (16, 128)
        BS = 64
        EPS = 1e-06
        SCALING = K ** (-0.5)
        key = jax.random.key(seed)
        ks = jax.random.split(key, 8)
        sin = HID ** (-0.5)
        sout = (H * K) ** (-0.5)
        return {'x': jax.random.normal(ks[0], (B, T, HID), jnp.float32), 'Wq': jax.random.normal(ks[1], (HID, H * K), jnp.float32) * sin, 'Wk': jax.random.normal(ks[2], (HID, H * K), jnp.float32) * sin, 'Wv': jax.random.normal(ks[3], (HID, H * K), jnp.float32) * sin, 'phi_scale': 1.0 + 0.1 * jax.random.normal(ks[4], (H, 1, K), jnp.float32), 'phi_bias': 0.1 * jax.random.normal(ks[5], (H, 1, K), jnp.float32), 'Wo': jax.random.normal(ks[6], (H * K, HID), jnp.float32) * sout, 'bo': jnp.zeros((HID,), jnp.float32)}
    _L0_attn_in = _L0_attn_setup()

    def _L0_ffn_setup():
        import jax, jax.numpy as jnp
        import numpy as np
        B, S, D = (2, 256, 256)
        H, HD = (16, 128)
        E, K, I = (16, 6, 176)
        SI = 352
        EPS = 1e-06

        def rmsnorm(x, w):
            v = jnp.mean(jnp.square(x), axis=-1, keepdims=True)
            return x * jax.lax.rsqrt(v + EPS) * w
        key = jax.random.key(seed)
        ks = jax.random.split(key, 14)
        s = 0.02
        return {'hidden_states': jax.random.normal(ks[0], (B, S, D), jnp.float32), 'ln1_w': jnp.ones((D,), jnp.float32), 'ln2_w': jnp.ones((D,), jnp.float32), 'wq': jax.random.normal(ks[1], (D, H * HD), jnp.float32) * s, 'wk': jax.random.normal(ks[2], (D, H * HD), jnp.float32) * s, 'wv': jax.random.normal(ks[3], (D, H * HD), jnp.float32) * s, 'wo': jax.random.normal(ks[4], (H * HD, D), jnp.float32) * s, 'gate_w': jax.random.normal(ks[5], (E, D), jnp.float32) * s, 'eg_w': jax.random.normal(ks[6], (E, I, D), jnp.float32) * s, 'eu_w': jax.random.normal(ks[7], (E, I, D), jnp.float32) * s, 'ed_w': jax.random.normal(ks[8], (E, D, I), jnp.float32) * s, 'sg_w': jax.random.normal(ks[9], (SI, D), jnp.float32) * s, 'su_w': jax.random.normal(ks[10], (SI, D), jnp.float32) * s, 'sd_w': jax.random.normal(ks[11], (D, SI), jnp.float32) * s}
    _L0_ffn_in = _L0_ffn_setup()
    _d = {'L0_attn_x': _L0_attn_in['x'], 'L0_attn_Wq': _L0_attn_in['Wq'], 'L0_attn_Wk': _L0_attn_in['Wk'], 'L0_attn_Wv': _L0_attn_in['Wv'], 'L0_attn_phi_scale': _L0_attn_in['phi_scale'], 'L0_attn_phi_bias': _L0_attn_in['phi_bias'], 'L0_attn_Wo': _L0_attn_in['Wo'], 'L0_attn_bo': _L0_attn_in['bo'], 'L0_ffn_ln1_w': _L0_ffn_in['ln1_w'], 'L0_ffn_ln2_w': _L0_ffn_in['ln2_w'], 'L0_ffn_wq': _L0_ffn_in['wq'], 'L0_ffn_wk': _L0_ffn_in['wk'], 'L0_ffn_wv': _L0_ffn_in['wv'], 'L0_ffn_wo': _L0_ffn_in['wo'], 'L0_ffn_gate_w': _L0_ffn_in['gate_w'], 'L0_ffn_eg_w': _L0_ffn_in['eg_w'], 'L0_ffn_eu_w': _L0_ffn_in['eu_w'], 'L0_ffn_ed_w': _L0_ffn_in['ed_w'], 'L0_ffn_sg_w': _L0_ffn_in['sg_w'], 'L0_ffn_su_w': _L0_ffn_in['su_w'], 'L0_ffn_sd_w': _L0_ffn_in['sd_w']}
    _x0 = _d['L0_attn_x']
    _d['L0_attn_x'] = jax.random.normal(jax.random.fold_in(jax.random.key(seed), 1), (4, 512, 256), dtype=_x0.dtype)
    del _x0
    return _d

def reference(L0_attn_x, L0_attn_Wq, L0_attn_Wk, L0_attn_Wv, L0_attn_phi_scale, L0_attn_phi_bias, L0_attn_Wo, L0_attn_bo, L0_ffn_ln1_w, L0_ffn_ln2_w, L0_ffn_wq, L0_ffn_wk, L0_ffn_wv, L0_ffn_wo, L0_ffn_gate_w, L0_ffn_eg_w, L0_ffn_eu_w, L0_ffn_ed_w, L0_ffn_sg_w, L0_ffn_su_w, L0_ffn_sd_w):

    def _L0_attn_ref(x, Wq, Wk, Wv, phi_scale, phi_bias, Wo, bo):
        import jax, jax.numpy as jnp
        import numpy as np
        B, T, HID = (2, 512, 256)
        H, K = (16, 128)
        BS = 64
        EPS = 1e-06
        SCALING = K ** (-0.5)
        b, t, _ = x.shape
        nb = t // BS
        dt = x.dtype

        def proj(W):
            return (x @ W).reshape(b, t, H, K).transpose(0, 2, 1, 3).reshape(b, H, nb, BS, K)
        q_b, k_b, v_b = (proj(Wq), proj(Wk), proj(Wv))
        scores = jnp.einsum('bhntk,bhnsk->bhnts', q_b, k_b) * SCALING
        attn = jax.nn.softmax(scores.astype(jnp.float32), axis=-1).astype(dt)
        local = jnp.einsum('bhnts,bhnsk->bhntk', attn, v_b)
        ps = phi_scale[None, :, None]
        pb = phi_bias[None, :, None]
        phi = lambda z: jnp.clip(jax.nn.elu(z * ps + pb) + 1.0, 0.0, 10.0)
        phi_q = phi(q_b)
        phi_k = phi(k_b)
        pk_s = jnp.moveaxis(phi_k, 2, 0).astype(jnp.float32)
        pq_s = jnp.moveaxis(phi_q, 2, 0).astype(jnp.float32)
        v_s = jnp.moveaxis(v_b, 2, 0).astype(jnp.float32)

        def step(carry, xs):
            S, Z = carry
            pk, vn, pq = xs
            S = S + jnp.einsum('bhtk,bhtv->bhkv', pk, vn)
            Z = Z + pk.sum(axis=-2)
            num = jnp.einsum('bhtk,bhkv->bhtv', pq, S)
            den = jnp.maximum(jnp.einsum('bhtk,bhk->bht', pq, Z), EPS)[..., None]
            return ((S, Z), (num / den).astype(dt))
        S0 = jnp.zeros((b, H, K, K), jnp.float32)
        Z0 = jnp.zeros((b, H, K), jnp.float32)
        _, glob = jax.lax.scan(step, (S0, Z0), (pk_s, v_s, pq_s))
        glob = jnp.moveaxis(glob, 0, 2)
        hybrid = (local + glob).reshape(b, H, t, K).transpose(0, 2, 1, 3).reshape(b, t, H * K)
        return hybrid @ Wo + bo

    def _L0_ffn_ref(hidden_states, ln1_w, ln2_w, wq, wk, wv, wo, gate_w, eg_w, eu_w, ed_w, sg_w, su_w, sd_w):
        import jax, jax.numpy as jnp
        import numpy as np
        B, S, D = (2, 256, 256)
        H, HD = (16, 128)
        E, K, I = (16, 6, 176)
        SI = 352
        EPS = 1e-06

        def rmsnorm(x, w):
            v = jnp.mean(jnp.square(x), axis=-1, keepdims=True)
            return x * jax.lax.rsqrt(v + EPS) * w
        b, s, d = hidden_states.shape
        x = hidden_states
        h = rmsnorm(x, ln1_w)
        q = (h @ wq).reshape(b, s, H, HD)
        k = (h @ wk).reshape(b, s, H, HD)
        v = (h @ wv).reshape(b, s, H, HD)
        scores = jnp.einsum('bqhd,bkhd->bhqk', q, k) / np.sqrt(HD).astype(np.float32)
        causal = jnp.tril(jnp.ones((s, s), bool))
        scores = jnp.where(causal, scores, jnp.float32(-1000000000.0))
        attn = jax.nn.softmax(scores, axis=-1)
        ao = jnp.einsum('bhqk,bkhd->bqhd', attn, v).reshape(b, s, H * HD) @ wo
        x = x + ao
        h = rmsnorm(x, ln2_w)
        t = h.reshape(-1, d)
        T = t.shape[0]
        logits = t @ gate_w.T
        probs = jax.nn.softmax(logits, axis=-1)
        topv, topi = jax.lax.top_k(probs, K)
        topv = topv / jnp.sum(topv, axis=-1, keepdims=True)
        cw = jnp.zeros((T, E), t.dtype).at[jnp.arange(T)[:, None], topi].add(topv)
        g = jnp.einsum('td,eid->eti', t, eg_w)
        u = jnp.einsum('td,eid->eti', t, eu_w)
        hh = jax.nn.silu(g) * u
        routed = jnp.einsum('eti,edi,te->td', hh, ed_w, cw)
        shared = jax.nn.silu(t @ sg_w.T) * (t @ su_w.T) @ sd_w.T
        out = x + (routed + shared).reshape(b, s, d)
        return out
    x = L0_attn_x
    x = x + 0.5 * _L0_ffn_ref(_layernorm(x, axis=-1), L0_ffn_ln1_w, L0_ffn_ln2_w, L0_ffn_wq, L0_ffn_wk, L0_ffn_wv, L0_ffn_wo, L0_ffn_gate_w, L0_ffn_eg_w, L0_ffn_eu_w, L0_ffn_ed_w, L0_ffn_sg_w, L0_ffn_su_w, L0_ffn_sd_w)
    x = x + _L0_attn_ref(_layernorm(x, axis=-1), L0_attn_Wq, L0_attn_Wk, L0_attn_Wv, L0_attn_phi_scale, L0_attn_phi_bias, L0_attn_Wo, L0_attn_bo)
    x = x + 0.5 * _L0_ffn_ref(_layernorm(x, axis=-1), L0_ffn_ln1_w, L0_ffn_ln2_w, L0_ffn_wq, L0_ffn_wk, L0_ffn_wv, L0_ffn_wo, L0_ffn_gate_w, L0_ffn_eg_w, L0_ffn_eu_w, L0_ffn_ed_w, L0_ffn_sg_w, L0_ffn_su_w, L0_ffn_sd_w)
    return x

_drawn_inputs = setup_inputs


def setup_inputs(seed=0):
    import zlib

    import numpy as np

    out = dict(_drawn_inputs(seed))
    spreads = {'L0_attn_bo': (0.0, 0.1), 'L0_ffn_ln1_w': (1.0, 0.6), 'L0_ffn_ln2_w': (1.0, 0.6)}
    factors = {'L0_attn_phi_scale': 8.0,
     'L0_attn_phi_bias': 8.0,
     'L0_ffn_wq': 8.0,
     'L0_ffn_wk': 8.0,
     'L0_ffn_gate_w': 8.0,
     'L0_ffn_eg_w': 8.0,
     'L0_ffn_eu_w': 8.0,
     'L0_ffn_ed_w': 8.0,
     'L0_ffn_sg_w': 4.436,
     'L0_ffn_su_w': 4.375,
     'L0_ffn_sd_w': 4.35}
    for name, (base, spread) in spreads.items():
        noise = np.random.default_rng([zlib.crc32(name.encode()), seed]).standard_normal(out[name].shape)
        drawn = base * np.exp(spread * noise) if base else spread * noise
        out[name] = jnp.asarray(drawn.astype(out[name].dtype))
    for name, factor in factors.items():
        out[name] = (out[name] * factor).astype(out[name].dtype)
    return out
```

```python
from contextlib import ExitStack, contextmanager

import concourse.bass as bass
from concourse import mybir

F32 = mybir.dt.float32
F32R = mybir.dt.float32r
BF16 = mybir.dt.bfloat16
ALU = mybir.AluOpType
ACT = mybir.ActivationFunctionType
AX = mybir.AxisListType

P = 128
SEQS, SEQ, D = 4, 512, 256
TOKENS = SEQS * SEQ
TILES = TOKENS // P
TPS = SEQ // P
KT = D // P
HEADS, HD = 16, 128
GROUP = 4
GROUPS = HEADS // GROUP
GW = GROUP * HD
STEPS = SEQS * GROUP
EXPERTS, TOPK, INNER, SHARED = 16, 6, 176, 352
CHUNKS = -(-(EXPERTS * INNER + SHARED) // P)
CPG = 5
CHUNK_GROUPS = CHUNKS // CPG
UNITS = SEQS * CPG
CW_ROWS = 3 * (EXPERTS + 1)
LN_EPS, RMS_EPS, DEN_EPS = 1e-5, 1e-6, 1e-6
SCALE = float(HD) ** -0.5
WIDTH = [P * (i + 1) for i in range(TPS)]
E_AT = [sum(WIDTH[:i]) for i in range(TPS)]
E_ALL = sum(WIDTH)
DOWN = list(range(TPS - 1, -1, -1))


@contextmanager
def phase_semaphores(nc):
    held = []

    def new_sem(name):
        held.append(nc.alloc_semaphore(name=name))
        return held[-1]

    yield new_sem
    nc.clear_and_free_semaphores(held)
    nc.all_engine_barrier()


def product(pe, out, a_hi, a_lo, b_hi, b_lo, first, last, shared_bank=False):
    pe.matmul(out, a_hi, b_hi, start=first, stop=False, skip_group_check=shared_bank)
    pe.matmul(out, a_hi, b_lo, start=False, stop=False, skip_group_check=shared_bank)
    return pe.matmul(out, a_lo, b_hi, start=False, stop=last, skip_group_check=shared_bank)


def norm_phase(nc, tag, src, ln_out, rms, weight, hT_hi, hT_lo, ident, loads=None, add_row=None):
    with ExitStack() as ctx:
        new_sem = ctx.enter_context(phase_semaphores(nc))

        def sb(name, shape, dt=F32):
            return ctx.enter_context(nc.sbuf_tensor(f"{tag}_{name}", shape, dt))

        def sem(name):
            return new_sem(f"{tag}_{name}")

        z = sb("z", [P, TILES, D])
        stats = sb("stats", [P, TILES, 6])
        mv = sb("mv", [P, TILES, 2])
        small = sb("small", [P, 6, TILES])
        var, std, rstd, ms, rms_std, rrms = (small[:, i, :] for i in range(6))
        squares = sb("squares", [P, TILES])
        BANKS = 4
        tp = ctx.enter_context(nc.psum_tensor(f"{tag}_tp", [P, BANKS, 512], F32))

        loaded = sem("loaded")
        stats_done = sem("stats_done")
        aggr_done = sem("aggr_done")
        var_ready = sem("var_ready")
        std_ready = sem("std_ready")
        rstd_ready = sem("rstd_ready")
        normed = sem("normed")
        squared = sem("squared")
        ms_ready = sem("ms_ready")
        rms_std_ready = sem("rms_std_ready")
        rrms_ready = sem("rrms_ready")
        z_ready = sem("z_ready")
        turned = sem("turned")
        hi_done = sem("hi_done")
        split_done = sem("split_done")
        block = ctx.enter_context(nc.Block())

        ln = ln_out is not None
        ln_dst = ln_out if rms else z
        n_loads = len(loads or [])

        @block.sync
        def _(sp):
            for dst, src_dram in loads or []:
                sp.dma_start(dst, src_dram).then_inc(loaded, 16)
            if n_loads:
                sp.wait_ge(loaded, 16 * n_loads)

        @block.vector
        def _(dve):
            dve.sem_inc(split_done, BANKS)
            if n_loads:
                dve.wait_ge(loaded, 16 * n_loads)
            if ln:
                for t in range(TILES):
                    dve.bn_stats(stats[:, t, :], src[:, t, :]).then_inc(stats_done, 1)
                for t in range(TILES):
                    dve.wait_ge(stats_done, t + 1)
                    dve.bn_aggr(mv[:, t, :], stats[:, t, :]).then_inc(aggr_done, 1)
                dve.wait_ge(aggr_done, TILES)
                dve.tensor_scalar(var, mv[:, :, 1], LN_EPS, None, ALU.add).then_inc(var_ready, 1)
                dve.wait_ge(std_ready, 1)
                dve.reciprocal(rstd, std).then_inc(rstd_ready, 1)
                dve.wait_ge(rstd_ready, 1)
                for t in range(TILES):
                    dve.tensor_scalar(ln_dst[:, t, :], src[:, t, :], mv[:, t, 0:1], rstd[:, t:t + 1],
                                      ALU.subtract, ALU.mult).then_inc(normed, 1)
            if rms:
                dve.wait_ge(squared, TILES)
                dve.tensor_scalar(ms, squares[:, :], 1.0 / D, RMS_EPS, ALU.mult, ALU.add).then_inc(ms_ready, 1)
                dve.wait_ge(rms_std_ready, 1)
                dve.reciprocal(rrms, rms_std).then_inc(rrms_ready, 1)
                dve.wait_ge(rrms_ready, 1)
            if add_row is not None:
                dve.wait_ge(normed, TILES)
                dve.tensor_tensor(src[:, :, :], src[:, :, :],
                                  add_row.unsqueeze(1).to_broadcast([P, TILES, D]), ALU.add).then_inc(rstd_ready, 1)

            def scaled(b):
                for t in range(TPS * b, TPS * b + TPS):
                    y = ln_out if ln else src
                    last = dve.tensor_scalar(z[:, t, :], y[:, t, :], rrms[:, t:t + 1], None, ALU.mult)
                last.then_inc(z_ready, 1)

            if rms:
                scaled(0)
            for b in range(SEQS):
                if rms and b + 1 < SEQS:
                    scaled(b + 1)
                for k in range(KT):
                    n = KT * b + k
                    dve.wait_ge(hi_done, n + 1)
                    bank = tp[:, n % BANKS, :]
                    at = slice(SEQ * b, SEQ * b + SEQ)
                    if weight is None:
                        dve.tensor_tensor(hT_lo[:, k, at], bank, hT_hi[:, k, at].bitcast(F32),
                                          ALU.subtract).then_inc(split_done, 1)
                    else:
                        dve.scalar_tensor_tensor(out=hT_lo[:, k, at], in0=bank, scalar=weight[:, k:k + 1],
                                                 in1=hT_hi[:, k, at].bitcast(F32), op0=ALU.mult,
                                                 op1=ALU.subtract).then_inc(split_done, 1)

        @block.scalar
        def _(act):
            if ln:
                act.wait_ge(var_ready, 1)
                act.activation(std, var, ACT.Sqrt).then_inc(std_ready, 1)
            if rms:
                for t in range(TILES):
                    if ln:
                        act.wait_ge(normed, t + 1)
                    act.activation(z[:, t, :], (ln_out if ln else src)[:, t, :], ACT.Square,
                                   accum_out=squares[:, t:t + 1]).then_inc(squared, 1)
                act.wait_ge(ms_ready, 1)
                act.activation(rms_std, ms, ACT.Sqrt).then_inc(rms_std_ready, 1)
            for b in range(SEQS):
                for k in range(KT):
                    n = KT * b + k
                    act.wait_ge(turned, n + 1)
                    act.activation(hT_hi[:, k, SEQ * b:SEQ * b + SEQ], tp[:, n % BANKS, :], ACT.Copy,
                                   scale=1.0 if weight is None else weight[:, k:k + 1]).then_inc(hi_done, 1)

        @block.tensor
        def _(pe):
            for b in range(SEQS):
                if rms:
                    pe.wait_ge(z_ready, b + 1)
                else:
                    pe.wait_ge(normed, TPS * b + TPS)
                for k in range(KT):
                    n = KT * b + k
                    pe.wait_ge(split_done, n + 1)
                    for i in range(TPS):
                        last = pe.transpose(tp[:, n % BANKS, P * i:P * i + P],
                                            z[:, TPS * b + i, P * k:P * k + P], ident[:, :])
                    last.then_inc(turned, 1)


def projection_order():
    order = [("q", 0), ("k", 0)] + [("v", 0, t) for t in range(TPS)]
    for n in range(STEPS):
        if n + 1 < STEPS:
            order += [("q", n + 1), ("k", n + 1)]
        if n // GROUP + 1 < SEQS:
            order.append(("v", n // GROUP + 1, n % GROUP))
    return order


PROJ = projection_order()
PROJ_AT = {unit: u for u, unit in enumerate(PROJ)}
PROJS = len(PROJ)
PIECES = ["qk0", "v", "qk1", "qk2", "qk3", "o"]
NP = len(PIECES)
PROJ_BANKS, S_BANKS, T_BANKS = 2, 2, 2
PT_AT = [sum(SEQ - P * i for i in range(j)) for j in range(TPS)]
LOADS = [("qk0", 4), ("qk1", 5), ("v", 6), ("qk2", NP + 1), ("qk3", NP + 3), ("o", NP + 2)]


def attention_phase(nc, tag, linear, hT_hi, hT_lo, acc, w_dram, consts):
    wq_dram, wk_dram, wv_dram, wo_dram = w_dram
    ident, ident_bf, causal_bf, local_bf, block_mask, phi_scale, phi_bias = consts
    with ExitStack() as ctx:
        new_sem = ctx.enter_context(phase_semaphores(nc))

        def sb(name, shape, dt=F32):
            return ctx.enter_context(nc.sbuf_tensor(f"{tag}_{name}", shape, dt))

        def ps(name, banks):
            return ctx.enter_context(nc.psum_tensor(f"{tag}_{name}", [P, banks, 512], F32))

        def sem(name):
            return new_sem(f"{tag}_{name}")

        raw_qk = sb("raw_qk", [P, 2, 2, KT, HD])
        raw_vo = sb("raw_vo", [P, KT * GW])
        raw_v = raw_vo[:, :].rearrange("p (k n) -> p k n", k=KT)
        raw_o = raw_vo[:, :].rearrange("p (h d) -> p h d", h=GROUP)
        wqk_hi, wqk_lo = (sb(f"wqk_{s}", [P, 2, KT, GW], F32R) for s in ("hi", "lo"))
        wv_hi, wv_lo = (sb(f"wv_{s}", [P, KT, GW], F32R) for s in ("hi", "lo"))
        wo_hi, wo_lo = (sb(f"wo_{s}", [P, GROUP, D], F32R) for s in ("hi", "lo"))
        qk_hi, qk_lo = (sb(f"qk_{s}", [P, 2, 2, SEQ], F32R) for s in ("hi", "lo"))
        v_hi, v_lo = (sb(f"v_{s}", [P, 2, TPS, GW], F32R) for s in ("hi", "lo"))
        e = sb("e", [P, 2, E_ALL])
        pt_hi, pt_lo = (sb(f"pt_{s}", [P, E_ALL], F32R) for s in ("hi", "lo"))
        ao_hi, ao_lo = (sb(f"ao_{s}", [P, GROUP, SEQ], F32R) for s in ("hi", "lo"))
        nmax = sb("nmax", [P, 2, TPS])
        den = sb("den", [P, 2, 2, TPS])
        rden = sb("rden", [P, 2, 2, TPS])
        if linear:
            loc = sb("loc", [P, 2, TPS, P])
            phi_hi, phi_lo = (sb(f"phi_{s}", [P, 2, 2, SEQ], F32R) for s in ("hi", "lo"))
            phi_sc = sb("phi_sc", [P, 2, GROUP])
            exp_z = sb("exp_z", [P, 2, SEQ])
            relu_z = sb("relu_z", [P, 2, SEQ])

        proj_ps = ps("proj_ps", PROJ_BANKS)
        s_ps = ps("s_ps", S_BANKS)
        t_ps = ps("t_ps", T_BANKS)
        pv_ps = ps("pv_ps", 1)
        o_ps = ps("o_ps", 1)

        raw_loaded = [sem(f"raw_{p}") for p in PIECES]
        w_hi_done = sem("w_hi_done")
        w_split = sem("w_split")
        proj_done = sem("proj_done")
        proj_hi = sem("proj_hi")
        proj_split = sem("proj_split")
        s_done = sem("s_done")
        max_done = sem("max_done")
        exp_done = sem("exp_done")
        rden_done = sem("rden_done")
        normed = sem("normed")
        t_done = sem("t_done")
        t_hi = sem("t_hi")
        t_split = sem("t_split")
        pv_done = sem("pv_done")
        ao_hi_done = sem("ao_hi_done")
        ao_split = sem("ao_split")
        o_done = sem("o_done")
        o_added = sem("o_added")
        dve_step = sem("dve_step")
        if linear:
            phi_loaded = sem("phi_loaded")
            local_done = sem("local_done")
            a_read = sem("a_read")
            phi_done = sem("phi_done")
            phi_step = sem("phi_step")
            pool_step = sem("pool_step")
        block = ctx.enter_context(nc.Block())

        @block.sync
        def _(sp):
            with sp.Fori(0, GROUPS) as g:
                for piece, count in LOADS:
                    done = raw_loaded[PIECES.index(piece)]
                    if linear and piece == "qk2":
                        sp.wait_ge(proj_hi, PROJS * g + PROJ_AT[("k", STEPS - 1)] + 1)
                        for j, a in enumerate((phi_scale, phi_bias)):
                            sp.dma_start(phi_sc[:, j, :], a[:, bass.ds(g * GROUP, GROUP)]).then_inc(phi_loaded, 16)
                    sp.wait_ge(w_split, NP * g + count)
                    if piece == "v":
                        sp.dma_start(raw_v, wv_dram[:, :, bass.ds(g * GW, GW)]).then_inc(done, 16)
                    elif piece == "o":
                        sp.dma_start(raw_o, wo_dram[:, bass.ds(g * GROUP, GROUP), :]).then_inc(done, 16)
                    else:
                        h = int(piece[2])
                        for j, w in enumerate((wq_dram, wk_dram)):
                            sp.dma_start(raw_qk[:, h % 2, j, :, :],
                                         w[:, :, bass.ds(g * GW + HD * h, HD)]).then_inc(done, 16)

        def piece_views(piece):
            if piece == "v":
                return [(raw_v, wv_hi[:, :, :], wv_lo[:, :, :])]
            if piece == "o":
                return [(raw_o, wo_hi[:, :, :], wo_lo[:, :, :])]
            h = int(piece[2])
            at = slice(HD * h, HD * h + HD)
            return [(raw_qk[:, h % 2, j, :, :], wqk_hi[:, j, :, at], wqk_lo[:, j, :, at]) for j in range(2)]

        @block.gpsimd
        def _(pool):
            pool.sem_inc(w_split, NP)

            def weights_lo(g, p):
                pool.wait_ge(w_hi_done, NP * g + p + 1)
                for raw, hi, lo in piece_views(PIECES[p]):
                    last = pool.tensor_tensor(lo, raw, hi.bitcast(F32), ALU.subtract)
                last.then_inc(w_split, 1)

            def normalise(g, n):
                buf = n % 2
                pool.wait_ge(rden_done, STEPS * g + n + 1)
                if linear:
                    pool.tensor_tensor(loc[:, buf, :, :], loc[:, buf, :, :],
                                       rden[:, buf, 0, :].unsqueeze(2).to_broadcast([P, TPS, P]),
                                       ALU.mult).then_inc(pool_step, 1)
                for i in DOWN:
                    w = e[:, buf, E_AT[i]:E_AT[i] + WIDTH[i]]
                    last = pool.tensor_tensor(w, w, rden[:, buf, int(linear), i:i + 1].to_broadcast([P, WIDTH[i]]),
                                              ALU.mult)
                    if linear:
                        last.then_inc(pool_step, 1)
                if linear:
                    pool.wait_ge(pool_step, (1 + TPS) * (STEPS * g + n + 1))
                    for i in DOWN:
                        w = e[:, buf, E_AT[i] + P * i:E_AT[i] + P * i + P]
                        last = pool.tensor_tensor(w, w, loc[:, buf, i, :], ALU.add)
                last.then_inc(normed, 1)

            with pool.Fori(0, GROUPS) as g:
                for p in range(3):
                    weights_lo(g, p)
                for n in range(STEPS):
                    if n < NP - 3:
                        weights_lo(g, 3 + n)
                    normalise(g, n)

        @block.tensor
        def _(pe):
            pe.sem_inc(proj_done, PROJS)
            pe.sem_inc(o_done, 2 * SEQS)

            def project(g, unit):
                u = PROJ_AT[unit]
                out = proj_ps[:, u % PROJ_BANKS, :]
                pe.wait_ge(proj_split, PROJS * g + u + 1)
                if unit[0] == "v":
                    _, b, t = unit
                    if unit == ("v", 0, 0):
                        pe.wait_ge(w_split, NP + NP * g + PIECES.index("v") + 1)
                    at = slice(SEQ * b + P * t, SEQ * b + P * t + P)
                    for k in range(KT):
                        last = product(pe, out, hT_hi[:, k, at], hT_lo[:, k, at], wv_hi[:, k, :], wv_lo[:, k, :],
                                       k == 0, k == KT - 1)
                else:
                    j, (b, h) = "qk".index(unit[0]), divmod(unit[1], GROUP)
                    if b == 0:
                        pe.wait_ge(w_split, NP + NP * g + PIECES.index(f"qk{h}") + 1)
                    cols, at = slice(HD * h, HD * h + HD), slice(SEQ * b, SEQ * b + SEQ)
                    for k in range(KT):
                        last = product(pe, out, wqk_hi[:, j, k, cols], wqk_lo[:, j, k, cols],
                                       hT_hi[:, k, at], hT_lo[:, k, at], k == 0, k == KT - 1)
                last.then_inc(proj_done, 1)

            def free_s_bank(g, n, slot):
                if not linear:
                    pe.wait_ge(exp_done, TPS * STEPS * g + TPS * n + slot + 1)
                elif slot == 2:
                    pe.wait_ge(exp_done, STEPS * g + n + 1)
                else:
                    pe.wait_ge(a_read, TPS * STEPS * g + TPS * n + [3, 4, 0, 5, 6][slot])

            def scores(g, n, i, slot):
                buf = n % 2
                units = (TPS + int(linear)) * n + slot
                out = s_ps[:, units % S_BANKS, 0:WIDTH[i]]
                free_s_bank(g, n, slot)
                a_hi, a_lo = (phi_hi, phi_lo) if linear else (qk_hi, qk_lo)
                if linear:
                    pe.wait_ge(phi_done, 2 + 2 * (STEPS * g + n) + 2)
                else:
                    pe.wait_ge(proj_split, PROJ_BANKS + PROJS * g + PROJ_AT[("k", n)] + 1)
                at = slice(P * i, P * i + P)
                last = product(pe, out, a_hi[:, 0, buf, at], a_lo[:, 0, buf, at],
                               a_hi[:, 1, buf, 0:WIDTH[i]], a_lo[:, 1, buf, 0:WIDTH[i]], True, linear)
                if not linear:
                    last = pe.matmul(out[:, P * i:P * i + P], ident_bf[:, :], causal_bf[:, :], start=False, stop=True)
                last.then_inc(s_done, 1)

            def local_scores(g, n):
                buf = n % 2
                out = s_ps[:, (TPS + 1) * n % S_BANKS, :]
                free_s_bank(g, n, 0)
                pe.wait_ge(proj_split, PROJ_BANKS + PROJS * g + PROJ_AT[("k", n)] + 1)
                pe.matmul(out, ident_bf[:, :], local_bf[:, :], start=True, stop=False)
                for i in range(TPS):
                    at = slice(P * i, P * i + P)
                    last = product(pe, out[:, at], qk_hi[:, 0, buf, at], qk_lo[:, 0, buf, at],
                                   qk_hi[:, 1, buf, at], qk_lo[:, 1, buf, at], False, i == TPS - 1)
                last.then_inc(local_done, 1)

            def turn(g, n, j):
                if j == 0:
                    pe.wait_ge(normed, STEPS * g + n + 1)
                pe.wait_ge(t_split, TPS * (STEPS * g + n) + j + 1)
                for i in range(j, TPS):
                    last = pe.transpose(t_ps[:, j % T_BANKS, P * (i - j):P * (i - j) + P],
                                        e[:, n % 2, E_AT[i] + P * j:E_AT[i] + P * j + P], ident[:, :])
                last.then_inc(t_done, 1)

            def times_v(g, n, j):
                b, h = divmod(n, GROUP)
                if j == 0:
                    pe.wait_ge(ao_split, STEPS * g + n + 1)
                    pe.wait_ge(proj_split, PROJ_BANKS + PROJS * g + PROJ_AT[("v", b, TPS - 1)] + 1)
                pe.wait_ge(t_split, T_BANKS + TPS * (STEPS * g + n) + j + 1)
                cols, w = slice(HD * h, HD * h + HD), SEQ - P * j
                last = product(pe, pv_ps[:, 0, P * j:SEQ], v_hi[:, b % 2, j, cols], v_lo[:, b % 2, j, cols],
                               pt_hi[:, PT_AT[j]:PT_AT[j] + w], pt_lo[:, PT_AT[j]:PT_AT[j] + w], j == 0, j == TPS - 1)
                if j == TPS - 1:
                    last.then_inc(pv_done, 1)

            def out_project(g, b, m):
                if b == 0 and m == 0:
                    pe.wait_ge(w_split, NP + NP * g + PIECES.index("o") + 1)
                pe.wait_ge(ao_split, 1 + STEPS * g + GROUP * b + GROUP)
                pe.wait_ge(o_added, 2 * SEQS * g + 2 * b + m + 1)
                for half in range(2):
                    at = slice(P * (2 * m + half), P * (2 * m + half) + P)
                    for h in range(GROUP):
                        last = product(pe, o_ps[:, 0, D * half:D * half + D], ao_hi[:, h, at], ao_lo[:, h, at],
                                       wo_hi[:, h, :], wo_lo[:, h, :], h == 0, h == GROUP - 1)
                last.then_inc(o_done, 1)

            with pe.Fori(0, GROUPS) as g:
                for unit in PROJ[:2 + TPS]:
                    project(g, unit)
                for n in range(STEPS + 1):
                    now, before = n < STEPS, n >= 1
                    o_turn = n % GROUP == 1 and n > GROUP
                    if o_turn:
                        out_project(g, n // GROUP - 1, 0)
                    if now and linear:
                        local_scores(g, n)
                    if now:
                        scores(g, n, 3, int(linear))
                    if n + 1 < STEPS:
                        project(g, ("q", n + 1))
                    if now:
                        scores(g, n, 2, 1 + int(linear))
                    if o_turn:
                        out_project(g, n // GROUP - 1, 1)
                    if n + 1 < STEPS:
                        project(g, ("k", n + 1))
                    if before:
                        turn(g, n - 1, 0)
                    if now:
                        scores(g, n, 1, 2 + int(linear))
                    if before:
                        turn(g, n - 1, 1)
                        times_v(g, n - 1, 0)
                    if now:
                        scores(g, n, 0, 3 + int(linear))
                    if before:
                        turn(g, n - 1, 2)
                        times_v(g, n - 1, 1)
                        turn(g, n - 1, 3)
                        times_v(g, n - 1, 2)
                        times_v(g, n - 1, 3)
                    if n // GROUP + 1 < SEQS:
                        project(g, ("v", n // GROUP + 1, n % GROUP))
                for m in range(2):
                    out_project(g, SEQS - 1, m)

        @block.scalar
        def _(act):
            act.sem_inc(proj_hi, PROJS)
            if not linear:
                act.sem_inc(exp_done, S_BANKS)

            def weights_hi(g, p):
                piece = PIECES[p]
                n_dma = 1 if piece in "vo" else 2
                act.wait_ge(raw_loaded[p], 16 * n_dma * (g + 1))
                if piece == "o":
                    act.wait_ge(o_done, 2 * SEQS * g + 2 * SEQS)
                elif piece == "v":
                    act.wait_ge(proj_done, PROJS * g + PROJ_AT[("v", SEQS - 1, TPS - 1)] + 1)
                else:
                    act.wait_ge(proj_done, PROJS * g + PROJ_AT[("k", STEPS - GROUP + int(piece[2]))] + 1)
                for raw, hi, _ in piece_views(piece):
                    last = act.activation(hi, raw, ACT.Copy)
                last.then_inc(w_hi_done, 1)

            def project_hi(g, unit):
                u = PROJ_AT[unit]
                bank = proj_ps[:, u % PROJ_BANKS, :]
                act.wait_ge(proj_done, PROJS + PROJS * g + u + 1)
                if unit[0] == "v":
                    last = act.activation(v_hi[:, unit[1] % 2, unit[2], :], bank, ACT.Copy)
                else:
                    j, n = "qk".index(unit[0]), unit[1]
                    last = act.activation(qk_hi[:, j, n % 2, :], bank, ACT.Copy, scale=SCALE if j == 0 else 1.0)
                    if linear:
                        act.wait_ge(phi_done, 2 * (STEPS * g + n) + j + 1)
                        act.wait_ge(phi_loaded, 32 * (g + 1))
                        s, c = (phi_sc[:, i, n % GROUP:n % GROUP + 1] for i in range(2))
                        act.activation(exp_z[:, j, :], bank, ACT.Exp, bias=c, scale=s)
                        last = act.activation(relu_z[:, j, :], bank, ACT.Relu, bias=c, scale=s)
                last.then_inc(proj_hi, 1)

            def exponent(g, n, i, slot):
                buf = n % 2
                act.wait_ge(max_done, TPS * (STEPS * g + n) + slot + 1)
                act.activation(e[:, buf, E_AT[i]:E_AT[i] + WIDTH[i]], s_ps[:, (TPS * n + slot) % S_BANKS, 0:WIDTH[i]],
                               ACT.Exp, bias=nmax[:, buf, i:i + 1],
                               accum_out=den[:, buf, 0, i:i + 1]).then_inc(exp_done, 1)

            def local_exponents(g, n):
                buf = n % 2
                act.wait_ge(max_done, STEPS * g + n + 1)
                for i in range(TPS):
                    last = act.activation(loc[:, buf, i, :], s_ps[:, (TPS + 1) * n % S_BANKS, P * i:P * i + P],
                                          ACT.Exp, bias=nmax[:, buf, i:i + 1], accum_out=den[:, buf, 0, i:i + 1])
                last.then_inc(exp_done, 1)

            def turned_hi(g, n, j):
                act.wait_ge(t_done, TPS * (STEPS * g + n) + j + 1)
                w = SEQ - P * j
                act.activation(pt_hi[:, PT_AT[j]:PT_AT[j] + w], t_ps[:, j % T_BANKS, 0:w], ACT.Copy).then_inc(t_hi, 1)

            def out_hi(g, n):
                act.wait_ge(pv_done, STEPS * g + n + 1)
                act.activation(ao_hi[:, n % GROUP, :], pv_ps[:, 0, :], ACT.Copy).then_inc(ao_hi_done, 1)

            with act.Fori(0, GROUPS) as g:
                weights_hi(g, 0)
                weights_hi(g, 1)
                project_hi(g, ("q", 0))
                project_hi(g, ("k", 0))
                weights_hi(g, 2)
                for t in range(TPS):
                    project_hi(g, ("v", 0, t))
                for n in range(STEPS + 1):
                    now, before = n < STEPS, n >= 1
                    if n < NP - 3:
                        weights_hi(g, 3 + n)
                    if now and linear:
                        local_exponents(g, n)
                    if now and not linear:
                        exponent(g, n, 3, 0)
                    if n + 1 < STEPS:
                        project_hi(g, ("q", n + 1))
                    if now and not linear:
                        exponent(g, n, 2, 1)
                    if n + 1 < STEPS:
                        project_hi(g, ("k", n + 1))
                    if before:
                        turned_hi(g, n - 1, 0)
                    if now and not linear:
                        exponent(g, n, 1, 2)
                    if before:
                        turned_hi(g, n - 1, 1)
                    if now and not linear:
                        exponent(g, n, 0, 3)
                    if before:
                        turned_hi(g, n - 1, 2)
                        turned_hi(g, n - 1, 3)
                        out_hi(g, n - 1)
                    if n // GROUP + 1 < SEQS:
                        project_hi(g, ("v", n // GROUP + 1, n % GROUP))

        @block.vector
        def _(dve):
            dve.sem_inc(proj_split, PROJ_BANKS)
            dve.sem_inc(t_split, T_BANKS)
            dve.sem_inc(ao_split, 1)
            dve.sem_inc(o_added, 1)
            if linear:
                dve.sem_inc(a_read, TPS)
                dve.sem_inc(phi_done, 2)

            def project_lo(g, unit):
                u = PROJ_AT[unit]
                bank = proj_ps[:, u % PROJ_BANKS, :]
                dve.wait_ge(proj_hi, PROJS + PROJS * g + u + 1)
                if unit[0] == "v":
                    at = (slice(None), unit[1] % 2, unit[2], slice(None))
                    dve.tensor_tensor(v_lo[at], bank, v_hi[at].bitcast(F32), ALU.subtract).then_inc(proj_split, 1)
                    return
                j, n = "qk".index(unit[0]), unit[1]
                at = (slice(None), j, n % 2, slice(None))
                if j == 0:
                    dve.scalar_tensor_tensor(out=qk_lo[at], in0=bank, scalar=SCALE, in1=qk_hi[at].bitcast(F32),
                                             op0=ALU.mult, op1=ALU.subtract).then_inc(proj_split, 1)
                else:
                    dve.tensor_tensor(qk_lo[at], bank, qk_hi[at].bitcast(F32), ALU.subtract).then_inc(proj_split, 1)
                if linear:
                    u = 2 * n + j
                    dve.scalar_tensor_tensor(out=relu_z[:, j, :], in0=exp_z[:, j, :], scalar=1.0, in1=relu_z[:, j, :],
                                             op0=ALU.min, op1=ALU.add).then_inc(phi_step, 1)
                    dve.wait_ge(phi_step, 4 * STEPS * g + 2 * u + 1)
                    dve.tensor_scalar(phi_hi[at], relu_z[:, j, :], 10.0, None, ALU.min).then_inc(phi_step, 1)
                    dve.wait_ge(phi_step, 4 * STEPS * g + 2 * u + 2)
                    dve.scalar_tensor_tensor(out=phi_lo[at], in0=relu_z[:, j, :], scalar=10.0,
                                             in1=phi_hi[at].bitcast(F32), op0=ALU.min,
                                             op1=ALU.subtract).then_inc(phi_done, 1)

            def row_max(g, n, i, slot):
                dve.wait_ge(s_done, TPS * (STEPS * g + n) + slot + 1)
                dve.tensor_reduce(nmax[:, n % 2, i:i + 1], s_ps[:, (TPS * n + slot) % S_BANKS, 0:WIDTH[i]],
                                  AX.X, ALU.max, negate=True).then_inc(max_done, 1)

            def local_max(g, n):
                dve.wait_ge(local_done, STEPS * g + n + 1)
                dve.tensor_reduce(nmax[:, n % 2, :],
                                  s_ps[:, (TPS + 1) * n % S_BANKS, :].rearrange("p (i k) -> p i k", k=P),
                                  AX.X, ALU.max, negate=True).then_inc(max_done, 1)

            def linear_weights(g, n, i, slot):
                dve.wait_ge(s_done, TPS * (STEPS * g + n) + slot)
                dve.tensor_tensor_reduce(e[:, n % 2, E_AT[i]:E_AT[i] + WIDTH[i]],
                                         s_ps[:, ((TPS + 1) * n + slot) % S_BANKS, 0:WIDTH[i]],
                                         block_mask[:, SEQ - WIDTH[i]:SEQ], 1.0, 0.0, ALU.mult, ALU.add,
                                         den[:, n % 2, 1, i:i + 1]).then_inc(a_read, 1)

            def invert(g, n):
                buf = n % 2
                if linear:
                    dve.wait_ge(exp_done, STEPS * g + n + 1)
                    dve.wait_ge(a_read, TPS + TPS * (STEPS * g + n + 1))
                    dve.tensor_scalar(den[:, buf, :, :], den[:, buf, :, :], DEN_EPS, None,
                                      ALU.max).then_inc(dve_step, 1)
                    dve.wait_ge(dve_step, STEPS * g + n + 1)
                    dve.reciprocal(rden[:, buf, :, :], den[:, buf, :, :]).then_inc(rden_done, 1)
                else:
                    dve.wait_ge(exp_done, S_BANKS + TPS * (STEPS * g + n + 1))
                    dve.reciprocal(rden[:, buf, 0, :], den[:, buf, 0, :]).then_inc(rden_done, 1)

            def turned_lo(g, n, j):
                dve.wait_ge(t_hi, TPS * (STEPS * g + n) + j + 1)
                w = SEQ - P * j
                at = slice(PT_AT[j], PT_AT[j] + w)
                dve.tensor_tensor(pt_lo[:, at], t_ps[:, j % T_BANKS, 0:w], pt_hi[:, at].bitcast(F32),
                                  ALU.subtract).then_inc(t_split, 1)

            def out_lo(g, n):
                dve.wait_ge(ao_hi_done, STEPS * g + n + 1)
                h = n % GROUP
                dve.tensor_tensor(ao_lo[:, h, :], pv_ps[:, 0, :], ao_hi[:, h, :].bitcast(F32),
                                  ALU.subtract).then_inc(ao_split, 1)

            def add_out(g, b, m):
                dve.wait_ge(o_done, 2 * SEQS + 2 * SEQS * g + 2 * b + m + 1)
                t = TPS * b + 2 * m
                dve.tensor_tensor(acc[:, t:t + 2, :], o_ps[:, 0, :].rearrange("p (t d) -> p t d", d=D),
                                  acc[:, t:t + 2, :], ALU.add).then_inc(o_added, 1)

            with dve.Fori(0, GROUPS) as g:
                for unit in PROJ[:2 + TPS]:
                    project_lo(g, unit)
                for n in range(STEPS + 1):
                    now, before = n < STEPS, n >= 1
                    o_turn = n % GROUP == 1 and n > GROUP
                    if o_turn:
                        add_out(g, n // GROUP - 1, 0)
                    if now and linear:
                        local_max(g, n)
                        linear_weights(g, n, 3, 1)
                    elif now:
                        row_max(g, n, 3, 0)
                    if n + 1 < STEPS:
                        project_lo(g, ("q", n + 1))
                    if now and linear:
                        linear_weights(g, n, 2, 2)
                    elif now:
                        row_max(g, n, 2, 1)
                    if o_turn:
                        add_out(g, n // GROUP - 1, 1)
                    if n + 1 < STEPS:
                        project_lo(g, ("k", n + 1))
                    if before:
                        turned_lo(g, n - 1, 0)
                    if now and linear:
                        linear_weights(g, n, 1, 3)
                    elif now:
                        row_max(g, n, 1, 2)
                    if before:
                        turned_lo(g, n - 1, 1)
                    if now and linear:
                        linear_weights(g, n, 0, 4)
                    elif now:
                        row_max(g, n, 0, 3)
                    if before:
                        turned_lo(g, n - 1, 2)
                    if now:
                        invert(g, n)
                    if before:
                        turned_lo(g, n - 1, 3)
                        out_lo(g, n - 1)
                    if n // GROUP + 1 < SEQS:
                        project_lo(g, ("v", n // GROUP + 1, n % GROUP))
                for m in range(2):
                    add_out(g, SEQS - 1, m)


def routing_phase(nc, tag, tT_hi, tT_lo, gate_dram, ident_bf, cwT):
    E1 = EXPERTS + 1
    with ExitStack() as ctx:
        new_sem = ctx.enter_context(phase_semaphores(nc))

        def sb(name, shape, dt=F32):
            return ctx.enter_context(nc.sbuf_tensor(f"{tag}_{name}", shape, dt))

        def sem(name):
            return new_sem(f"{tag}_{name}")

        gate = sb("gate", [P, KT, EXPERTS])
        gate_hi, gate_lo = (sb(f"gate_{s}", [P, KT, EXPERTS], F32R) for s in ("hi", "lo"))
        rowmax = sb("rowmax", [P, TILES])
        rowsum = sb("rowsum", [P, TILES])
        rsum = sb("rsum", [P, TILES])
        topsum = sb("topsum", [P, TILES])
        rtop = sb("rtop", [P, TILES])
        shifted = sb("shifted", [P, TILES, EXPERTS])
        ex = sb("ex", [P, TILES, EXPERTS])
        probs = sb("probs", [P, TILES, EXPERTS + 2])
        top8 = sb("top8", [P, TILES, 8])
        rest = sb("rest", [P, TILES, EXPERTS + 2])
        sel = sb("sel", [P, TILES, EXPERTS])
        cw = sb("cw", [P, TILES, EXPERTS])
        left1 = sb("left1", [P, TILES, EXPERTS])
        left2 = sb("left2", [P, TILES, EXPERTS])
        cw3 = sb("cw3", [P, TILES, CW_ROWS], BF16)
        logits = ctx.enter_context(nc.psum_tensor(f"{tag}_logits", [P, TILES, EXPERTS], F32))
        cw_ps = ctx.enter_context(nc.psum_tensor(f"{tag}_cw_ps", [P, 2, 8 * P], BF16))

        loaded, split, logits_done, vec = sem("loaded"), sem("split"), sem("logits_done"), sem("vec")
        shifted_done, exp_done, cw_ready, turned, copied = (
            sem("shifted_done"), sem("exp_done"), sem("cw_ready"), sem("turned"), sem("copied"))
        block = ctx.enter_context(nc.Block())

        @block.sync
        def _(sp):
            sp.dma_start(gate[:, :, :], gate_dram).then_inc(loaded, 16)

        @block.tensor
        def _(pe):
            pe.wait_ge(split, 2)
            for t in range(TILES):
                for k in range(KT):
                    last = product(pe, logits[:, t, :], tT_hi[:, k, P * t:P * t + P], tT_lo[:, k, P * t:P * t + P],
                                   gate_hi[:, k, :], gate_lo[:, k, :], k == 0, k == KT - 1)
            last.then_inc(logits_done, 1)
            pe.wait_ge(cw_ready, 1)
            for t in range(TILES):
                last = pe.transpose(cw_ps[0:CW_ROWS, t // 8, P * (t % 8):P * (t % 8) + P], cw3[:, t, :], ident_bf[:, :])
            last.then_inc(turned, 1)

        @block.scalar
        def _(act):
            act.wait_ge(shifted_done, 1)
            act.activation(ex[:, :, :], shifted[:, :, :], ACT.Exp).then_inc(exp_done, 1)

        @block.vector
        def _(dve):
            def spread(column):
                return column[:, :].unsqueeze(2).to_broadcast([P, TILES, EXPERTS])

            dve.wait_ge(loaded, 16)
            dve.tensor_copy(gate_hi[:, :, :], gate[:, :, :]).then_inc(split, 1)
            dve.wait_ge(split, 1)
            dve.tensor_tensor(gate_lo[:, :, :], gate[:, :, :], gate_hi[:, :, :].bitcast(F32),
                              ALU.subtract).then_inc(split, 1)
            dve.memset(probs[:, :, EXPERTS:EXPERTS + 1], -1.0)
            dve.memset(probs[:, :, EXPERTS + 1:EXPERTS + 2], -2.0)
            dve.memset(cw3[:, :, EXPERTS:E1], 1.0)
            dve.memset(cw3[:, :, E1 + EXPERTS:2 * E1], 0.0)
            dve.memset(cw3[:, :, 2 * E1 + EXPERTS:3 * E1], 0.0).then_inc(vec, 1)
            dve.wait_ge(logits_done, 1)
            dve.tensor_reduce(rowmax[:, :], logits[:, :, :], AX.X, ALU.max).then_inc(vec, 1)
            dve.wait_ge(vec, 2)
            dve.tensor_tensor(shifted[:, :, :], logits[:, :, :], spread(rowmax), ALU.subtract).then_inc(shifted_done, 1)
            dve.wait_ge(exp_done, 1)
            dve.tensor_reduce(rowsum[:, :], ex[:, :, :], AX.X, ALU.add).then_inc(vec, 1)
            dve.wait_ge(vec, 3)
            dve.reciprocal(rsum[:, :], rowsum[:, :]).then_inc(vec, 1)
            dve.wait_ge(vec, 4)
            dve.tensor_tensor(probs[:, :, 0:EXPERTS], ex[:, :, :], spread(rsum), ALU.mult).then_inc(vec, 1)
            dve.wait_ge(vec, 5)
            for t in range(TILES):
                last = dve.max(top8[:, t, :], probs[:, t, 0:EXPERTS])
            last.then_inc(vec, 1)
            dve.wait_ge(vec, 6)
            dve.memset(top8[:, :, TOPK:TOPK + 1], -1.0).then_inc(vec, 1)
            dve.memset(top8[:, :, TOPK + 1:TOPK + 2], -2.0).then_inc(vec, 1)
            dve.wait_ge(vec, 8)
            for t in range(TILES):
                last = dve.match_replace(rest[:, t, :], top8[:, t, :], probs[:, t, :], 0.0)
            last.then_inc(vec, 1)
            dve.wait_ge(vec, 9)
            dve.tensor_tensor(sel[:, :, :], probs[:, :, 0:EXPERTS], rest[:, :, 0:EXPERTS],
                              ALU.subtract).then_inc(vec, 1)
            dve.wait_ge(vec, 10)
            dve.tensor_reduce(topsum[:, :], sel[:, :, :], AX.X, ALU.add).then_inc(vec, 1)
            dve.wait_ge(vec, 11)
            dve.reciprocal(rtop[:, :], topsum[:, :]).then_inc(vec, 1)
            dve.wait_ge(vec, 12)
            dve.tensor_tensor(cw[:, :, :], sel[:, :, :], spread(rtop), ALU.mult).then_inc(vec, 1)
            dve.wait_ge(vec, 13)
            parts = [cw3[:, :, E1 * i:E1 * i + EXPERTS] for i in range(3)]
            dve.tensor_copy(parts[0], cw[:, :, :]).then_inc(vec, 1)
            dve.wait_ge(vec, 14)
            dve.tensor_tensor(left1[:, :, :], cw[:, :, :], parts[0], ALU.subtract).then_inc(vec, 1)
            dve.wait_ge(vec, 15)
            dve.tensor_copy(parts[1], left1[:, :, :]).then_inc(vec, 1)
            dve.wait_ge(vec, 16)
            dve.tensor_tensor(left2[:, :, :], left1[:, :, :], parts[1], ALU.subtract).then_inc(vec, 1)
            dve.wait_ge(vec, 17)
            dve.tensor_copy(parts[2], left2[:, :, :]).then_inc(cw_ready, 1)
            dve.wait_ge(turned, 1)
            for i in range(2):
                dve.tensor_copy(cwT[:, 8 * P * i:8 * P * i + 8 * P], cw_ps[0:CW_ROWS, i, :]).then_inc(copied, 1)


def experts_phase(nc, tag, tT_hi, tT_lo, cwT, sel_dram, w_dram, y, x, out_dram):
    up_dram, down_dram = w_dram
    sel_words = sel_dram.bitcast(F32)
    with ExitStack() as ctx:
        new_sem = ctx.enter_context(phase_semaphores(nc))

        def sb(name, shape, dt=F32):
            return ctx.enter_context(nc.sbuf_tensor(f"{tag}_{name}", shape, dt))

        def ps(name, banks):
            return ctx.enter_context(nc.psum_tensor(f"{tag}_{name}", [P, banks, 512], F32))

        def sem(name):
            return new_sem(f"{tag}_{name}")

        raw_up = sb("raw_up", [P, CPG, 2, KT, P])
        raw_dn = sb("raw_dn", [P, CPG, D])
        up_hi, up_lo = (sb(f"up_{s}", [P, CPG, 2, KT, P], F32R) for s in ("hi", "lo"))
        dn_hi, dn_lo = (sb(f"dn_{s}", [P, CPG, D], F32R) for s in ("hi", "lo"))
        sel_bf = sb("sel_bf", [CW_ROWS, CPG, P], BF16)
        silu = sb("silu", [P, 2, SEQ])
        prod = sb("prod", [P, 2, SEQ])
        hh = sb("hh", [P, 2, SEQ])
        hh_hi, hh_lo = (sb(f"hh_{s}", [P, 2, SEQ], F32R) for s in ("hi", "lo"))
        g_ps, u_ps, cw_ps, dn_ps = ps("g_ps", 2), ps("u_ps", 2), ps("cw_ps", 2), ps("dn_ps", 2)

        raw_loaded = [sem(f"raw_{c}") for c in range(CPG)]
        sel_loaded = [sem(f"sel_{c}") for c in range(CPG)]
        w_hi_done = sem("w_hi_done")
        w_split = sem("w_split")
        up_done = sem("up_done")
        silu_done = sem("silu_done")
        prod_done = sem("prod_done")
        gated = sem("gated")
        hh_hi_done = sem("hh_hi_done")
        hh_split = sem("hh_split")
        dn_done = sem("dn_done")
        y_added = sem("y_added")
        x_added = sem("x_added")
        stored = sem("stored")
        block = ctx.enter_context(nc.Block())

        @block.sync
        def _(sp):
            with sp.Fori(0, CHUNK_GROUPS) as g:
                for c in range(CPG):
                    sp.wait_ge(w_split, CPG * g + c + 1)
                    for j in range(2):
                        sp.dma_start(raw_up[:, c, j, :, :],
                                     up_dram[j][:, :, bass.ds(g * (CPG * P) + c * P, P)]).then_inc(raw_loaded[c], 16)
                    sp.dma_start(raw_dn[:, c, :], down_dram[bass.ds(g * (CPG * P) + c * P, P), :]).then_inc(raw_loaded[c], 16)
                for c in range(CPG):
                    sp.wait_ge(dn_done, UNITS * g + CPG * (SEQS - 1) + c + 1)
                    sp.dma_start(sel_bf[:, c, :].bitcast(F32),
                                 sel_words[:, bass.ds(g * (CPG * P // 2) + c * P // 2, P // 2)]).then_inc(sel_loaded[c], 16)
            if out_dram is not None:
                for b in range(SEQS):
                    sp.wait_ge(x_added, b + 1)
                    sp.dma_start(out_dram[:, TPS * b:TPS * b + TPS, :],
                                 x[:, TPS * b:TPS * b + TPS, :]).then_inc(stored, 16)
                sp.wait_ge(stored, 16 * SEQS)

        @block.gpsimd
        def _(pool):
            pool.sem_inc(w_split, CPG)
            with pool.Fori(0, CHUNK_GROUPS) as g:
                for c in range(CPG):
                    pool.wait_ge(w_hi_done, CPG * g + c + 1)
                    pool.tensor_tensor(up_lo[:, c], raw_up[:, c], up_hi[:, c].bitcast(F32), ALU.subtract)
                    pool.tensor_tensor(dn_lo[:, c, :], raw_dn[:, c, :], dn_hi[:, c, :].bitcast(F32),
                                       ALU.subtract).then_inc(w_split, 1)

        @block.tensor
        def _(pe):
            pe.sem_inc(dn_done, UNITS)

            def up(g, k):
                b, c = divmod(k, CPG)
                if b == 0:
                    pe.wait_ge(w_split, CPG + CPG * g + c + 1)
                    pe.wait_ge(sel_loaded[c], 16 * (g + 1))
                pe.wait_ge(gated, UNITS * g + k + 1)
                at = slice(SEQ * b, SEQ * b + SEQ)
                for j, bank in enumerate((g_ps, u_ps)):
                    for kt in range(KT):
                        product(pe, bank[:, k % 2, :], up_hi[:, c, j, kt, :], up_lo[:, c, j, kt, :],
                                tT_hi[:, kt, at], tT_lo[:, kt, at], kt == 0, kt == KT - 1)
                pe.matmul(cw_ps[:, k % 2, :], sel_bf[:, c, :], cwT[:, at], start=True, stop=True).then_inc(up_done, 1)

            def down(g, k):
                b, c = divmod(k, CPG)
                pe.wait_ge(hh_split, UNITS * g + k + 1)
                if c == 0:
                    pe.wait_ge(y_added, 2 * SEQS * g + 2 * b + 2)
                for t in range(TPS):
                    at = slice(P * t, P * t + P)
                    last = product(pe, dn_ps[:, t // 2, D * (t % 2):D * (t % 2) + D], hh_hi[:, k % 2, at],
                                   hh_lo[:, k % 2, at], dn_hi[:, c, :], dn_lo[:, c, :],
                                   c == 0 and t % 2 == 0, c == CPG - 1, shared_bank=True)
                last.then_inc(dn_done, 1)

            with pe.Fori(0, CHUNK_GROUPS) as g:
                up(g, 0)
                for k in range(UNITS):
                    if k + 1 < UNITS:
                        up(g, k + 1)
                    down(g, k)

        @block.scalar
        def _(act):
            def weights_hi(g, c):
                act.wait_ge(raw_loaded[c], 48 * (g + 1))
                act.wait_ge(dn_done, UNITS * g + CPG * (SEQS - 1) + c + 1)
                act.activation(up_hi[:, c], raw_up[:, c], ACT.Copy)
                act.activation(dn_hi[:, c, :], raw_dn[:, c, :], ACT.Copy).then_inc(w_hi_done, 1)

            with act.Fori(0, CHUNK_GROUPS) as g:
                weights_hi(g, 0)
                for k in range(UNITS):
                    if k + 1 < CPG:
                        weights_hi(g, k + 1)
                    act.wait_ge(up_done, UNITS * g + k + 1)
                    act.activation(silu[:, k % 2, :], g_ps[:, k % 2, :], ACT.Silu).then_inc(silu_done, 1)
                    act.wait_ge(gated, 2 + UNITS * g + k + 1)
                    act.activation(hh_hi[:, k % 2, :], hh[:, k % 2, :], ACT.Copy).then_inc(hh_hi_done, 1)

        @block.vector
        def _(dve):
            dve.sem_inc(gated, 2)
            dve.sem_inc(y_added, 2)

            def add_down(g, b, m):
                t = TPS * b + 2 * m
                dve.tensor_tensor(y[:, t:t + 2, :], dn_ps[:, m, :].rearrange("p (t d) -> p t d", d=D),
                                  y[:, t:t + 2, :], ALU.add).then_inc(y_added, 1)

            with dve.Fori(0, CHUNK_GROUPS) as g:
                for k in range(UNITS + 1):
                    if k < UNITS:
                        dve.wait_ge(silu_done, UNITS * g + k + 1)
                        dve.tensor_tensor(prod[:, k % 2, :], u_ps[:, k % 2, :], silu[:, k % 2, :],
                                          ALU.mult).then_inc(prod_done, 1)
                        dve.wait_ge(prod_done, UNITS * g + k + 1)
                        dve.tensor_tensor(hh[:, k % 2, :], cw_ps[:, k % 2, :], prod[:, k % 2, :],
                                          ALU.mult).then_inc(gated, 1)
                        dve.wait_ge(hh_hi_done, UNITS * g + k + 1)
                        dve.tensor_tensor(hh_lo[:, k % 2, :], hh[:, k % 2, :], hh_hi[:, k % 2, :].bitcast(F32),
                                          ALU.subtract).then_inc(hh_split, 1)
                    if k % CPG == 0 and k:
                        dve.wait_ge(dn_done, UNITS + UNITS * g + k)
                        for m in range(2):
                            add_down(g, k // CPG - 1, m)
            dve.wait_ge(y_added, 2 + 2 * SEQS * CHUNK_GROUPS)
            for b in range(SEQS):
                at = slice(TPS * b, TPS * b + TPS)
                dve.scalar_tensor_tensor(out=x[:, at, :], in0=y[:, at, :], scalar=0.5, in1=x[:, at, :],
                                         op0=ALU.mult, op1=ALU.add).then_inc(x_added, 1)


def macaron_kernel(nc, x_in, Wq, Wk, Wv, phi_scale_in, phi_bias_in, Wo, bo_in, ln1_in, ln2_in, wq, wk, wv, wo,
                   gate_w, eg_w, eu_w, ed_w, ident_in, ident_bf_in, causal_in, local_in, block_mask_in, sel_in, out):
    with ExitStack() as ctx:
        def sb(name, shape, dt=F32):
            return ctx.enter_context(nc.sbuf_tensor(name, shape, dt))

        ident = sb("ident", [P, P])
        ident_bf = sb("ident_bf", [P, P], BF16)
        causal_bf = sb("causal_bf", [P, P], BF16)
        ln_w = sb("ln_w", [P, 2, KT])
        x = sb("x", [P, TILES, D])
        hT_hi, hT_lo = (sb(f"hT_{s}", [P, KT, TOKENS], F32R) for s in ("hi", "lo"))

        def by_k(w):
            return w.rearrange("(k p) n -> p k n", p=P)

        def by_token(a):
            return a.rearrange("(t p) d -> p t d", p=P)

        attn_w = (by_k(Wq), by_k(Wk), by_k(Wv), by_k(Wo))
        ffn_w = (by_k(wq), by_k(wk), by_k(wv), by_k(wo))
        up_w = ((by_k(eg_w), by_k(eu_w)), ed_w)
        first_loads = [(x[:, :, :], by_token(x_in)), (ident[:, :], ident_in), (ident_bf[:, :], ident_bf_in),
                       (causal_bf[:, :], causal_in), (ln_w[:, 0, :], ln1_in), (ln_w[:, 1, :], ln2_in)]

        def ffn(tag, loads, out_dram):
            with ExitStack() as inner:
                def sbi(name, shape, dt=F32):
                    return inner.enter_context(nc.sbuf_tensor(f"{tag}_{name}", shape, dt))

                y = sbi("y", [P, TILES, D])
                norm_phase(nc, f"{tag}n1", x, y, True, ln_w[:, 0, :], hT_hi, hT_lo, ident, loads=loads)
                attention_phase(nc, f"{tag}at", False, hT_hi, hT_lo, y, ffn_w,
                                (ident, ident_bf, causal_bf, None, None, None, None))
                cwT = sbi("cwT", [CW_ROWS, TOKENS], BF16)
                norm_phase(nc, f"{tag}n2", y, None, True, ln_w[:, 1, :], hT_hi, hT_lo, ident)
                routing_phase(nc, f"{tag}rt", hT_hi, hT_lo, by_k(gate_w), ident_bf, cwT)
                experts_phase(nc, f"{tag}ex", hT_hi, hT_lo, cwT, sel_in, up_w, y, x, out_dram)

        ffn("f1", first_loads, None)
        with ExitStack() as inner:
            def sbi(name, shape, dt=F32):
                return inner.enter_context(nc.sbuf_tensor(name, shape, dt))

            local_bf = sbi("local_bf", [P, SEQ], BF16)
            block_mask = sbi("block_mask", [P, SEQ])
            bo = sbi("bo", [P, D])
            norm_phase(nc, "an", x, x, False, None, hT_hi, hT_lo, ident, add_row=bo[:, :],
                       loads=[(local_bf[:, :], local_in), (block_mask[:, :], block_mask_in),
                              (bo[:, :], bo_in)])
            attention_phase(nc, "aa", True, hT_hi, hT_lo, x, attn_w,
                            (ident, ident_bf, None, local_bf, block_mask, phi_scale_in, phi_bias_in))
        ffn("f2", None, by_token(out))


def kernel(**inputs):
    import ml_dtypes
    import numpy as np
    import concourse.bacc as bacc
    from concourse.bass_utils import run_bass_kernel_spmd

    def arr(name):
        return np.asarray(inputs[name])

    def experts_side_by_side(routed, shared):
        flat = np.concatenate([routed.reshape(EXPERTS * INNER, D), shared], axis=0)
        return np.concatenate([flat, np.zeros((CHUNKS * P - flat.shape[0], D), flat.dtype)], axis=0)

    bf = ml_dtypes.bfloat16
    below = np.tril(np.ones((P, P), bool))
    hidden = -1e9 / SCALE
    causal = np.where(below, 0.0, hidden).astype(bf)
    same = np.kron(np.eye(P // 64), np.ones((64, 64))).astype(bool)
    local = np.tile(np.where(same, 0.0, hidden), (1, TPS)).astype(bf)
    block_mask = np.ones((P, SEQ), np.float32)
    block_mask[:64, SEQ - 64:] = 0.0
    sel = np.zeros((CW_ROWS, CHUNKS * P), np.float32)
    for c in range(EXPERTS * INNER + SHARED):
        for part in range(3):
            sel[part * (EXPERTS + 1) + min(c // INNER, EXPERTS), c] = 1.0

    arrays = {
        "x_in": arr("L0_attn_x").reshape(TOKENS, D),
        "Wq": arr("L0_attn_Wq"), "Wk": arr("L0_attn_Wk"), "Wv": arr("L0_attn_Wv"),
        "phi_scale_in": np.ascontiguousarray(arr("L0_attn_phi_scale").reshape(HEADS, HD).T),
        "phi_bias_in": np.ascontiguousarray(arr("L0_attn_phi_bias").reshape(HEADS, HD).T),
        "Wo": arr("L0_attn_Wo"),
        "bo_in": np.ascontiguousarray(np.broadcast_to(arr("L0_attn_bo"), (P, D))),
        "ln1_in": np.ascontiguousarray(arr("L0_ffn_ln1_w").reshape(KT, P).T),
        "ln2_in": np.ascontiguousarray(arr("L0_ffn_ln2_w").reshape(KT, P).T),
        "wq": arr("L0_ffn_wq"), "wk": arr("L0_ffn_wk"), "wv": arr("L0_ffn_wv"), "wo": arr("L0_ffn_wo"),
        "gate_w": np.ascontiguousarray(arr("L0_ffn_gate_w").T),
        "eg_w": np.ascontiguousarray(experts_side_by_side(arr("L0_ffn_eg_w"), arr("L0_ffn_sg_w")).T),
        "eu_w": np.ascontiguousarray(experts_side_by_side(arr("L0_ffn_eu_w"), arr("L0_ffn_su_w")).T),
        "ed_w": experts_side_by_side(arr("L0_ffn_ed_w").transpose(0, 2, 1), arr("L0_ffn_sd_w").T),
        "ident_in": np.eye(P, dtype=np.float32), "ident_bf_in": np.eye(P).astype(bf),
        "causal_in": causal, "local_in": local, "block_mask_in": block_mask, "sel_in": sel.astype(bf),
    }
    nc = bacc.Bacc("TRN2", target_bir_lowering=False, num_devices=1)
    args = [nc.dram_tensor(name, a.shape, mybir.dt.from_np(a.dtype), kind="ExternalInput").ap()
            for name, a in arrays.items()]
    args.append(nc.dram_tensor("out", (TOKENS, D), F32, kind="ExternalOutput").ap())
    macaron_kernel(nc, *args)
    r = run_bass_kernel_spmd(nc, [{k: np.ascontiguousarray(a) for k, a in arrays.items()}], core_ids=[0])
    return r.results[0]["out"].reshape(SEQS, SEQ, D)
```

```python
from contextlib import ExitStack, contextmanager

import concourse.bass as bass
from concourse import mybir

F32 = mybir.dt.float32
F32R = mybir.dt.float32r
BF16 = mybir.dt.bfloat16
ALU = mybir.AluOpType
ACT = mybir.ActivationFunctionType
AX = mybir.AxisListType

P = 128
SEQS, SEQ, D = 4, 512, 256
TOKENS = SEQS * SEQ
TILES = TOKENS // P
TPS = SEQ // P
KT = D // P
HEADS, HD = 16, 128
GROUP = 4
GROUPS = HEADS // GROUP
GW = GROUP * HD
STEPS = SEQS * GROUP
EXPERTS, TOPK, INNER, SHARED = 16, 6, 176, 352
CHUNKS = -(-(EXPERTS * INNER + SHARED) // P)
CPG = 5
CHUNK_GROUPS = CHUNKS // CPG
UNITS = SEQS * CPG
CW_ROWS = 3 * (EXPERTS + 1)
LN_EPS, RMS_EPS, DEN_EPS = 1e-5, 1e-6, 1e-6
SCALE = float(HD) ** -0.5
WIDTH = [P * (i + 1) for i in range(TPS)]
E_AT = [sum(WIDTH[:i]) for i in range(TPS)]
E_ALL = sum(WIDTH)
DOWN = list(range(TPS - 1, -1, -1))


@contextmanager
def phase_semaphores(nc):
    held = []

    def new_sem(name):
        held.append(nc.alloc_semaphore(name=name))
        return held[-1]

    yield new_sem
    nc.clear_and_free_semaphores(held)
    nc.all_engine_barrier()


def product(pe, out, a_hi, a_lo, b_hi, b_lo, first, last, shared_bank=False):
    pe.matmul(out, a_hi, b_hi, start=first, stop=False, skip_group_check=shared_bank)
    pe.matmul(out, a_hi, b_lo, start=False, stop=False, skip_group_check=shared_bank)
    return pe.matmul(out, a_lo, b_hi, start=False, stop=last, skip_group_check=shared_bank)


def norm_phase(nc, tag, src, ln_out, rms, weight, hT_hi, hT_lo, ident, loads=None, add_row=None):
    with ExitStack() as ctx:
        new_sem = ctx.enter_context(phase_semaphores(nc))

        def sb(name, shape, dt=F32):
            return ctx.enter_context(nc.sbuf_tensor(f"{tag}_{name}", shape, dt))

        def sem(name):
            return new_sem(f"{tag}_{name}")

        z = sb("z", [P, TILES, D])
        stats = sb("stats", [P, TILES, 6])
        mv = sb("mv", [P, TILES, 2])
        small = sb("small", [P, 6, TILES])
        var, std, rstd, ms, rms_std, rrms = (small[:, i, :] for i in range(6))
        squares = sb("squares", [P, TILES])
        BANKS = 4
        tp = ctx.enter_context(nc.psum_tensor(f"{tag}_tp", [P, BANKS, 512], F32))

        loaded = sem("loaded")
        stats_done = sem("stats_done")
        aggr_done = sem("aggr_done")
        var_ready = sem("var_ready")
        std_ready = sem("std_ready")
        rstd_ready = sem("rstd_ready")
        normed = sem("normed")
        squared = sem("squared")
        ms_ready = sem("ms_ready")
        rms_std_ready = sem("rms_std_ready")
        rrms_ready = sem("rrms_ready")
        z_ready = sem("z_ready")
        turned = sem("turned")
        hi_done = sem("hi_done")
        split_done = sem("split_done")
        block = ctx.enter_context(nc.Block())

        ln = ln_out is not None
        ln_dst = ln_out if rms else z
        n_loads = len(loads or [])

        @block.sync
        def _(sp):
            for dst, src_dram in loads or []:
                sp.dma_start(dst, src_dram).then_inc(loaded, 16)
            if n_loads:
                sp.wait_ge(loaded, 16 * n_loads)

        @block.vector
        def _(dve):
            dve.sem_inc(split_done, BANKS)
            if n_loads:
                dve.wait_ge(loaded, 16 * n_loads)
            if ln:
                for t in range(TILES):
                    dve.bn_stats(stats[:, t, :], src[:, t, :]).then_inc(stats_done, 1)
                for t in range(TILES):
                    dve.wait_ge(stats_done, t + 1)
                    dve.bn_aggr(mv[:, t, :], stats[:, t, :]).then_inc(aggr_done, 1)
                dve.wait_ge(aggr_done, TILES)
                dve.tensor_scalar(var, mv[:, :, 1], LN_EPS, None, ALU.add).then_inc(var_ready, 1)
                dve.wait_ge(std_ready, 1)
                dve.reciprocal(rstd, std).then_inc(rstd_ready, 1)
                dve.wait_ge(rstd_ready, 1)
                for t in range(TILES):
                    dve.tensor_scalar(ln_dst[:, t, :], src[:, t, :], mv[:, t, 0:1], rstd[:, t:t + 1],
                                      ALU.subtract, ALU.mult).then_inc(normed, 1)
            if rms:
                dve.wait_ge(squared, TILES)
                dve.tensor_scalar(ms, squares[:, :], 1.0 / D, RMS_EPS, ALU.mult, ALU.add).then_inc(ms_ready, 1)
                dve.wait_ge(rms_std_ready, 1)
                dve.reciprocal(rrms, rms_std).then_inc(rrms_ready, 1)
                dve.wait_ge(rrms_ready, 1)
            if add_row is not None:
                dve.wait_ge(normed, TILES)
                dve.tensor_tensor(src[:, :, :], src[:, :, :],
                                  add_row.unsqueeze(1).to_broadcast([P, TILES, D]), ALU.add).then_inc(rstd_ready, 1)

            def scaled(b):
                for t in range(TPS * b, TPS * b + TPS):
                    y = ln_out if ln else src
                    last = dve.tensor_scalar(z[:, t, :], y[:, t, :], rrms[:, t:t + 1], None, ALU.mult)
                last.then_inc(z_ready, 1)

            if rms:
                scaled(0)
            for b in range(SEQS):
                if rms and b + 1 < SEQS:
                    scaled(b + 1)
                for k in range(KT):
                    n = KT * b + k
                    dve.wait_ge(hi_done, n + 1)
                    bank = tp[:, n % BANKS, :]
                    at = slice(SEQ * b, SEQ * b + SEQ)
                    if weight is None:
                        dve.tensor_tensor(hT_lo[:, k, at], bank, hT_hi[:, k, at].bitcast(F32),
                                          ALU.subtract).then_inc(split_done, 1)
                    else:
                        dve.scalar_tensor_tensor(out=hT_lo[:, k, at], in0=bank, scalar=weight[:, k:k + 1],
                                                 in1=hT_hi[:, k, at].bitcast(F32), op0=ALU.mult,
                                                 op1=ALU.subtract).then_inc(split_done, 1)

        @block.scalar
        def _(act):
            if ln:
                act.wait_ge(var_ready, 1)
                act.activation(std, var, ACT.Sqrt).then_inc(std_ready, 1)
            if rms:
                for t in range(TILES):
                    if ln:
                        act.wait_ge(normed, t + 1)
                    act.activation(z[:, t, :], (ln_out if ln else src)[:, t, :], ACT.Square,
                                   accum_out=squares[:, t:t + 1]).then_inc(squared, 1)
                act.wait_ge(ms_ready, 1)
                act.activation(rms_std, ms, ACT.Sqrt).then_inc(rms_std_ready, 1)
            for b in range(SEQS):
                for k in range(KT):
                    n = KT * b + k
                    act.wait_ge(turned, n + 1)
                    act.activation(hT_hi[:, k, SEQ * b:SEQ * b + SEQ], tp[:, n % BANKS, :], ACT.Copy,
                                   scale=1.0 if weight is None else weight[:, k:k + 1]).then_inc(hi_done, 1)

        @block.tensor
        def _(pe):
            for b in range(SEQS):
                if rms:
                    pe.wait_ge(z_ready, b + 1)
                else:
                    pe.wait_ge(normed, TPS * b + TPS)
                for k in range(KT):
                    n = KT * b + k
                    pe.wait_ge(split_done, n + 1)
                    for i in range(TPS):
                        last = pe.transpose(tp[:, n % BANKS, P * i:P * i + P],
                                            z[:, TPS * b + i, P * k:P * k + P], ident[:, :])
                    last.then_inc(turned, 1)


def projection_order():
    order = [("q", 0), ("k", 0)] + [("v", 0, t) for t in range(TPS)]
    for n in range(STEPS):
        if n + 1 < STEPS:
            order += [("q", n + 1), ("k", n + 1)]
        order += extra_units(n)
    return order + [("o", SEQS - 1, m) for m in range(2)]


def extra_units(n):
    b, h = divmod(n, GROUP)
    return ([("v", b + 1, h)] if b + 1 < SEQS else []) + ([("o", b - 1, m) for m in range(2)] if h == 1 and b else [])


PROJ = projection_order()
PROJ_AT = {unit: u for u, unit in enumerate(PROJ)}
PROJS = len(PROJ)
SPLIT = [unit for unit in PROJ if unit[0] != "o"]
SPLIT_AT = {unit: u for u, unit in enumerate(SPLIT)}
SPLITS = len(SPLIT)
PIECES = ["qk0", "v", "qk1", "qk2", "qk3", "o"]
NP = len(PIECES)
PROJ_BANKS, S_BANKS, T_BANKS = 2, 2, 3
S_UNITS = [[3], [2], [1, 0]]
SU = len(S_UNITS)
LINEAR_BANK, LOCAL_BANK = [0, 0, 1], 1
T_UNITS = [[0], [1], [2, 3]]
TU = len(T_UNITS)
PT_AT = [sum(SEQ - P * i for i in range(j)) for j in range(TPS)]
LOADS = [("qk0", 4), ("qk1", 5), ("v", 6), ("qk2", NP + 1), ("qk3", NP + 3), ("o", NP + 2)]


def turned_columns(tiles):
    w = sum(SEQ - P * j for j in tiles)
    return slice(PT_AT[tiles[0]], PT_AT[tiles[0]] + w), w


def attention_phase(nc, tag, linear, hT_hi, hT_lo, acc, w_dram, consts):
    wq_dram, wk_dram, wv_dram, wo_dram = w_dram
    ident, ident_bf, causal_bf, local_bf, block_mask, phi_scale, phi_bias = consts
    with ExitStack() as ctx:
        new_sem = ctx.enter_context(phase_semaphores(nc))

        def sb(name, shape, dt=F32):
            return ctx.enter_context(nc.sbuf_tensor(f"{tag}_{name}", shape, dt))

        def ps(name, banks):
            return ctx.enter_context(nc.psum_tensor(f"{tag}_{name}", [P, banks, 512], F32))

        def sem(name):
            return new_sem(f"{tag}_{name}")

        raw_qk = sb("raw_qk", [P, 2, 2, KT, HD])
        raw_vo = sb("raw_vo", [P, KT * GW])
        raw_v = raw_vo[:, :].rearrange("p (k n) -> p k n", k=KT)
        raw_o = raw_vo[:, :].rearrange("p (h d) -> p h d", h=GROUP)
        wqk_hi, wqk_lo = (sb(f"wqk_{s}", [P, 2, KT, GW], F32R) for s in ("hi", "lo"))
        wv_hi, wv_lo = (sb(f"wv_{s}", [P, KT, GW], F32R) for s in ("hi", "lo"))
        wo_hi, wo_lo = (sb(f"wo_{s}", [P, GROUP, D], F32R) for s in ("hi", "lo"))
        qk_hi, qk_lo = (sb(f"qk_{s}", [P, 2, 2, SEQ], F32R) for s in ("hi", "lo"))
        v_hi, v_lo = (sb(f"v_{s}", [P, 2, TPS, GW], F32R) for s in ("hi", "lo"))
        e = sb("e", [P, 2, E_ALL])
        pt_hi, pt_lo = (sb(f"pt_{s}", [P, E_ALL], F32R) for s in ("hi", "lo"))
        ao_hi, ao_lo = (sb(f"ao_{s}", [P, GROUP, SEQ], F32R) for s in ("hi", "lo"))
        nmax = sb("nmax", [P, 2, TPS])
        den = sb("den", [P, 2, 2, TPS])
        rden = sb("rden", [P, 2, 2, TPS])
        if linear:
            loc = sb("loc", [P, 2, TPS, P])
            phi_hi, phi_lo = (sb(f"phi_{s}", [P, 2, 2, SEQ], F32R) for s in ("hi", "lo"))
            phi_sc = sb("phi_sc", [P, 2, GROUP])
            exp_z = sb("exp_z", [P, 2, SEQ])
            relu_z = sb("relu_z", [P, 2, SEQ])

        proj_ps = ps("proj_ps", PROJ_BANKS)
        s_ps = ps("s_ps", S_BANKS)
        t_ps = ps("t_ps", T_BANKS)
        pv_ps = ps("pv_ps", 1)

        raw_loaded = [sem(f"raw_{p}") for p in PIECES]
        w_hi_done = sem("w_hi_done")
        w_split = sem("w_split")
        proj_done = sem("proj_done")
        proj_hi = sem("proj_hi")
        proj_split = sem("proj_split")
        s_done = sem("s_done")
        max_done = sem("max_done")
        exp_done = sem("exp_done")
        rden_done = sem("rden_done")
        normed = sem("normed")
        t_done = sem("t_done")
        t_hi = sem("t_hi")
        t_split = sem("t_split")
        pv_done = sem("pv_done")
        ao_hi_done = sem("ao_hi_done")
        ao_split = sem("ao_split")
        dve_step = sem("dve_step")
        if linear:
            phi_loaded = sem("phi_loaded")
            local_done = sem("local_done")
            a_read = sem("a_read")
            phi_done = sem("phi_done")
            phi_step = sem("phi_step")
            pool_step = sem("pool_step")
        block = ctx.enter_context(nc.Block())

        @block.sync
        def _(sp):
            with sp.Fori(0, GROUPS) as g:
                for piece, count in LOADS:
                    done = raw_loaded[PIECES.index(piece)]
                    if linear and piece == "qk2":
                        sp.wait_ge(proj_hi, SPLITS * g + SPLIT_AT[("k", STEPS - 1)] + 1)
                        for j, a in enumerate((phi_scale, phi_bias)):
                            sp.dma_start(phi_sc[:, j, :], a[:, bass.ds(g * GROUP, GROUP)]).then_inc(phi_loaded, 16)
                    sp.wait_ge(w_split, NP * g + count)
                    if piece == "v":
                        sp.dma_start(raw_v, wv_dram[:, :, bass.ds(g * GW, GW)]).then_inc(done, 16)
                    elif piece == "o":
                        sp.dma_start(raw_o, wo_dram[:, bass.ds(g * GROUP, GROUP), :]).then_inc(done, 16)
                    else:
                        h = int(piece[2])
                        for j, w in enumerate((wq_dram, wk_dram)):
                            sp.dma_start(raw_qk[:, h % 2, j, :, :],
                                         w[:, :, bass.ds(g * GW + HD * h, HD)]).then_inc(done, 16)

        def piece_views(piece):
            if piece == "v":
                return [(raw_v, wv_hi[:, :, :], wv_lo[:, :, :])]
            if piece == "o":
                return [(raw_o, wo_hi[:, :, :], wo_lo[:, :, :])]
            h = int(piece[2])
            at = slice(HD * h, HD * h + HD)
            return [(raw_qk[:, h % 2, j, :, :], wqk_hi[:, j, :, at], wqk_lo[:, j, :, at]) for j in range(2)]

        @block.gpsimd
        def _(pool):
            pool.sem_inc(w_split, NP)

            def weights_lo(g, p):
                pool.wait_ge(w_hi_done, NP * g + p + 1)
                for raw, hi, lo in piece_views(PIECES[p]):
                    last = pool.tensor_tensor(lo, raw, hi.bitcast(F32), ALU.subtract)
                last.then_inc(w_split, 1)

            def normalise(g, n):
                buf = n % 2
                pool.wait_ge(rden_done, STEPS * g + n + 1)
                if linear:
                    pool.tensor_tensor(loc[:, buf, :, :], loc[:, buf, :, :],
                                       rden[:, buf, 0, :].unsqueeze(2).to_broadcast([P, TPS, P]),
                                       ALU.mult).then_inc(pool_step, 1)
                for i in DOWN:
                    w = e[:, buf, E_AT[i]:E_AT[i] + WIDTH[i]]
                    last = pool.tensor_tensor(w, w, rden[:, buf, int(linear), i:i + 1].to_broadcast([P, WIDTH[i]]),
                                              ALU.mult)
                    if linear:
                        last.then_inc(pool_step, 1)
                if linear:
                    pool.wait_ge(pool_step, (1 + TPS) * (STEPS * g + n + 1))
                    for i in DOWN:
                        w = e[:, buf, E_AT[i] + P * i:E_AT[i] + P * i + P]
                        last = pool.tensor_tensor(w, w, loc[:, buf, i, :], ALU.add)
                last.then_inc(normed, 1)

            with pool.Fori(0, GROUPS) as g:
                for p in range(3):
                    weights_lo(g, p)
                for n in range(STEPS):
                    if n < NP - 3:
                        weights_lo(g, 3 + n)
                    normalise(g, n)

        @block.tensor
        def _(pe):
            pe.sem_inc(proj_done, PROJS)

            def project(g, unit):
                u = PROJ_AT[unit]
                out = proj_ps[:, u % PROJ_BANKS, :]
                pe.wait_ge(proj_split, PROJS * g + u + 1)
                if unit[0] == "o":
                    last = out_project(g, unit[1], unit[2], out)
                elif unit[0] == "v":
                    _, b, t = unit
                    if unit == ("v", 0, 0):
                        pe.wait_ge(w_split, NP + NP * g + PIECES.index("v") + 1)
                    at = slice(SEQ * b + P * t, SEQ * b + P * t + P)
                    for k in range(KT):
                        last = product(pe, out, hT_hi[:, k, at], hT_lo[:, k, at], wv_hi[:, k, :], wv_lo[:, k, :],
                                       k == 0, k == KT - 1)
                else:
                    j, (b, h) = "qk".index(unit[0]), divmod(unit[1], GROUP)
                    if b == 0:
                        pe.wait_ge(w_split, NP + NP * g + PIECES.index(f"qk{h}") + 1)
                    cols, at = slice(HD * h, HD * h + HD), slice(SEQ * b, SEQ * b + SEQ)
                    for k in range(KT):
                        last = product(pe, out, wqk_hi[:, j, k, cols], wqk_lo[:, j, k, cols],
                                       hT_hi[:, k, at], hT_lo[:, k, at], k == 0, k == KT - 1)
                last.then_inc(proj_done, 1)

            def scores(g, n, unit):
                buf = n % 2
                bank = s_ps[:, (LINEAR_BANK[unit] if linear else unit + SU * n) % S_BANKS, :]
                if not linear:
                    pe.wait_ge(exp_done, SU * (STEPS * g + n) + unit + 1)
                elif unit == 2:
                    pe.wait_ge(exp_done, STEPS * g + n + 1)
                else:
                    pe.wait_ge(a_read, SU * (STEPS * g + n) + SU + (-1, 1)[unit])
                a_hi, a_lo = (phi_hi, phi_lo) if linear else (qk_hi, qk_lo)
                if linear:
                    pe.wait_ge(phi_done, 2 + 2 * (STEPS * g + n) + 2)
                else:
                    pe.wait_ge(proj_split, PROJ_BANKS + PROJS * g + PROJ_AT[("k", n)] + 1)
                start = 0
                for i in S_UNITS[unit]:
                    at, out = slice(P * i, P * i + P), bank[:, start:start + WIDTH[i]]
                    last = product(pe, out, a_hi[:, 0, buf, at], a_lo[:, 0, buf, at],
                                   a_hi[:, 1, buf, 0:WIDTH[i]], a_lo[:, 1, buf, 0:WIDTH[i]], True, linear)
                    if not linear:
                        last = pe.matmul(out[:, P * i:P * i + P], ident_bf[:, :], causal_bf[:, :],
                                         start=False, stop=True)
                    start += WIDTH[i]
                last.then_inc(s_done, 1)

            def local_scores(g, n):
                buf = n % 2
                out = s_ps[:, LOCAL_BANK, :]
                pe.wait_ge(a_read, SU * (STEPS * g + n) + SU)
                pe.wait_ge(proj_split, PROJ_BANKS + PROJS * g + PROJ_AT[("k", n)] + 1)
                pe.matmul(out, ident_bf[:, :], local_bf[:, :], start=True, stop=False)
                for i in range(TPS):
                    at = slice(P * i, P * i + P)
                    last = product(pe, out[:, at], qk_hi[:, 0, buf, at], qk_lo[:, 0, buf, at],
                                   qk_hi[:, 1, buf, at], qk_lo[:, 1, buf, at], False, i == TPS - 1)
                last.then_inc(local_done, 1)

            def turn(g, n):
                pe.wait_ge(normed, STEPS * g + n + 1)
                for unit, tiles in enumerate(T_UNITS):
                    pe.wait_ge(t_split, TU * (STEPS * g + n) + unit + 1)
                    for j in tiles:
                        for i in range(j, TPS):
                            start = PT_AT[j] - PT_AT[tiles[0]] + P * (i - j)
                            last = pe.transpose(t_ps[:, unit, start:start + P],
                                                e[:, n % 2, E_AT[i] + P * j:E_AT[i] + P * j + P], ident[:, :])
                    last.then_inc(t_done, 1)

            def times_v(g, n):
                b, h = divmod(n, GROUP)
                pe.wait_ge(ao_split, STEPS * g + n + 1)
                pe.wait_ge(proj_split, PROJ_BANKS + PROJS * g + PROJ_AT[("v", b, TPS - 1)] + 1)
                cols = slice(HD * h, HD * h + HD)
                for unit, tiles in enumerate(T_UNITS):
                    pe.wait_ge(t_split, T_BANKS + TU * (STEPS * g + n) + unit + 1)
                    for j in tiles:
                        at = slice(PT_AT[j], PT_AT[j] + SEQ - P * j)
                        last = product(pe, pv_ps[:, 0, P * j:SEQ], v_hi[:, b % 2, j, cols], v_lo[:, b % 2, j, cols],
                                       pt_hi[:, at], pt_lo[:, at], j == 0, j == TPS - 1)
                last.then_inc(pv_done, 1)

            def out_project(g, b, m, bank):
                if b == 0 and m == 0:
                    pe.wait_ge(w_split, NP + NP * g + PIECES.index("o") + 1)
                pe.wait_ge(ao_split, 1 + STEPS * g + GROUP * b + GROUP)
                for half in range(2):
                    at = slice(P * (2 * m + half), P * (2 * m + half) + P)
                    for h in range(GROUP):
                        last = product(pe, bank[:, D * half:D * half + D], ao_hi[:, h, at], ao_lo[:, h, at],
                                       wo_hi[:, h, :], wo_lo[:, h, :], h == 0, h == GROUP - 1)
                return last

            with pe.Fori(0, GROUPS) as g:
                for unit in PROJ[:2 + TPS]:
                    project(g, unit)
                for n in range(STEPS + 1):
                    if n < STEPS:
                        scores(g, n, 0)
                        if linear:
                            local_scores(g, n)
                    if n + 1 < STEPS:
                        project(g, ("q", n + 1))
                    if n < STEPS:
                        for unit in range(1, SU):
                            scores(g, n, unit)
                    if n >= 1:
                        turn(g, n - 1)
                    if n + 1 < STEPS:
                        project(g, ("k", n + 1))
                    if n % GROUP == 0 and n >= 1:
                        times_v(g, n - 1)
                    if n < STEPS:
                        for unit in extra_units(n):
                            project(g, unit)
                    if n % GROUP:
                        times_v(g, n - 1)
                for m in range(2):
                    project(g, ("o", SEQS - 1, m))

        @block.scalar
        def _(act):
            act.sem_inc(proj_hi, SPLITS)
            if not linear:
                act.sem_inc(exp_done, S_BANKS)

            def weights_hi(g, p):
                piece = PIECES[p]
                n_dma = 1 if piece in "vo" else 2
                act.wait_ge(raw_loaded[p], 16 * n_dma * (g + 1))
                if piece == "o":
                    act.wait_ge(proj_done, PROJS * g + PROJ_AT[("o", SEQS - 1, 1)] + 1)
                elif piece == "v":
                    act.wait_ge(proj_done, PROJS * g + PROJ_AT[("v", SEQS - 1, TPS - 1)] + 1)
                else:
                    act.wait_ge(proj_done, PROJS * g + PROJ_AT[("k", STEPS - GROUP + int(piece[2]))] + 1)
                for raw, hi, _ in piece_views(piece):
                    last = act.activation(hi, raw, ACT.Copy)
                last.then_inc(w_hi_done, 1)

            def project_hi(g, unit):
                u = PROJ_AT[unit]
                bank = proj_ps[:, u % PROJ_BANKS, :]
                act.wait_ge(proj_done, PROJS + PROJS * g + u + 1)
                if unit[0] == "v":
                    last = act.activation(v_hi[:, unit[1] % 2, unit[2], :], bank, ACT.Copy)
                else:
                    j, n = "qk".index(unit[0]), unit[1]
                    last = act.activation(qk_hi[:, j, n % 2, :], bank, ACT.Copy, scale=SCALE if j == 0 else 1.0)
                    if linear:
                        act.wait_ge(phi_done, 2 * (STEPS * g + n) + j + 1)
                        act.wait_ge(phi_loaded, 32 * (g + 1))
                        s, c = (phi_sc[:, i, n % GROUP:n % GROUP + 1] for i in range(2))
                        act.activation(exp_z[:, j, :], bank, ACT.Exp, bias=c, scale=s)
                        last = act.activation(relu_z[:, j, :], bank, ACT.Relu, bias=c, scale=s)
                last.then_inc(proj_hi, 1)

            def exponents(g, n, unit):
                buf, start = n % 2, 0
                act.wait_ge(max_done, SU * (STEPS * g + n) + unit + 1)
                for i in S_UNITS[unit]:
                    last = act.activation(e[:, buf, E_AT[i]:E_AT[i] + WIDTH[i]],
                                          s_ps[:, (SU * n + unit) % S_BANKS, start:start + WIDTH[i]],
                                          ACT.Exp, bias=nmax[:, buf, i:i + 1], accum_out=den[:, buf, 0, i:i + 1])
                    start += WIDTH[i]
                last.then_inc(exp_done, 1)

            def local_exponents(g, n):
                buf = n % 2
                act.wait_ge(max_done, STEPS * g + n + 1)
                for i in range(TPS):
                    last = act.activation(loc[:, buf, i, :], s_ps[:, LOCAL_BANK, P * i:P * i + P],
                                          ACT.Exp, bias=nmax[:, buf, i:i + 1], accum_out=den[:, buf, 0, i:i + 1])
                last.then_inc(exp_done, 1)

            def turned_hi(g, n):
                for unit, tiles in enumerate(T_UNITS):
                    act.wait_ge(t_done, TU * (STEPS * g + n) + unit + 1)
                    at, w = turned_columns(tiles)
                    act.activation(pt_hi[:, at], t_ps[:, unit, 0:w], ACT.Copy).then_inc(t_hi, 1)

            def out_hi(g, n):
                act.wait_ge(pv_done, STEPS * g + n + 1)
                act.activation(ao_hi[:, n % GROUP, :], pv_ps[:, 0, :], ACT.Copy).then_inc(ao_hi_done, 1)

            with act.Fori(0, GROUPS) as g:
                weights_hi(g, 0)
                weights_hi(g, 1)
                project_hi(g, ("q", 0))
                project_hi(g, ("k", 0))
                weights_hi(g, 2)
                for t in range(TPS):
                    project_hi(g, ("v", 0, t))
                for n in range(STEPS + 1):
                    if n < NP - 3:
                        weights_hi(g, 3 + n)
                    if n < STEPS:
                        if linear:
                            local_exponents(g, n)
                        else:
                            exponents(g, n, 0)
                    if n + 1 < STEPS:
                        project_hi(g, ("q", n + 1))
                    if n < STEPS and not linear:
                        for unit in range(1, SU):
                            exponents(g, n, unit)
                    if n >= 1:
                        turned_hi(g, n - 1)
                    if n + 1 < STEPS:
                        project_hi(g, ("k", n + 1))
                    if n % GROUP == 0 and n >= 1:
                        out_hi(g, n - 1)
                    if n < STEPS:
                        for unit in extra_units(n):
                            if unit[0] == "v":
                                project_hi(g, unit)
                    if n % GROUP:
                        out_hi(g, n - 1)

        @block.vector
        def _(dve):
            dve.sem_inc(proj_split, PROJ_BANKS)
            dve.sem_inc(t_split, T_BANKS)
            dve.sem_inc(ao_split, 1)
            if linear:
                dve.sem_inc(a_read, SU)
                dve.sem_inc(phi_done, 2)

            def project_lo(g, unit):
                u = PROJ_AT[unit]
                bank = proj_ps[:, u % PROJ_BANKS, :]
                if unit[0] == "o":
                    dve.wait_ge(proj_done, PROJS + PROJS * g + u + 1)
                    t = TPS * unit[1] + 2 * unit[2]
                    dve.tensor_tensor(acc[:, t:t + 2, :], bank.rearrange("p (t d) -> p t d", d=D),
                                      acc[:, t:t + 2, :], ALU.add).then_inc(proj_split, 1)
                    return
                dve.wait_ge(proj_hi, SPLITS + SPLITS * g + SPLIT_AT[unit] + 1)
                if unit[0] == "v":
                    at = (slice(None), unit[1] % 2, unit[2], slice(None))
                    dve.tensor_tensor(v_lo[at], bank, v_hi[at].bitcast(F32), ALU.subtract).then_inc(proj_split, 1)
                    return
                j, n = "qk".index(unit[0]), unit[1]
                at = (slice(None), j, n % 2, slice(None))
                if j == 0:
                    dve.scalar_tensor_tensor(out=qk_lo[at], in0=bank, scalar=SCALE, in1=qk_hi[at].bitcast(F32),
                                             op0=ALU.mult, op1=ALU.subtract).then_inc(proj_split, 1)
                else:
                    dve.tensor_tensor(qk_lo[at], bank, qk_hi[at].bitcast(F32), ALU.subtract).then_inc(proj_split, 1)
                if linear:
                    u = 2 * n + j
                    dve.scalar_tensor_tensor(out=relu_z[:, j, :], in0=exp_z[:, j, :], scalar=1.0, in1=relu_z[:, j, :],
                                             op0=ALU.min, op1=ALU.add).then_inc(phi_step, 1)
                    dve.wait_ge(phi_step, 4 * STEPS * g + 2 * u + 1)
                    dve.tensor_scalar(phi_hi[at], relu_z[:, j, :], 10.0, None, ALU.min).then_inc(phi_step, 1)
                    dve.wait_ge(phi_step, 4 * STEPS * g + 2 * u + 2)
                    dve.scalar_tensor_tensor(out=phi_lo[at], in0=relu_z[:, j, :], scalar=10.0,
                                             in1=phi_hi[at].bitcast(F32), op0=ALU.min,
                                             op1=ALU.subtract).then_inc(phi_done, 1)

            def row_max(g, n, unit):
                dve.wait_ge(s_done, SU * (STEPS * g + n) + unit + 1)
                start = 0
                for i in S_UNITS[unit]:
                    last = dve.tensor_reduce(nmax[:, n % 2, i:i + 1],
                                             s_ps[:, (SU * n + unit) % S_BANKS, start:start + WIDTH[i]],
                                             AX.X, ALU.max, negate=True)
                    start += WIDTH[i]
                last.then_inc(max_done, 1)

            def local_max(g, n):
                dve.wait_ge(local_done, STEPS * g + n + 1)
                dve.tensor_reduce(nmax[:, n % 2, :],
                                  s_ps[:, LOCAL_BANK, :].rearrange("p (i k) -> p i k", k=P),
                                  AX.X, ALU.max, negate=True).then_inc(max_done, 1)

            def linear_weights(g, n, unit):
                dve.wait_ge(s_done, SU * (STEPS * g + n) + unit + 1)
                start = 0
                for i in S_UNITS[unit]:
                    last = dve.tensor_tensor_reduce(e[:, n % 2, E_AT[i]:E_AT[i] + WIDTH[i]],
                                                    s_ps[:, LINEAR_BANK[unit], start:start + WIDTH[i]],
                                                    block_mask[:, SEQ - WIDTH[i]:SEQ], 1.0, 0.0, ALU.mult, ALU.add,
                                                    den[:, n % 2, 1, i:i + 1])
                    start += WIDTH[i]
                last.then_inc(a_read, 1)

            def invert(g, n):
                buf = n % 2
                if linear:
                    dve.wait_ge(exp_done, STEPS * g + n + 1)
                    dve.wait_ge(a_read, SU + SU * (STEPS * g + n + 1))
                    dve.tensor_scalar(den[:, buf, :, :], den[:, buf, :, :], DEN_EPS, None,
                                      ALU.max).then_inc(dve_step, 1)
                    dve.wait_ge(dve_step, STEPS * g + n + 1)
                    dve.reciprocal(rden[:, buf, :, :], den[:, buf, :, :]).then_inc(rden_done, 1)
                else:
                    dve.wait_ge(exp_done, S_BANKS + SU * (STEPS * g + n + 1))
                    dve.reciprocal(rden[:, buf, 0, :], den[:, buf, 0, :]).then_inc(rden_done, 1)

            def turned_lo(g, n):
                for unit, tiles in enumerate(T_UNITS):
                    dve.wait_ge(t_hi, TU * (STEPS * g + n) + unit + 1)
                    at, w = turned_columns(tiles)
                    dve.tensor_tensor(pt_lo[:, at], t_ps[:, unit, 0:w], pt_hi[:, at].bitcast(F32),
                                      ALU.subtract).then_inc(t_split, 1)

            def out_lo(g, n):
                dve.wait_ge(ao_hi_done, STEPS * g + n + 1)
                h = n % GROUP
                dve.tensor_tensor(ao_lo[:, h, :], pv_ps[:, 0, :], ao_hi[:, h, :].bitcast(F32),
                                  ALU.subtract).then_inc(ao_split, 1)

            with dve.Fori(0, GROUPS) as g:
                for unit in PROJ[:2 + TPS]:
                    project_lo(g, unit)
                for n in range(STEPS + 1):
                    if n < STEPS:
                        if linear:
                            linear_weights(g, n, 0)
                            local_max(g, n)
                        else:
                            row_max(g, n, 0)
                    if n + 1 < STEPS:
                        project_lo(g, ("q", n + 1))
                    if n < STEPS:
                        for unit in range(1, SU):
                            if linear:
                                linear_weights(g, n, unit)
                            else:
                                row_max(g, n, unit)
                    if n >= 1:
                        turned_lo(g, n - 1)
                    if n < STEPS:
                        invert(g, n)
                    if n + 1 < STEPS:
                        project_lo(g, ("k", n + 1))
                    if n % GROUP == 0 and n >= 1:
                        out_lo(g, n - 1)
                    if n < STEPS:
                        for unit in extra_units(n):
                            project_lo(g, unit)
                    if n % GROUP:
                        out_lo(g, n - 1)
                for m in range(2):
                    project_lo(g, ("o", SEQS - 1, m))


def routing_phase(nc, tag, tT_hi, tT_lo, gate_dram, ident_bf, cwT):
    E1 = EXPERTS + 1
    with ExitStack() as ctx:
        new_sem = ctx.enter_context(phase_semaphores(nc))

        def sb(name, shape, dt=F32):
            return ctx.enter_context(nc.sbuf_tensor(f"{tag}_{name}", shape, dt))

        def sem(name):
            return new_sem(f"{tag}_{name}")

        gate = sb("gate", [P, KT, EXPERTS])
        gate_hi, gate_lo = (sb(f"gate_{s}", [P, KT, EXPERTS], F32R) for s in ("hi", "lo"))
        rowmax = sb("rowmax", [P, TILES])
        rowsum = sb("rowsum", [P, TILES])
        rsum = sb("rsum", [P, TILES])
        topsum = sb("topsum", [P, TILES])
        rtop = sb("rtop", [P, TILES])
        shifted = sb("shifted", [P, TILES, EXPERTS])
        ex = sb("ex", [P, TILES, EXPERTS])
        probs = sb("probs", [P, TILES, EXPERTS + 2])
        top8 = sb("top8", [P, TILES, 8])
        rest = sb("rest", [P, TILES, EXPERTS + 2])
        sel = sb("sel", [P, TILES, EXPERTS])
        cw = sb("cw", [P, TILES, EXPERTS])
        left1 = sb("left1", [P, TILES, EXPERTS])
        left2 = sb("left2", [P, TILES, EXPERTS])
        cw3 = sb("cw3", [P, TILES, CW_ROWS], BF16)
        logits = ctx.enter_context(nc.psum_tensor(f"{tag}_logits", [P, TILES, EXPERTS], F32))
        cw_ps = ctx.enter_context(nc.psum_tensor(f"{tag}_cw_ps", [P, 2, 8 * P], BF16))

        loaded, split, logits_done, vec = sem("loaded"), sem("split"), sem("logits_done"), sem("vec")
        shifted_done, exp_done, cw_ready, turned, copied = (
            sem("shifted_done"), sem("exp_done"), sem("cw_ready"), sem("turned"), sem("copied"))
        block = ctx.enter_context(nc.Block())

        @block.sync
        def _(sp):
            sp.dma_start(gate[:, :, :], gate_dram).then_inc(loaded, 16)

        @block.tensor
        def _(pe):
            pe.wait_ge(split, 2)
            for t in range(TILES):
                for k in range(KT):
                    last = product(pe, logits[:, t, :], tT_hi[:, k, P * t:P * t + P], tT_lo[:, k, P * t:P * t + P],
                                   gate_hi[:, k, :], gate_lo[:, k, :], k == 0, k == KT - 1)
            last.then_inc(logits_done, 1)
            pe.wait_ge(cw_ready, 1)
            for t in range(TILES):
                last = pe.transpose(cw_ps[0:CW_ROWS, t // 8, P * (t % 8):P * (t % 8) + P], cw3[:, t, :], ident_bf[:, :])
            last.then_inc(turned, 1)

        @block.scalar
        def _(act):
            act.wait_ge(shifted_done, 1)
            act.activation(ex[:, :, :], shifted[:, :, :], ACT.Exp).then_inc(exp_done, 1)

        @block.vector
        def _(dve):
            def spread(column):
                return column[:, :].unsqueeze(2).to_broadcast([P, TILES, EXPERTS])

            dve.wait_ge(loaded, 16)
            dve.tensor_copy(gate_hi[:, :, :], gate[:, :, :]).then_inc(split, 1)
            dve.wait_ge(split, 1)
            dve.tensor_tensor(gate_lo[:, :, :], gate[:, :, :], gate_hi[:, :, :].bitcast(F32),
                              ALU.subtract).then_inc(split, 1)
            dve.memset(probs[:, :, EXPERTS:EXPERTS + 1], -1.0)
            dve.memset(probs[:, :, EXPERTS + 1:EXPERTS + 2], -2.0)
            dve.memset(cw3[:, :, EXPERTS:E1], 1.0)
            dve.memset(cw3[:, :, E1 + EXPERTS:2 * E1], 0.0)
            dve.memset(cw3[:, :, 2 * E1 + EXPERTS:3 * E1], 0.0).then_inc(vec, 1)
            dve.wait_ge(logits_done, 1)
            dve.tensor_reduce(rowmax[:, :], logits[:, :, :], AX.X, ALU.max).then_inc(vec, 1)
            dve.wait_ge(vec, 2)
            dve.tensor_tensor(shifted[:, :, :], logits[:, :, :], spread(rowmax), ALU.subtract).then_inc(shifted_done, 1)
            dve.wait_ge(exp_done, 1)
            dve.tensor_reduce(rowsum[:, :], ex[:, :, :], AX.X, ALU.add).then_inc(vec, 1)
            dve.wait_ge(vec, 3)
            dve.reciprocal(rsum[:, :], rowsum[:, :]).then_inc(vec, 1)
            dve.wait_ge(vec, 4)
            dve.tensor_tensor(probs[:, :, 0:EXPERTS], ex[:, :, :], spread(rsum), ALU.mult).then_inc(vec, 1)
            dve.wait_ge(vec, 5)
            for t in range(TILES):
                last = dve.max(top8[:, t, :], probs[:, t, 0:EXPERTS])
            last.then_inc(vec, 1)
            dve.wait_ge(vec, 6)
            dve.memset(top8[:, :, TOPK:TOPK + 1], -1.0).then_inc(vec, 1)
            dve.memset(top8[:, :, TOPK + 1:TOPK + 2], -2.0).then_inc(vec, 1)
            dve.wait_ge(vec, 8)
            for t in range(TILES):
                last = dve.match_replace(rest[:, t, :], top8[:, t, :], probs[:, t, :], 0.0)
            last.then_inc(vec, 1)
            dve.wait_ge(vec, 9)
            dve.tensor_tensor(sel[:, :, :], probs[:, :, 0:EXPERTS], rest[:, :, 0:EXPERTS],
                              ALU.subtract).then_inc(vec, 1)
            dve.wait_ge(vec, 10)
            dve.tensor_reduce(topsum[:, :], sel[:, :, :], AX.X, ALU.add).then_inc(vec, 1)
            dve.wait_ge(vec, 11)
            dve.reciprocal(rtop[:, :], topsum[:, :]).then_inc(vec, 1)
            dve.wait_ge(vec, 12)
            dve.tensor_tensor(cw[:, :, :], sel[:, :, :], spread(rtop), ALU.mult).then_inc(vec, 1)
            dve.wait_ge(vec, 13)
            parts = [cw3[:, :, E1 * i:E1 * i + EXPERTS] for i in range(3)]
            dve.tensor_copy(parts[0], cw[:, :, :]).then_inc(vec, 1)
            dve.wait_ge(vec, 14)
            dve.tensor_tensor(left1[:, :, :], cw[:, :, :], parts[0], ALU.subtract).then_inc(vec, 1)
            dve.wait_ge(vec, 15)
            dve.tensor_copy(parts[1], left1[:, :, :]).then_inc(vec, 1)
            dve.wait_ge(vec, 16)
            dve.tensor_tensor(left2[:, :, :], left1[:, :, :], parts[1], ALU.subtract).then_inc(vec, 1)
            dve.wait_ge(vec, 17)
            dve.tensor_copy(parts[2], left2[:, :, :]).then_inc(cw_ready, 1)
            dve.wait_ge(turned, 1)
            for i in range(2):
                dve.tensor_copy(cwT[:, 8 * P * i:8 * P * i + 8 * P], cw_ps[0:CW_ROWS, i, :]).then_inc(copied, 1)


def experts_phase(nc, tag, tT_hi, tT_lo, cwT, sel_dram, w_dram, y, x, out_dram):
    up_dram, down_dram = w_dram
    sel_words = sel_dram.bitcast(F32)
    with ExitStack() as ctx:
        new_sem = ctx.enter_context(phase_semaphores(nc))

        def sb(name, shape, dt=F32):
            return ctx.enter_context(nc.sbuf_tensor(f"{tag}_{name}", shape, dt))

        def ps(name, banks):
            return ctx.enter_context(nc.psum_tensor(f"{tag}_{name}", [P, banks, 512], F32))

        def sem(name):
            return new_sem(f"{tag}_{name}")

        raw_up = sb("raw_up", [P, CPG, 2, KT, P])
        raw_dn = sb("raw_dn", [P, CPG, D])
        up_hi, up_lo = (sb(f"up_{s}", [P, CPG, 2, KT, P], F32R) for s in ("hi", "lo"))
        dn_hi, dn_lo = (sb(f"dn_{s}", [P, CPG, D], F32R) for s in ("hi", "lo"))
        sel_bf = sb("sel_bf", [CW_ROWS, CPG, P], BF16)
        silu = sb("silu", [P, 2, SEQ])
        prod = sb("prod", [P, 2, SEQ])
        hh = sb("hh", [P, 2, SEQ])
        hh_hi, hh_lo = (sb(f"hh_{s}", [P, 2, SEQ], F32R) for s in ("hi", "lo"))
        g_ps, u_ps, cw_ps, dn_ps = ps("g_ps", 2), ps("u_ps", 2), ps("cw_ps", 2), ps("dn_ps", 2)

        raw_loaded = [sem(f"raw_{c}") for c in range(CPG)]
        sel_loaded = [sem(f"sel_{c}") for c in range(CPG)]
        w_hi_done = sem("w_hi_done")
        w_split = sem("w_split")
        up_done = sem("up_done")
        silu_done = sem("silu_done")
        prod_done = sem("prod_done")
        gated = sem("gated")
        hh_hi_done = sem("hh_hi_done")
        hh_split = sem("hh_split")
        dn_done = sem("dn_done")
        y_added = sem("y_added")
        x_added = sem("x_added")
        stored = sem("stored")
        block = ctx.enter_context(nc.Block())

        @block.sync
        def _(sp):
            with sp.Fori(0, CHUNK_GROUPS) as g:
                for c in range(CPG):
                    sp.wait_ge(w_split, CPG * g + c + 1)
                    for j in range(2):
                        sp.dma_start(raw_up[:, c, j, :, :],
                                     up_dram[j][:, :, bass.ds(g * (CPG * P) + c * P, P)]).then_inc(raw_loaded[c], 16)
                    sp.dma_start(raw_dn[:, c, :], down_dram[bass.ds(g * (CPG * P) + c * P, P), :]).then_inc(raw_loaded[c], 16)
                for c in range(CPG):
                    sp.wait_ge(dn_done, UNITS * g + CPG * (SEQS - 1) + c + 1)
                    sp.dma_start(sel_bf[:, c, :].bitcast(F32),
                                 sel_words[:, bass.ds(g * (CPG * P // 2) + c * P // 2, P // 2)]).then_inc(sel_loaded[c], 16)
            if out_dram is not None:
                for b in range(SEQS):
                    sp.wait_ge(x_added, b + 1)
                    sp.dma_start(out_dram[:, TPS * b:TPS * b + TPS, :],
                                 x[:, TPS * b:TPS * b + TPS, :]).then_inc(stored, 16)
                sp.wait_ge(stored, 16 * SEQS)

        @block.gpsimd
        def _(pool):
            pool.sem_inc(w_split, CPG)
            with pool.Fori(0, CHUNK_GROUPS) as g:
                for c in range(CPG):
                    pool.wait_ge(w_hi_done, CPG * g + c + 1)
                    pool.tensor_tensor(up_lo[:, c], raw_up[:, c], up_hi[:, c].bitcast(F32), ALU.subtract)
                    pool.tensor_tensor(dn_lo[:, c, :], raw_dn[:, c, :], dn_hi[:, c, :].bitcast(F32),
                                       ALU.subtract).then_inc(w_split, 1)

        @block.tensor
        def _(pe):
            pe.sem_inc(dn_done, UNITS)

            def up(g, k):
                b, c = divmod(k, CPG)
                if b == 0:
                    pe.wait_ge(w_split, CPG + CPG * g + c + 1)
                    pe.wait_ge(sel_loaded[c], 16 * (g + 1))
                pe.wait_ge(gated, UNITS * g + k + 1)
                at = slice(SEQ * b, SEQ * b + SEQ)
                for j, bank in enumerate((g_ps, u_ps)):
                    for kt in range(KT):
                        product(pe, bank[:, k % 2, :], up_hi[:, c, j, kt, :], up_lo[:, c, j, kt, :],
                                tT_hi[:, kt, at], tT_lo[:, kt, at], kt == 0, kt == KT - 1)
                pe.matmul(cw_ps[:, k % 2, :], sel_bf[:, c, :], cwT[:, at], start=True, stop=True).then_inc(up_done, 1)

            def down(g, k):
                b, c = divmod(k, CPG)
                pe.wait_ge(hh_split, UNITS * g + k + 1)
                if c == 0:
                    pe.wait_ge(y_added, 2 * SEQS * g + 2 * b + 2)
                for t in range(TPS):
                    at = slice(P * t, P * t + P)
                    last = product(pe, dn_ps[:, t // 2, D * (t % 2):D * (t % 2) + D], hh_hi[:, k % 2, at],
                                   hh_lo[:, k % 2, at], dn_hi[:, c, :], dn_lo[:, c, :],
                                   c == 0 and t % 2 == 0, c == CPG - 1, shared_bank=True)
                last.then_inc(dn_done, 1)

            with pe.Fori(0, CHUNK_GROUPS) as g:
                up(g, 0)
                for k in range(UNITS):
                    if k + 1 < UNITS:
                        up(g, k + 1)
                    down(g, k)

        @block.scalar
        def _(act):
            def weights_hi(g, c):
                act.wait_ge(raw_loaded[c], 48 * (g + 1))
                act.wait_ge(dn_done, UNITS * g + CPG * (SEQS - 1) + c + 1)
                act.activation(up_hi[:, c], raw_up[:, c], ACT.Copy)
                act.activation(dn_hi[:, c, :], raw_dn[:, c, :], ACT.Copy).then_inc(w_hi_done, 1)

            with act.Fori(0, CHUNK_GROUPS) as g:
                weights_hi(g, 0)
                for k in range(UNITS):
                    if k + 1 < CPG:
                        weights_hi(g, k + 1)
                    act.wait_ge(up_done, UNITS * g + k + 1)
                    act.activation(silu[:, k % 2, :], g_ps[:, k % 2, :], ACT.Silu).then_inc(silu_done, 1)
                    act.wait_ge(gated, 2 + UNITS * g + k + 1)
                    act.activation(hh_hi[:, k % 2, :], hh[:, k % 2, :], ACT.Copy).then_inc(hh_hi_done, 1)

        @block.vector
        def _(dve):
            dve.sem_inc(gated, 2)
            dve.sem_inc(y_added, 2)

            def add_down(g, b, m):
                t = TPS * b + 2 * m
                dve.tensor_tensor(y[:, t:t + 2, :], dn_ps[:, m, :].rearrange("p (t d) -> p t d", d=D),
                                  y[:, t:t + 2, :], ALU.add).then_inc(y_added, 1)

            with dve.Fori(0, CHUNK_GROUPS) as g:
                for k in range(UNITS + 1):
                    if k < UNITS:
                        dve.wait_ge(silu_done, UNITS * g + k + 1)
                        dve.tensor_tensor(prod[:, k % 2, :], u_ps[:, k % 2, :], silu[:, k % 2, :],
                                          ALU.mult).then_inc(prod_done, 1)
                        dve.wait_ge(prod_done, UNITS * g + k + 1)
                        dve.tensor_tensor(hh[:, k % 2, :], cw_ps[:, k % 2, :], prod[:, k % 2, :],
                                          ALU.mult).then_inc(gated, 1)
                        dve.wait_ge(hh_hi_done, UNITS * g + k + 1)
                        dve.tensor_tensor(hh_lo[:, k % 2, :], hh[:, k % 2, :], hh_hi[:, k % 2, :].bitcast(F32),
                                          ALU.subtract).then_inc(hh_split, 1)
                    if k % CPG == 0 and k:
                        dve.wait_ge(dn_done, UNITS + UNITS * g + k)
                        for m in range(2):
                            add_down(g, k // CPG - 1, m)
            dve.wait_ge(y_added, 2 + 2 * SEQS * CHUNK_GROUPS)
            for b in range(SEQS):
                at = slice(TPS * b, TPS * b + TPS)
                dve.scalar_tensor_tensor(out=x[:, at, :], in0=y[:, at, :], scalar=0.5, in1=x[:, at, :],
                                         op0=ALU.mult, op1=ALU.add).then_inc(x_added, 1)


def macaron_kernel(nc, x_in, Wq, Wk, Wv, phi_scale_in, phi_bias_in, Wo, bo_in, ln1_in, ln2_in, wq, wk, wv, wo,
                   gate_w, eg_w, eu_w, ed_w, ident_in, ident_bf_in, causal_in, local_in, block_mask_in, sel_in, out):
    with ExitStack() as ctx:
        def sb(name, shape, dt=F32):
            return ctx.enter_context(nc.sbuf_tensor(name, shape, dt))

        ident = sb("ident", [P, P])
        ident_bf = sb("ident_bf", [P, P], BF16)
        causal_bf = sb("causal_bf", [P, P], BF16)
        ln_w = sb("ln_w", [P, 2, KT])
        x = sb("x", [P, TILES, D])
        hT_hi, hT_lo = (sb(f"hT_{s}", [P, KT, TOKENS], F32R) for s in ("hi", "lo"))

        def by_k(w):
            return w.rearrange("(k p) n -> p k n", p=P)

        def by_token(a):
            return a.rearrange("(t p) d -> p t d", p=P)

        attn_w = (by_k(Wq), by_k(Wk), by_k(Wv), by_k(Wo))
        ffn_w = (by_k(wq), by_k(wk), by_k(wv), by_k(wo))
        up_w = ((by_k(eg_w), by_k(eu_w)), ed_w)
        first_loads = [(x[:, :, :], by_token(x_in)), (ident[:, :], ident_in), (ident_bf[:, :], ident_bf_in),
                       (causal_bf[:, :], causal_in), (ln_w[:, 0, :], ln1_in), (ln_w[:, 1, :], ln2_in)]

        def ffn(tag, loads, out_dram):
            with ExitStack() as inner:
                def sbi(name, shape, dt=F32):
                    return inner.enter_context(nc.sbuf_tensor(f"{tag}_{name}", shape, dt))

                y = sbi("y", [P, TILES, D])
                norm_phase(nc, f"{tag}n1", x, y, True, ln_w[:, 0, :], hT_hi, hT_lo, ident, loads=loads)
                attention_phase(nc, f"{tag}at", False, hT_hi, hT_lo, y, ffn_w,
                                (ident, ident_bf, causal_bf, None, None, None, None))
                cwT = sbi("cwT", [CW_ROWS, TOKENS], BF16)
                norm_phase(nc, f"{tag}n2", y, None, True, ln_w[:, 1, :], hT_hi, hT_lo, ident)
                routing_phase(nc, f"{tag}rt", hT_hi, hT_lo, by_k(gate_w), ident_bf, cwT)
                experts_phase(nc, f"{tag}ex", hT_hi, hT_lo, cwT, sel_in, up_w, y, x, out_dram)

        ffn("f1", first_loads, None)
        with ExitStack() as inner:
            def sbi(name, shape, dt=F32):
                return inner.enter_context(nc.sbuf_tensor(name, shape, dt))

            local_bf = sbi("local_bf", [P, SEQ], BF16)
            block_mask = sbi("block_mask", [P, SEQ])
            bo = sbi("bo", [P, D])
            norm_phase(nc, "an", x, x, False, None, hT_hi, hT_lo, ident, add_row=bo[:, :],
                       loads=[(local_bf[:, :], local_in), (block_mask[:, :], block_mask_in),
                              (bo[:, :], bo_in)])
            attention_phase(nc, "aa", True, hT_hi, hT_lo, x, attn_w,
                            (ident, ident_bf, None, local_bf, block_mask, phi_scale_in, phi_bias_in))
        ffn("f2", None, by_token(out))


def kernel(**inputs):
    import ml_dtypes
    import numpy as np
    import concourse.bacc as bacc
    from concourse.bass_utils import run_bass_kernel_spmd

    def arr(name):
        return np.asarray(inputs[name])

    def experts_side_by_side(routed, shared):
        flat = np.concatenate([routed.reshape(EXPERTS * INNER, D), shared], axis=0)
        return np.concatenate([flat, np.zeros((CHUNKS * P - flat.shape[0], D), flat.dtype)], axis=0)

    bf = ml_dtypes.bfloat16
    below = np.tril(np.ones((P, P), bool))
    hidden = -1e9 / SCALE
    causal = np.where(below, 0.0, hidden).astype(bf)
    same = np.kron(np.eye(P // 64), np.ones((64, 64))).astype(bool)
    local = np.tile(np.where(same, 0.0, hidden), (1, TPS)).astype(bf)
    block_mask = np.ones((P, SEQ), np.float32)
    block_mask[:64, SEQ - 64:] = 0.0
    sel = np.zeros((CW_ROWS, CHUNKS * P), np.float32)
    for c in range(EXPERTS * INNER + SHARED):
        for part in range(3):
            sel[part * (EXPERTS + 1) + min(c // INNER, EXPERTS), c] = 1.0

    arrays = {
        "x_in": arr("L0_attn_x").reshape(TOKENS, D),
        "Wq": arr("L0_attn_Wq"), "Wk": arr("L0_attn_Wk"), "Wv": arr("L0_attn_Wv"),
        "phi_scale_in": np.ascontiguousarray(arr("L0_attn_phi_scale").reshape(HEADS, HD).T),
        "phi_bias_in": np.ascontiguousarray(arr("L0_attn_phi_bias").reshape(HEADS, HD).T),
        "Wo": arr("L0_attn_Wo"),
        "bo_in": np.ascontiguousarray(np.broadcast_to(arr("L0_attn_bo"), (P, D))),
        "ln1_in": np.ascontiguousarray(arr("L0_ffn_ln1_w").reshape(KT, P).T),
        "ln2_in": np.ascontiguousarray(arr("L0_ffn_ln2_w").reshape(KT, P).T),
        "wq": arr("L0_ffn_wq"), "wk": arr("L0_ffn_wk"), "wv": arr("L0_ffn_wv"), "wo": arr("L0_ffn_wo"),
        "gate_w": np.ascontiguousarray(arr("L0_ffn_gate_w").T),
        "eg_w": np.ascontiguousarray(experts_side_by_side(arr("L0_ffn_eg_w"), arr("L0_ffn_sg_w")).T),
        "eu_w": np.ascontiguousarray(experts_side_by_side(arr("L0_ffn_eu_w"), arr("L0_ffn_su_w")).T),
        "ed_w": experts_side_by_side(arr("L0_ffn_ed_w").transpose(0, 2, 1), arr("L0_ffn_sd_w").T),
        "ident_in": np.eye(P, dtype=np.float32), "ident_bf_in": np.eye(P).astype(bf),
        "causal_in": causal, "local_in": local, "block_mask_in": block_mask, "sel_in": sel.astype(bf),
    }
    nc = bacc.Bacc("TRN2", target_bir_lowering=False, num_devices=1)
    args = [nc.dram_tensor(name, a.shape, mybir.dt.from_np(a.dtype), kind="ExternalInput").ap()
            for name, a in arrays.items()]
    args.append(nc.dram_tensor("out", (TOKENS, D), F32, kind="ExternalOutput").ap())
    macaron_kernel(nc, *args)
    r = run_bass_kernel_spmd(nc, [{k: np.ascontiguousarray(a) for k, a in arrays.items()}], core_ids=[0])
    return r.results[0]["out"].reshape(SEQS, SEQ, D)
```

```python
from contextlib import ExitStack, contextmanager

import concourse.bass as bass
from concourse import mybir

F32 = mybir.dt.float32
F32R = mybir.dt.float32r
BF16 = mybir.dt.bfloat16
ALU = mybir.AluOpType
ACT = mybir.ActivationFunctionType
AX = mybir.AxisListType

P = 128
SEQS, SEQ, D = 4, 512, 256
TOKENS = SEQS * SEQ
TILES = TOKENS // P
TPS = SEQ // P
KT = D // P
HEADS, HD = 16, 128
GROUP = 4
GROUPS = HEADS // GROUP
GW = GROUP * HD
STEPS = SEQS * GROUP
EXPERTS, TOPK, INNER, SHARED = 16, 6, 176, 352
CHUNKS = -(-(EXPERTS * INNER + SHARED) // P)
CPG = 5
CHUNK_GROUPS = CHUNKS // CPG
UNITS = SEQS * CPG
CW_ROWS = 3 * (EXPERTS + 1)
LN_EPS, RMS_EPS, DEN_EPS = 1e-5, 1e-6, 1e-6
SCALE = float(HD) ** -0.5
WIDTH = [P * (i + 1) for i in range(TPS)]
E_AT = [sum(WIDTH[:i]) for i in range(TPS)]
E_ALL = sum(WIDTH)
DOWN = list(range(TPS - 1, -1, -1))


@contextmanager
def phase_semaphores(nc):
    held = []

    def new_sem(name):
        held.append(nc.alloc_semaphore(name=name))
        return held[-1]

    yield new_sem
    nc.clear_and_free_semaphores(held)
    nc.all_engine_barrier()


def product(pe, out, a_hi, a_lo, b_hi, b_lo, first, last, shared_bank=False):
    pe.matmul(out, a_hi, b_hi, start=first, stop=False, skip_group_check=shared_bank)
    pe.matmul(out, a_hi, b_lo, start=False, stop=False, skip_group_check=shared_bank)
    return pe.matmul(out, a_lo, b_hi, start=False, stop=last, skip_group_check=shared_bank)


def fetch_weights(sp, pieces, fetched):
    for (loads, _), done in zip(pieces, fetched):
        for dst, src_dram in loads:
            sp.dma_start(dst, src_dram).then_inc(done, 16)
    for (loads, _), done in zip(pieces, fetched):
        sp.wait_ge(done, 16 * len(loads))


def split_weights(pool, pieces, fetched, hi_done):
    n = 0
    for (loads, views), done in zip(pieces, fetched):
        pool.wait_ge(done, 16 * len(loads))
        for raw, hi, lo in views:
            pool.tensor_copy(hi, raw).then_inc(hi_done, 1)
            n += 1
            pool.wait_ge(hi_done, n)
            pool.tensor_tensor(lo, raw, hi.bitcast(F32), ALU.subtract)


def norm_phase(nc, tag, src, ln_out, weight, hT_hi, hT_lo, ident, pieces, x_loads=None, loads=None):
    with ExitStack() as ctx:
        new_sem = ctx.enter_context(phase_semaphores(nc))

        def sb(name, shape, dt=F32):
            return ctx.enter_context(nc.sbuf_tensor(f"{tag}_{name}", shape, dt))

        def sem(name):
            return new_sem(f"{tag}_{name}")

        z = sb("z", [P, TILES, D])
        stats = sb("stats", [P, TILES, 6])
        mv = sb("mv", [P, TILES, 2])
        var, std, rstd, ms, rms_std, rrms, squares = (
            sb(name, [P, TILES]) for name in ("var", "std", "rstd", "ms", "rms_std", "rrms", "squares"))
        BANKS = 4
        tp = ctx.enter_context(nc.psum_tensor(f"{tag}_tp", [P, BANKS, 512], F32))

        x_loaded = [sem(f"x_loaded_{b}") for b in range(SEQS if x_loads else 0)]
        loaded = sem("loaded")
        stats_done = sem("stats_done")
        aggr_done = sem("aggr_done")
        var_ready = sem("var_ready")
        std_ready = sem("std_ready")
        rstd_ready = sem("rstd_ready")
        normed = sem("normed")
        squared = sem("squared")
        ms_ready = sem("ms_ready")
        rms_std_ready = sem("rms_std_ready")
        rrms_ready = sem("rrms_ready")
        z_ready = sem("z_ready")
        turned = sem("turned")
        hi_done = sem("hi_done")
        split_done = sem("split_done")
        fetched = [sem(f"fetched_{i}") for i in range(len(pieces))]
        w_hi_done = sem("w_hi_done")
        block = ctx.enter_context(nc.Block())

        rms = ln_out is not None
        ln_dst = ln_out if rms else z
        n_loads = len(loads or [])

        def tiles(b):
            return range(TPS * b, TPS * b + TPS)

        def cols(b):
            return slice(TPS * b, TPS * b + TPS)

        @block.sync
        def _(sp):
            for b, done in enumerate(x_loaded):
                sp.dma_start(*x_loads[b]).then_inc(done, 16)
            for dst, src_dram in loads or []:
                sp.dma_start(dst, src_dram).then_inc(loaded, 16)
            fetch_weights(sp, pieces, fetched)
            if n_loads:
                sp.wait_ge(loaded, 16 * n_loads)

        @block.gpsimd
        def _(pool):
            split_weights(pool, pieces, fetched, w_hi_done)

        @block.vector
        def _(dve):
            def variance(b):
                if x_loads:
                    dve.wait_ge(x_loaded[b], 16)
                for t in tiles(b):
                    dve.bn_stats(stats[:, t, :], src[:, t, :]).then_inc(stats_done, 1)
                for t in tiles(b):
                    dve.wait_ge(stats_done, t + 1)
                    dve.bn_aggr(mv[:, t, :], stats[:, t, :]).then_inc(aggr_done, 1)
                dve.wait_ge(aggr_done, TPS * (b + 1))
                dve.tensor_scalar(var[:, cols(b)], mv[:, cols(b), 1], LN_EPS, None, ALU.add).then_inc(var_ready, 1)

            def layer_norm(b):
                dve.wait_ge(std_ready, b + 1)
                dve.reciprocal(rstd[:, cols(b)], std[:, cols(b)]).then_inc(rstd_ready, 1)
                dve.wait_ge(rstd_ready, b + 1)
                for t in tiles(b):
                    dve.tensor_scalar(ln_dst[:, t, :], src[:, t, :], mv[:, t, 0:1], rstd[:, t:t + 1],
                                      ALU.subtract, ALU.mult).then_inc(normed, 1)

            def mean_square(b):
                dve.wait_ge(squared, TPS * (b + 1))
                dve.tensor_scalar(ms[:, cols(b)], squares[:, cols(b)], 1.0 / D, RMS_EPS,
                                  ALU.mult, ALU.add).then_inc(ms_ready, 1)

            def rms_norm(b):
                dve.wait_ge(rms_std_ready, b + 1)
                dve.reciprocal(rrms[:, cols(b)], rms_std[:, cols(b)]).then_inc(rrms_ready, 1)
                dve.wait_ge(rrms_ready, b + 1)
                for t in tiles(b):
                    last = dve.tensor_scalar(z[:, t, :], ln_out[:, t, :], rrms[:, t:t + 1], None, ALU.mult)
                last.then_inc(z_ready, 1)

            def low(b):
                if b == 0 and n_loads:
                    dve.wait_ge(loaded, 16 * n_loads)
                for k in range(KT):
                    n = KT * b + k
                    dve.wait_ge(hi_done, n + 1)
                    bank = tp[:, n % BANKS, :]
                    at = slice(SEQ * b, SEQ * b + SEQ)
                    if weight is None:
                        dve.tensor_tensor(hT_lo[:, k, at], bank, hT_hi[:, k, at].bitcast(F32),
                                          ALU.subtract).then_inc(split_done, 1)
                    else:
                        dve.scalar_tensor_tensor(out=hT_lo[:, k, at], in0=bank, scalar=weight[:, k:k + 1],
                                                 in1=hT_hi[:, k, at].bitcast(F32), op0=ALU.mult,
                                                 op1=ALU.subtract).then_inc(split_done, 1)

            dve.sem_inc(split_done, BANKS)
            variance(0)
            variance(1)
            layer_norm(0)
            variance(2)
            layer_norm(1)
            if rms:
                mean_square(0)
                rms_norm(0)
            variance(3)
            for b in range(2, SEQS + 2):
                if b < SEQS:
                    layer_norm(b)
                if rms and b - 1 < SEQS:
                    mean_square(b - 1)
                    rms_norm(b - 1)
                low(b - 2)

        @block.scalar
        def _(act):
            def deviation(b):
                act.wait_ge(var_ready, b + 1)
                act.activation(std[:, cols(b)], var[:, cols(b)], ACT.Sqrt).then_inc(std_ready, 1)

            def square(b):
                for t in tiles(b):
                    act.wait_ge(normed, t + 1)
                    act.activation(z[:, t, :], ln_out[:, t, :], ACT.Square,
                                   accum_out=squares[:, t:t + 1]).then_inc(squared, 1)

            def root_mean_square(b):
                act.wait_ge(ms_ready, b + 1)
                act.activation(rms_std[:, cols(b)], ms[:, cols(b)], ACT.Sqrt).then_inc(rms_std_ready, 1)

            def high(b):
                if b == 0 and n_loads:
                    act.wait_ge(loaded, 16 * n_loads)
                for k in range(KT):
                    n = KT * b + k
                    act.wait_ge(turned, n + 1)
                    act.activation(hT_hi[:, k, SEQ * b:SEQ * b + SEQ], tp[:, n % BANKS, :], ACT.Copy,
                                   scale=1.0 if weight is None else weight[:, k:k + 1]).then_inc(hi_done, 1)

            deviation(0)
            deviation(1)
            if rms:
                square(0)
            deviation(2)
            if rms:
                root_mean_square(0)
                square(1)
            deviation(3)
            for b in range(2, SEQS + 2):
                if rms and b - 1 < SEQS:
                    root_mean_square(b - 1)
                if rms and b < SEQS:
                    square(b)
                high(b - 2)

        @block.tensor
        def _(pe):
            if n_loads:
                pe.wait_ge(loaded, 16 * n_loads)
            for b in range(SEQS):
                if rms:
                    pe.wait_ge(z_ready, b + 1)
                else:
                    pe.wait_ge(normed, TPS * b + TPS)
                for k in range(KT):
                    n = KT * b + k
                    pe.wait_ge(split_done, n + 1)
                    for i in range(TPS):
                        last = pe.transpose(tp[:, n % BANKS, P * i:P * i + P],
                                            z[:, TPS * b + i, P * k:P * k + P], ident[:, :])
                    last.then_inc(turned, 1)


def q_at(n):
    return 3 * n + 2


def k_at(n):
    return 3 * n + 3


def v_at(step):
    return 3 * step + 7


def v_unit(step):
    return (step - 1) // GROUP + 1, (step - 1) % GROUP


NO_V = STEPS - 3
FIRST_UNITS = [("v", 0, 0), ("v", 0, 1), ("q", 0), ("k", 0), ("v", 0, 2)]
PIECES = ["v", "qk0", "qk1", "qk2", "qk3", "o"]
NP = len(PIECES)
SPLIT_STEP = {12: "v", 13: "qk0", 14: "qk1", 15: "qk2", 16: "qk3", 2: "o"}
PROJ_BANKS, S_BANKS, T_BANKS = 2, 2, 3
S_UNITS = [[3], [2], [1, 0]]
SU = len(S_UNITS)
LINEAR_BANK, LOCAL_BANK = [0, 1, 0], 1
T_UNITS = [[0], [1], [2, 3]]
TU = len(T_UNITS)
PT_AT = [sum(SEQ - P * i for i in range(j)) for j in range(TPS)]
LOADS = [("v", NP), ("qk0", 4), ("qk1", 5), ("o", NP + 1), ("qk2", NP + 2), ("qk3", NP + 3)]


def turned_columns(tiles):
    w = sum(SEQ - P * j for j in tiles)
    return slice(PT_AT[tiles[0]], PT_AT[tiles[0]] + w), w


FIRST_PIECES = 3


def attention_weights(ctx, nc, tag, w_dram, phi_dram):
    wq_dram, wk_dram, wv_dram, wo_dram = w_dram

    def sb(name, shape, dt=F32):
        return ctx.enter_context(nc.sbuf_tensor(f"{tag}_{name}", shape, dt))

    raw_qk = sb("raw_qk", [P, 2, 2, KT, HD])
    raw_vo = sb("raw_vo", [P, KT * GW])
    raw_v = raw_vo[:, :].rearrange("p (k n) -> p k n", k=KT)
    raw_o = raw_vo[:, :].rearrange("p (h d) -> p h d", h=GROUP)
    wqk_hi, wqk_lo = (sb(f"wqk_{s}", [P, 2, KT, GW], F32R) for s in ("hi", "lo"))
    wv_hi, wv_lo = (sb(f"wv_{s}", [P, KT, GW], F32R) for s in ("hi", "lo"))
    wo_hi, wo_lo = (sb(f"wo_{s}", [P, GROUP, D], F32R) for s in ("hi", "lo"))
    phi_sc = sb("phi_sc", [P, GROUP, 2]) if phi_dram is not None else None

    def loads(g, piece):
        if piece == "v":
            return [(raw_v, wv_dram[:, :, bass.ds(g * GW, GW)])]
        if piece == "o":
            return [(raw_o, wo_dram[:, bass.ds(g * GROUP, GROUP), :])]
        h = int(piece[2])
        return [(raw_qk[:, h % 2, j, :, :], w[:, :, bass.ds(g * GW + HD * h, HD)])
                for j, w in enumerate((wq_dram, wk_dram))]

    def phi_load(g, h):
        return phi_sc[:, h, :], phi_dram[:, bass.ds(g * (2 * GROUP) + 2 * h, 2)]

    def views(piece):
        if piece == "v":
            return [(raw_v, wv_hi[:, :, :], wv_lo[:, :, :])]
        if piece == "o":
            return [(raw_o, wo_hi[:, :, :], wo_lo[:, :, :])]
        h = int(piece[2])
        at = slice(HD * h, HD * h + HD)
        return [(raw_qk[:, h % 2, j, :, :], wqk_hi[:, j, :, at], wqk_lo[:, j, :, at]) for j in range(2)]

    def first_pieces():
        out = []
        for piece in PIECES[:FIRST_PIECES]:
            phi = [phi_load(0, int(piece[2]))] if phi_sc is not None and piece != "v" else []
            out.append((phi + loads(0, piece), views(piece)))
        return out

    return (wqk_hi, wqk_lo, wv_hi, wv_lo, wo_hi, wo_lo, phi_sc), (loads, phi_load, views), first_pieces()


def attention_phase(nc, tag, linear, hT_hi, hT_lo, acc, weights, consts):
    ident, ident_bf, causal_bf, local_bf, block_mask, bo = consts
    (wqk_hi, wqk_lo, wv_hi, wv_lo, wo_hi, wo_lo, phi_sc), (w_loads, phi_load, w_views) = weights
    with ExitStack() as ctx:
        new_sem = ctx.enter_context(phase_semaphores(nc))

        def sb(name, shape, dt=F32):
            return ctx.enter_context(nc.sbuf_tensor(f"{tag}_{name}", shape, dt))

        def ps(name, banks):
            return ctx.enter_context(nc.psum_tensor(f"{tag}_{name}", [P, banks, 512], F32))

        def sem(name):
            return new_sem(f"{tag}_{name}")

        qk_hi, qk_lo = (sb(f"qk_{s}", [P, 2, 2, SEQ], F32R) for s in ("hi", "lo"))
        v_hi, v_lo = (sb(f"v_{s}", [P, 2, TPS, GW], F32R) for s in ("hi", "lo"))
        e = sb("e", [P, 2, E_ALL])
        pt_hi, pt_lo = (sb(f"pt_{s}", [P, E_ALL], F32R) for s in ("hi", "lo"))
        ao_hi, ao_lo = (sb(f"ao_{s}", [P, GROUP, SEQ], F32R) for s in ("hi", "lo"))
        nmax = sb("nmax", [P, 2, TPS])
        den = sb("den", [P, 2, 2, TPS])
        rden = sb("rden", [P, 2, 2, TPS])
        if linear:
            loc = sb("loc", [P, 2, TPS, P])
            phi_hi, phi_lo = (sb(f"phi_{s}", [P, 2, 2, SEQ], F32R) for s in ("hi", "lo"))
            exp_z = sb("exp_z", [P, 2, SEQ])
            relu_z = sb("relu_z", [P, 2, SEQ])

        proj_ps = ps("proj_ps", PROJ_BANKS)
        s_ps = ps("s_ps", S_BANKS)
        t_ps = ps("t_ps", T_BANKS)
        pv_ps = ps("pv_ps", 1)

        raw_loaded = [sem(f"raw_{p}") for p in PIECES]
        w_hi_done = sem("w_hi_done")
        w_split = sem("w_split")
        proj_done = sem("proj_done")
        proj_hi = sem("proj_hi")
        proj_split = sem("proj_split")
        s_done = sem("s_done")
        max_done = sem("max_done")
        exp_done = sem("exp_done")
        rden_done = sem("rden_done")
        normed = sem("normed")
        t_done = sem("t_done")
        t_hi = sem("t_hi")
        t_split = sem("t_split")
        pv_done = sem("pv_done")
        ao_hi_done = sem("ao_hi_done")
        ao_split = sem("ao_split")
        o_done = sem("o_done")
        o_added = sem("o_added")
        dve_step = sem("dve_step")
        if linear:
            local_done = sem("local_done")
            rlocal_done = sem("rlocal_done")
            a_read = sem("a_read")
            z_read = sem("z_read")
            phi_q_hi, phi_q_done, phi_k_done = sem("phi_q_hi"), sem("phi_q_done"), sem("phi_k_done")
            phi_step = sem("phi_step")
            pool_step = sem("pool_step")
            bias_added = sem("bias_added")
        block = ctx.enter_context(nc.Block())

        def loads_of(piece):
            return 1 if piece in "vo" else 2 + linear

        @block.sync
        def _(sp):
            def load(g, piece, count):
                done = raw_loaded[PIECES.index(piece)]
                if linear and piece.startswith("qk"):
                    h = int(piece[2])
                    sp.wait_ge(z_read, 2 * STEPS * g + 2 * (h + 1))
                    sp.dma_start(*phi_load(g, h)).then_inc(done, 16)
                sp.wait_ge(w_split, NP * g + count)
                for dst, src_dram in w_loads(g, piece):
                    sp.dma_start(dst, src_dram).then_inc(done, 16)

            for p, piece in enumerate(PIECES[:FIRST_PIECES]):
                sp.sem_inc(raw_loaded[p], 16 * loads_of(piece))
            for piece, count in LOADS:
                if PIECES.index(piece) >= FIRST_PIECES:
                    load(0, piece, count)
            with sp.Fori(1, GROUPS) as g:
                for piece, count in LOADS:
                    load(g, piece, count)

        def split_piece(split, g, n, last):
            piece = SPLIT_STEP.get(n)
            if piece == "o":
                split(g, PIECES.index(piece))
            elif piece is not None and not last:
                split(g + 1, PIECES.index(piece))

        def run_steps(engine, step):
            with engine.Fori(0, GROUPS - 1) as g:
                for n in range(2, 2 + STEPS):
                    step(g, n)
            for n in range(2, 2 + STEPS):
                step(GROUPS - 1, n, last=True)

        @block.gpsimd
        def _(pool):
            pool.sem_inc(w_split, NP + FIRST_PIECES)

            if linear:
                pool.sem_inc(phi_q_done, 1)

            def add_bias(b):
                if linear:
                    at = slice(TPS * b, TPS * b + TPS)
                    pool.tensor_tensor(acc[:, at, :], acc[:, at, :], bo[:, :].unsqueeze(1).to_broadcast([P, TPS, D]),
                                       ALU.add).then_inc(bias_added, 1)

            def weights_lo(g, p):
                pool.wait_ge(w_hi_done, NP * g + p + 1)
                for raw, hi, lo in w_views(PIECES[p]):
                    last = pool.tensor_tensor(lo, raw, hi.bitcast(F32), ALU.subtract)
                last.then_inc(w_split, 1)

            def normalise(g, n):
                pool.wait_ge(rden_done, STEPS * g + n + 1)
                for i in DOWN:
                    w = e[:, n % 2, E_AT[i]:E_AT[i] + WIDTH[i]]
                    last = pool.tensor_tensor(w, w, rden[:, n % 2, int(linear), i:i + 1].to_broadcast([P, WIDTH[i]]),
                                              ALU.mult)
                    if linear:
                        last.then_inc(pool_step, 1)
                if not linear:
                    last.then_inc(normed, 1)

            def add_local(g, n):
                pool.wait_ge(rlocal_done, STEPS * g + n + 1)
                pool.tensor_tensor(loc[:, n % 2, :, :], loc[:, n % 2, :, :],
                                   rden[:, n % 2, 0, :].unsqueeze(2).to_broadcast([P, TPS, P]),
                                   ALU.mult).then_inc(pool_step, 1)
                pool.wait_ge(pool_step, (1 + TPS) * (STEPS * g + n + 1))
                for i in DOWN:
                    w = e[:, n % 2, E_AT[i] + P * i:E_AT[i] + P * i + P]
                    last = pool.tensor_tensor(w, w, loc[:, n % 2, i, :], ALU.add)
                last.then_inc(normed, 1)

            def q_features_lo(g, n):
                pool.wait_ge(phi_q_hi, STEPS * g + n + 1)
                pool.tensor_tensor(phi_lo[:, 0, n % 2, :], relu_z[:, 0, :], phi_hi[:, 0, n % 2, :].bitcast(F32),
                                   ALU.subtract).then_inc(phi_q_done, 1)

            def step(g, n, last=False):
                if not last or n < STEPS:
                    normalise(g, n)
                if linear and (not last or n + 1 < STEPS):
                    q_features_lo(g, n + 1)
                if linear and (not last or n < STEPS):
                    add_local(g, n)
                split_piece(weights_lo, g, n, last)

            for b in range(SEQS):
                add_bias(b)
            if linear:
                q_features_lo(0, 0)
            weights_lo(0, 3)
            step(0, 0)
            weights_lo(0, 4)
            step(0, 1)
            run_steps(pool, step)

        @block.tensor
        def _(pe):
            pe.sem_inc(o_done, 1)

            def free_bank(g, pos):
                pe.wait_ge(proj_split, 3 * STEPS * g + pos + 1)
                return proj_ps[:, pos % PROJ_BANKS, :]

            def project_v(g, b, t, pos):
                out = free_bank(g, pos)
                if linear and pos > 3:
                    pe.wait_ge(z_read, 2 * GROUP + 2 * STEPS * g + 2 * ((pos - 4) // 3) + 1)
                if b % SEQS == 0 and t == 0:
                    pe.wait_ge(w_split, NP + NP * (g + b // SEQS) + PIECES.index("v") + 1)
                at = slice(SEQ * (b % SEQS) + P * t, SEQ * (b % SEQS) + P * t + P)
                for k in range(KT):
                    last = product(pe, out, hT_hi[:, k, at], hT_lo[:, k, at], wv_hi[:, k, :], wv_lo[:, k, :],
                                   k == 0, k == KT - 1)
                last.then_inc(proj_done, 1)

            def project_qk(g, j, n):
                (b, h), pos = divmod(n, GROUP), (q_at, k_at)[j](n)
                out = free_bank(g, pos)
                if linear and j == 0:
                    pe.wait_ge(z_read, 2 * GROUP + 2 * STEPS * g + 2 * n)
                if h == GROUP - 1:
                    pe.wait_ge(o_added, 2 + 2 * (SEQS * g + b - 1) + j + 1)
                if b % SEQS == 0:
                    pe.wait_ge(w_split, NP + NP * (g + b // SEQS) + PIECES.index(f"qk{h}") + 1)
                cols, at = slice(HD * h, HD * h + HD), slice(SEQ * (b % SEQS), SEQ * (b % SEQS) + SEQ)
                for k in range(KT):
                    last = product(pe, out, wqk_hi[:, j, k, cols], wqk_lo[:, j, k, cols],
                                   hT_hi[:, k, at], hT_lo[:, k, at], k == 0, k == KT - 1)
                last.then_inc(proj_done, 1)

            def scores(g, n, unit):
                buf = n % 2
                bank = s_ps[:, (LINEAR_BANK[unit] if linear else unit + SU * n) % S_BANKS, :]
                if not linear:
                    pe.wait_ge(exp_done, SU * (STEPS * g + n) + unit + 1)
                elif unit == 1:
                    pe.wait_ge(exp_done, STEPS * g + n + 1)
                else:
                    pe.wait_ge(a_read, SU * (STEPS * g + n) + SU + (0, None, 1)[unit])
                a_hi, a_lo = (phi_hi, phi_lo) if linear else (qk_hi, qk_lo)
                if linear:
                    pe.wait_ge(phi_q_done, 1 + STEPS * g + n + 1)
                    pe.wait_ge(phi_k_done, 1 + STEPS * g + n + 1)
                else:
                    pe.wait_ge(proj_split, PROJ_BANKS + 3 * STEPS * g + k_at(n) + 1)
                start = 0
                for i in S_UNITS[unit]:
                    at, out = slice(P * i, P * i + P), bank[:, start:start + WIDTH[i]]
                    last = product(pe, out, a_hi[:, 0, buf, at], a_lo[:, 0, buf, at], a_hi[:, 1, buf, 0:WIDTH[i]],
                                   a_lo[:, 1, buf, 0:WIDTH[i]], start == 0, linear, shared_bank=True)
                    start += WIDTH[i]
                if not linear:
                    diagonal = slice(WIDTH[S_UNITS[unit][0]] - P, start)
                    last = pe.matmul(bank[:, diagonal], ident_bf[:, :], causal_bf[:, 0:diagonal.stop - diagonal.start],
                                     start=False, stop=True, skip_group_check=True)
                last.then_inc(s_done, 1)

            def local_scores(g, n):
                buf = n % 2
                out = s_ps[:, LOCAL_BANK, :]
                pe.wait_ge(a_read, SU * (STEPS * g + n) + SU + 2)
                pe.wait_ge(proj_split, PROJ_BANKS + 3 * STEPS * g + k_at(n) + 1)
                pe.matmul(out, ident_bf[:, :], local_bf[:, :], start=True, stop=False)
                for i in range(TPS):
                    at = slice(P * i, P * i + P)
                    last = product(pe, out[:, at], qk_hi[:, 0, buf, at], qk_lo[:, 0, buf, at],
                                   qk_hi[:, 1, buf, at], qk_lo[:, 1, buf, at], False, i == TPS - 1)
                last.then_inc(local_done, 1)

            def turn(g, n):
                pe.wait_ge(normed, STEPS * g + n + 1)
                for unit, tiles in enumerate(T_UNITS):
                    pe.wait_ge(t_split, TU * (STEPS * g + n) + unit + 1)
                    for j in tiles:
                        for i in range(j, TPS):
                            start = PT_AT[j] - PT_AT[tiles[0]] + P * (i - j)
                            last = pe.transpose(t_ps[:, unit, start:start + P],
                                                e[:, n % 2, E_AT[i] + P * j:E_AT[i] + P * j + P], ident[:, :])
                    last.then_inc(t_done, 1)

            def times_v(g, n):
                b, h = divmod(n, GROUP)
                pe.wait_ge(ao_split, STEPS * g + n + 1)
                pe.wait_ge(proj_split, PROJ_BANKS + 3 * STEPS * g + v_at(GROUP * b) + 1)
                cols = slice(HD * h, HD * h + HD)
                for unit, tiles in enumerate(T_UNITS):
                    pe.wait_ge(t_split, T_BANKS + TU * (STEPS * g + n) + unit + 1)
                    for j in tiles:
                        at = slice(PT_AT[j], PT_AT[j] + SEQ - P * j)
                        last = product(pe, pv_ps[:, 0, P * j:SEQ], v_hi[:, b % 2, j, cols], v_lo[:, b % 2, j, cols],
                                       pt_hi[:, at], pt_lo[:, at], j == 0, j == TPS - 1)
                last.then_inc(pv_done, 1)

            def out_project(g, n, m, last):
                b = n // GROUP - 1
                pos = (k_at(n + 1), v_at(n))[m]
                end = k_at(STEPS - 1) if last and n > STEPS else pos
                pe.wait_ge(proj_split, PROJ_BANKS + 3 * STEPS * g + end + 1)
                if linear and m == 0:
                    pe.wait_ge(z_read, 2 * GROUP + 2 * STEPS * g + (2 * STEPS if last and n > STEPS else 2 * n + 4))
                if b == 0 and m == 0:
                    pe.wait_ge(w_split, NP + NP * g + PIECES.index("o") + 1)
                pe.wait_ge(ao_split, 1 + STEPS * g + GROUP * b + GROUP)
                for half in range(2):
                    at = slice(P * (2 * m + half), P * (2 * m + half) + P)
                    for h in range(GROUP):
                        end = product(pe, proj_ps[:, pos % PROJ_BANKS, D * half:D * half + D], ao_hi[:, h, at],
                                      ao_lo[:, h, at], wo_hi[:, h, :], wo_lo[:, h, :], h == 0, h == GROUP - 1)
                end.then_inc(o_done, 1)

            def step(g, n, last=False):
                scored = not last or n < STEPS
                projects = not last or n + 1 < STEPS
                if linear and projects:
                    project_qk(g, 0, n + 1)
                    project_qk(g, 1, n + 1)
                if scored:
                    scores(g, n, 0)
                if not linear and projects:
                    project_qk(g, 0, n + 1)
                if scored:
                    scores(g, n, 1)
                    scores(g, n, 2)
                if n >= 1 and (not last or n <= STEPS):
                    turn(g, n - 1)
                if scored and linear:
                    local_scores(g, n)
                if projects and not linear:
                    project_qk(g, 1, n + 1)
                b, t = v_unit(n)
                if not last or b < SEQS:
                    project_v(g, b, t, v_at(n))
                elif n == NO_V:
                    pe.wait_ge(proj_done, 3 * STEPS * g + k_at(n + 1) + 1)
                    pe.sem_inc(proj_done, 1)
                if n >= 1 and (not last or n <= STEPS):
                    times_v(g, n - 1)
                if n % GROUP == 1 and n > 1:
                    for m in range(2):
                        out_project(g, n, m, last)

            for pos, unit in enumerate(FIRST_UNITS):
                if unit[0] == "v":
                    project_v(0, unit[1], unit[2], pos)
                else:
                    project_qk(0, "qk".index(unit[0]), 0)
            step(0, 0)
            step(0, 1)
            run_steps(pe, step)

        @block.scalar
        def _(act):
            act.sem_inc(exp_done, 1 if linear else S_BANKS)
            if linear:
                act.sem_inc(z_read, 2 * GROUP)

            def weights_hi(g, p, first=False):
                piece = PIECES[p]
                act.wait_ge(raw_loaded[p], 16 * loads_of(piece) * (g + 1))
                if piece == "o":
                    act.wait_ge(o_done, 1 + 2 * SEQS * g)
                elif not first:
                    last_use = v_at(STEPS - GROUP) if piece == "v" else k_at(STEPS - GROUP + int(piece[2]))
                    act.wait_ge(proj_done, 3 * STEPS * (g - 1) + last_use + 1)
                for raw, hi, _ in w_views(piece):
                    last = act.activation(hi, raw, ACT.Copy)
                last.then_inc(w_hi_done, 1)

            def v_part(g, b, t, pos):
                act.wait_ge(proj_done, 3 * STEPS * g + pos + 1)
                act.activation(v_hi[:, b % 2, t, :], proj_ps[:, pos % PROJ_BANKS, :], ACT.Copy).then_inc(proj_hi, 1)

            def qk_part(g, j, n):
                pos = (q_at, k_at)[j](n)
                act.wait_ge(proj_done, 3 * STEPS * g + pos + 1)
                act.activation(qk_hi[:, j, n % 2, :], proj_ps[:, pos % PROJ_BANKS, :], ACT.Copy,
                               scale=SCALE if j == 0 else 1.0).then_inc(proj_hi, 1)

            def feature_parts(g, j, n):
                pos, h = (q_at, k_at)[j](n), n % GROUP
                act.wait_ge((phi_q_done, phi_k_done)[j], STEPS * g + n + 1)
                act.wait_ge(proj_split, PROJ_BANKS + 3 * STEPS * g + pos + 1)
                bank = proj_ps[:, pos % PROJ_BANKS, :]
                s, c = (phi_sc[:, h, i:i + 1] for i in range(2))
                act.activation(exp_z[:, j, :], bank, ACT.Exp, bias=c, scale=s)
                act.activation(relu_z[:, j, :], bank, ACT.Relu, bias=c, scale=s).then_inc(z_read, 1)

            def q_features_hi(g, n):
                act.wait_ge(phi_step, 4 * (STEPS * g + n) + 2)
                act.activation(phi_hi[:, 0, n % 2, :], relu_z[:, 0, :], ACT.Copy).then_inc(phi_q_hi, 1)

            def exponents(g, n, unit):
                buf, start = n % 2, 0
                act.wait_ge(max_done, SU * (STEPS * g + n) + unit + 1)
                for i in S_UNITS[unit]:
                    last = act.activation(e[:, buf, E_AT[i]:E_AT[i] + WIDTH[i]],
                                          s_ps[:, (SU * n + unit) % S_BANKS, start:start + WIDTH[i]],
                                          ACT.Exp, bias=nmax[:, buf, i:i + 1], accum_out=den[:, buf, 0, i:i + 1])
                    start += WIDTH[i]
                last.then_inc(exp_done, 1)

            def local_exponents(g, n):
                buf = n % 2
                act.wait_ge(max_done, STEPS * g + n + 1)
                for i in range(TPS):
                    last = act.activation(loc[:, buf, i, :], s_ps[:, LOCAL_BANK, P * i:P * i + P],
                                          ACT.Exp, bias=nmax[:, buf, i:i + 1], accum_out=den[:, buf, 0, i:i + 1])
                last.then_inc(exp_done, 1)

            def turned_hi(g, n):
                for unit, tiles in enumerate(T_UNITS):
                    act.wait_ge(t_done, TU * (STEPS * g + n) + unit + 1)
                    at, w = turned_columns(tiles)
                    act.activation(pt_hi[:, at], t_ps[:, unit, 0:w], ACT.Copy).then_inc(t_hi, 1)

            def out_hi(g, n):
                act.wait_ge(pv_done, STEPS * g + n + 1)
                if n % GROUP == 0 and n:
                    act.wait_ge(o_done, 1 + 2 * (SEQS * g + n // GROUP))
                act.activation(ao_hi[:, n % GROUP, :], pv_ps[:, 0, :], ACT.Copy).then_inc(ao_hi_done, 1)

            def step(g, n, last=False):
                scored = not last or n < STEPS
                projects = not last or n + 1 < STEPS
                if SPLIT_STEP.get(n) != "v":
                    split_piece(weights_hi, g, n, last)
                if scored and not linear:
                    exponents(g, n, 0)
                if projects:
                    qk_part(g, 0, n + 1)
                    if linear:
                        qk_part(g, 1, n + 1)
                        feature_parts(g, 0, n + 1)
                        feature_parts(g, 1, n + 1)
                if scored and not linear:
                    for unit in range(1, SU):
                        exponents(g, n, unit)
                if n >= 1 and (not last or n <= STEPS):
                    turned_hi(g, n - 1)
                if projects and linear:
                    q_features_hi(g, n + 1)
                if projects and not linear:
                    qk_part(g, 1, n + 1)
                b, t = v_unit(n)
                if not last or b < SEQS:
                    v_part(g, b, t, v_at(n))
                elif n == NO_V:
                    act.wait_ge(proj_hi, 3 * STEPS * g + k_at(n + 1) + 1)
                    act.sem_inc(proj_hi, 1)
                if SPLIT_STEP.get(n) == "v":
                    split_piece(weights_hi, g, n, last)
                if scored and linear:
                    local_exponents(g, n)
                if n >= 1 and (not last or n <= STEPS):
                    out_hi(g, n - 1)

            act.sem_inc(w_hi_done, FIRST_PIECES)
            for pos, unit in enumerate(FIRST_UNITS):
                if unit[0] == "v":
                    v_part(0, unit[1], unit[2], pos)
                else:
                    qk_part(0, "qk".index(unit[0]), 0)
                if linear and unit == ("k", 0):
                    feature_parts(0, 0, 0)
                    feature_parts(0, 1, 0)
                    q_features_hi(0, 0)
            weights_hi(0, 3, first=True)
            step(0, 0)
            weights_hi(0, 4, first=True)
            step(0, 1)
            run_steps(act, step)

        @block.vector
        def _(dve):
            dve.sem_inc(proj_split, PROJ_BANKS)
            dve.sem_inc(t_split, T_BANKS)
            dve.sem_inc(ao_split, 1)
            dve.sem_inc(o_added, 2)
            if linear:
                dve.sem_inc(a_read, SU)
                dve.sem_inc(phi_k_done, 1)

            def v_part(g, b, t, pos):
                dve.wait_ge(proj_hi, 3 * STEPS * g + pos + 1)
                at = (slice(None), b % 2, t, slice(None))
                dve.tensor_tensor(v_lo[at], proj_ps[:, pos % PROJ_BANKS, :], v_hi[at].bitcast(F32),
                                  ALU.subtract).then_inc(proj_split, 1)

            def qk_part(g, j, n):
                pos, at = (q_at, k_at)[j](n), (slice(None), j, n % 2, slice(None))
                bank = proj_ps[:, pos % PROJ_BANKS, :]
                dve.wait_ge(proj_hi, 3 * STEPS * g + pos + 1)
                if j == 0:
                    dve.scalar_tensor_tensor(out=qk_lo[at], in0=bank, scalar=SCALE, in1=qk_hi[at].bitcast(F32),
                                             op0=ALU.mult, op1=ALU.subtract).then_inc(proj_split, 1)
                else:
                    dve.tensor_tensor(qk_lo[at], bank, qk_hi[at].bitcast(F32), ALU.subtract).then_inc(proj_split, 1)

            def add_out(g, n, m):
                b = n // GROUP - 1
                dve.wait_ge(o_done, 1 + 2 * (SEQS * g + b) + m + 1)
                t = TPS * b + 2 * m
                bank = proj_ps[:, (k_at(n + 1), v_at(n))[m] % PROJ_BANKS, :]
                dve.tensor_tensor(acc[:, t:t + 2, :], bank.rearrange("p (t d) -> p t d", d=D),
                                  acc[:, t:t + 2, :], ALU.add).then_inc(o_added, 1)

            def features(g, j, n):
                at, u = (slice(None), j, n % 2, slice(None)), 2 * n + j
                dve.wait_ge(z_read, 2 * GROUP + 2 * STEPS * g + u + 1)
                dve.scalar_tensor_tensor(out=relu_z[:, j, :], in0=exp_z[:, j, :], scalar=1.0, in1=relu_z[:, j, :],
                                         op0=ALU.min, op1=ALU.add).then_inc(phi_step, 1)
                dve.wait_ge(phi_step, 4 * STEPS * g + 2 * u + 1)
                if j == 0:
                    dve.tensor_scalar(relu_z[:, 0, :], relu_z[:, 0, :], 10.0, None, ALU.min).then_inc(phi_step, 1)
                    return
                dve.tensor_scalar(phi_hi[at], relu_z[:, j, :], 10.0, None, ALU.min).then_inc(phi_step, 1)
                dve.wait_ge(phi_step, 4 * STEPS * g + 2 * u + 2)
                dve.scalar_tensor_tensor(out=phi_lo[at], in0=relu_z[:, j, :], scalar=10.0,
                                         in1=phi_hi[at].bitcast(F32), op0=ALU.min,
                                         op1=ALU.subtract).then_inc(phi_k_done, 1)

            def row_max(g, n, unit):
                dve.wait_ge(s_done, SU * (STEPS * g + n) + unit + 1)
                start = 0
                for i in S_UNITS[unit]:
                    last = dve.tensor_reduce(nmax[:, n % 2, i:i + 1],
                                             s_ps[:, (SU * n + unit) % S_BANKS, start:start + WIDTH[i]],
                                             AX.X, ALU.max, negate=True)
                    start += WIDTH[i]
                last.then_inc(max_done, 1)

            def local_max(g, n):
                dve.wait_ge(local_done, STEPS * g + n + 1)
                dve.tensor_reduce(nmax[:, n % 2, :],
                                  s_ps[:, LOCAL_BANK, :].rearrange("p (i k) -> p i k", k=P),
                                  AX.X, ALU.max, negate=True).then_inc(max_done, 1)

            def linear_weights(g, n, unit):
                dve.wait_ge(s_done, SU * (STEPS * g + n) + unit + 1)
                start = 0
                for i in S_UNITS[unit]:
                    last = dve.tensor_tensor_reduce(e[:, n % 2, E_AT[i]:E_AT[i] + WIDTH[i]],
                                                    s_ps[:, LINEAR_BANK[unit], start:start + WIDTH[i]],
                                                    block_mask[:, SEQ - WIDTH[i]:SEQ], 1.0, 0.0, ALU.mult, ALU.add,
                                                    den[:, n % 2, 1, i:i + 1])
                    start += WIDTH[i]
                last.then_inc(a_read, 1)

            def invert(g, n):
                dve.wait_ge(exp_done, S_BANKS + SU * (STEPS * g + n + 1))
                dve.reciprocal(rden[:, n % 2, 0, :], den[:, n % 2, 0, :]).then_inc(rden_done, 1)

            def invert_linear(g, n):
                at = (slice(None), n % 2, 1, slice(None))
                dve.wait_ge(a_read, SU + SU * (STEPS * g + n + 1))
                dve.tensor_scalar(den[at], den[at], DEN_EPS, None, ALU.max).then_inc(dve_step, 1)
                dve.wait_ge(dve_step, STEPS * g + n + 1)
                dve.reciprocal(rden[at], den[at]).then_inc(rden_done, 1)

            def invert_local(g, n):
                dve.wait_ge(exp_done, 1 + STEPS * g + n + 1)
                dve.reciprocal(rden[:, n % 2, 0, :], den[:, n % 2, 0, :]).then_inc(rlocal_done, 1)

            def turned_lo(g, n):
                for unit, tiles in enumerate(T_UNITS):
                    dve.wait_ge(t_hi, TU * (STEPS * g + n) + unit + 1)
                    at, w = turned_columns(tiles)
                    dve.tensor_tensor(pt_lo[:, at], t_ps[:, unit, 0:w], pt_hi[:, at].bitcast(F32),
                                      ALU.subtract).then_inc(t_split, 1)

            def out_lo(g, n):
                dve.wait_ge(ao_hi_done, STEPS * g + n + 1)
                h = n % GROUP
                dve.tensor_tensor(ao_lo[:, h, :], pv_ps[:, 0, :], ao_hi[:, h, :].bitcast(F32),
                                  ALU.subtract).then_inc(ao_split, 1)

            def has_v(n, last):
                return not last or v_unit(n)[0] < SEQS

            def has_out(n):
                return n % GROUP == 1 and n > 1

            def v_step(g, n, last):
                if not last or v_unit(n)[0] < SEQS:
                    v_part(g, *v_unit(n), v_at(n))
                elif n == NO_V:
                    dve.wait_ge(proj_split, PROJ_BANKS + 3 * STEPS * g + k_at(n + 1) + 1)
                    dve.sem_inc(proj_split, 1)

            def out_step(g, n):
                if n > 1 and n % GROUP == 1:
                    add_out(g, n, 0)
                    if n % STEPS == 1:
                        add_out(g, n, 1)

            def late_part(g, n, last):
                if n % GROUP == 2 and n % STEPS != 2:
                    add_out(g, n - 1, 1)
                if n >= 2 and (not last or n - 1 <= STEPS):
                    out_lo(g, n - 2)

            def softmax_step(g, n, last=False):
                scored = not last or n < STEPS
                projects = not last or n + 1 < STEPS
                if scored:
                    row_max(g, n, 0)
                late_part(g, n, last)
                if projects:
                    qk_part(g, 0, n + 1)
                if scored:
                    row_max(g, n, 1)
                    row_max(g, n, 2)
                if n >= 1 and (not last or n <= STEPS):
                    turned_lo(g, n - 1)
                if scored:
                    invert(g, n)
                if projects:
                    qk_part(g, 1, n + 1)
                v_step(g, n, last)
                out_step(g, n)

            def linear_step(g, n, last=False):
                scored = not last or n < STEPS
                projects = not last or n + 1 < STEPS
                late_part(g, n, last)
                if projects:
                    qk_part(g, 0, n + 1)
                if scored:
                    linear_weights(g, n, 0)
                if projects:
                    qk_part(g, 1, n + 1)
                if scored:
                    linear_weights(g, n, 1)
                    linear_weights(g, n, 2)
                    invert_linear(g, n)
                if projects:
                    features(g, 0, n + 1)
                if n >= 1 and (not last or n <= STEPS):
                    turned_lo(g, n - 1)
                if scored:
                    local_max(g, n)
                v_step(g, n, last)
                if projects:
                    features(g, 1, n + 1)
                if scored:
                    invert_local(g, n)
                out_step(g, n)

            for pos, unit in enumerate(FIRST_UNITS):
                if unit[0] == "v":
                    v_part(0, unit[1], unit[2], pos)
                else:
                    qk_part(0, "qk".index(unit[0]), 0)
                if linear and unit == ("k", 0):
                    features(0, 0, 0)
                    features(0, 1, 0)
            step = linear_step if linear else softmax_step
            step(0, 0)
            step(0, 1)
            if linear:
                dve.wait_ge(bias_added, SEQS)
            run_steps(dve, step)


def routing_phase(nc, tag, src, weight, hT_hi, hT_lo, gate_dram, ident, ident_bf, cwT, pieces):
    E1 = EXPERTS + 1
    with ExitStack() as ctx:
        new_sem = ctx.enter_context(phase_semaphores(nc))

        def sb(name, shape, dt=F32):
            return ctx.enter_context(nc.sbuf_tensor(f"{tag}_{name}", shape, dt))

        def sem(name):
            return new_sem(f"{tag}_{name}")

        z = sb("z", [P, TILES, D])
        ms = sb("ms", [P, TILES])
        rms_std = sb("rms_std", [P, TILES])
        rrms = sb("rrms", [P, TILES])
        squares = sb("squares", [P, TILES])
        gate = sb("gate", [P, KT, EXPERTS])
        gate_parts = sb("gate_parts", [P, KT, 2 * EXPERTS], F32R)
        lT = sb("lT", [2 * EXPERTS, 2, SEQ])
        logits = sb("logits", [P, TILES, EXPERTS])
        rowmax = sb("rowmax", [P, TILES])
        rowsum = sb("rowsum", [P, TILES])
        rsum = sb("rsum", [P, TILES])
        topsum = sb("topsum", [P, TILES])
        rtop = sb("rtop", [P, TILES])
        shifted = sb("shifted", [P, TILES, EXPERTS])
        ex = sb("ex", [P, TILES, EXPERTS])
        probs = sb("probs", [P, TILES, EXPERTS + 2])
        top8 = sb("top8", [P, TILES, 8])
        rest = sb("rest", [P, TILES, EXPERTS + 2])
        sel = sb("sel", [P, TILES, EXPERTS])
        cw = sb("cw", [P, TILES, EXPERTS])
        left1 = sb("left1", [P, TILES, EXPERTS])
        left2 = sb("left2", [P, TILES, EXPERTS])
        cw3 = sb("cw3", [P, TILES, CW_ROWS], BF16)
        BANKS = 3
        tp = ctx.enter_context(nc.psum_tensor(f"{tag}_tp", [P, BANKS, 512], F32))
        lT_ps = ctx.enter_context(nc.psum_tensor(f"{tag}_lT_ps", [2 * EXPERTS, 2, SEQ], F32))
        l_ps = ctx.enter_context(nc.psum_tensor(f"{tag}_l_ps", [P, TILES, 2 * EXPERTS], F32))
        cw_ps = ctx.enter_context(nc.psum_tensor(f"{tag}_cw_ps", [P, 2, 8 * P], BF16))

        loaded, gate_split, vec = sem("loaded"), sem("gate_split"), sem("vec")
        squared, squared_too = sem("squared"), sem("squared_too")
        ms_ready, rms_std_ready, rrms_ready, z_ready = (
            sem("ms_ready"), sem("rms_std_ready"), sem("rrms_ready"), sem("z_ready"))
        h_turned, hi_done = sem("h_turned"), sem("hi_done")
        split_done = sem("split_done")
        lT_done, lT_copied, logits_done = sem("lT_done"), sem("lT_copied"), sem("logits_done")
        shifted_done, exp_done, cw_ready, turned, copied = (
            sem("shifted_done"), sem("exp_done"), sem("cw_ready"), sem("turned"), sem("copied"))
        fetched = [sem(f"fetched_{i}") for i in range(len(pieces))]
        w_hi_done = sem("w_hi_done")
        block = ctx.enter_context(nc.Block())
        HALF = TILES // 2

        @block.sync
        def _(sp):
            sp.dma_start(gate[:, :, :], gate_dram).then_inc(loaded, 16)
            fetch_weights(sp, pieces, fetched)

        @block.gpsimd
        def _(pool):
            split_weights(pool, pieces, fetched, w_hi_done)

        @block.tensor
        def _(pe):
            def gate_products(b):
                pe.wait_ge(split_done, BANKS + KT * b + KT)
                if b >= 2:
                    pe.wait_ge(lT_copied, b - 1)
                at = slice(SEQ * b, SEQ * b + SEQ)
                for k in range(KT):
                    pe.matmul(lT_ps[:, b % 2, :], gate_parts[:, k, :], hT_hi[:, k, at], start=k == 0, stop=False,
                              skip_group_check=True)
                    last = pe.matmul(lT_ps[0:EXPERTS, b % 2, :], gate_parts[:, k, 0:EXPERTS], hT_lo[:, k, at],
                                     start=False, stop=k == KT - 1, skip_group_check=True)
                last.then_inc(lT_done, 1)

            def turn_logits(b):
                pe.wait_ge(lT_copied, b + 1)
                for i in range(TPS):
                    last = pe.transpose(l_ps[:, TPS * b + i, :], lT[:, b % 2, P * i:P * i + P],
                                        ident[0:2 * EXPERTS, 0:2 * EXPERTS])
                last.then_inc(logits_done, 1)

            pe.wait_ge(gate_split, 2)
            for b in range(SEQS + 2):
                if b < SEQS:
                    pe.wait_ge(z_ready, b + 1)
                    for k in range(KT):
                        n = KT * b + k
                        pe.wait_ge(split_done, n + 1)
                        for i in range(TPS):
                            last = pe.transpose(tp[:, n % BANKS, P * i:P * i + P],
                                                z[:, TPS * b + i, P * k:P * k + P], ident[:, :])
                        last.then_inc(h_turned, 1)
                if 0 <= b - 1 < SEQS:
                    gate_products(b - 1)
                if b >= 2:
                    turn_logits(b - 2)
            pe.wait_ge(cw_ready, 1)
            for t in range(TILES):
                last = pe.transpose(cw_ps[0:CW_ROWS, t // 8, P * (t % 8):P * (t % 8) + P], cw3[:, t, :], ident_bf[:, :])
            last.then_inc(turned, 1)

        @block.scalar
        def _(act):
            for t in range(HALF):
                act.activation(z[:, t, :], src[:, t, :], ACT.Square, accum_out=squares[:, t:t + 1]).then_inc(squared, 1)
            act.wait_ge(ms_ready, 1)
            act.activation(rms_std[:, :], ms[:, :], ACT.Sqrt).then_inc(rms_std_ready, 1)
            for b in range(SEQS + 1):
                if b < SEQS:
                    for k in range(KT):
                        n = KT * b + k
                        act.wait_ge(h_turned, n + 1)
                        act.activation(hT_hi[:, k, SEQ * b:SEQ * b + SEQ], tp[:, n % BANKS, :], ACT.Copy,
                                       scale=weight[:, k:k + 1]).then_inc(hi_done, 1)
                if b >= 1:
                    act.wait_ge(lT_done, b)
                    if b >= 3:
                        act.wait_ge(logits_done, b - 2)
                    act.activation(lT[:, (b - 1) % 2, :], lT_ps[:, (b - 1) % 2, :], ACT.Copy).then_inc(lT_copied, 1)
            act.wait_ge(shifted_done, 1)
            act.activation(ex[:, :, :], shifted[:, :, :], ACT.Exp).then_inc(exp_done, 1)

        @block.vector
        def _(dve):
            def spread(column):
                return column[:, :].unsqueeze(2).to_broadcast([P, TILES, EXPERTS])

            def scaled(b):
                for t in range(TPS * b, TPS * b + TPS):
                    last = dve.tensor_scalar(z[:, t, :], src[:, t, :], rrms[:, t:t + 1], None, ALU.mult)
                last.then_inc(z_ready, 1)

            dve.sem_inc(split_done, BANKS)
            for t in range(HALF, TILES):
                dve.tensor_tensor_reduce(z[:, t, :], src[:, t, :], src[:, t, :], 1.0, 0.0, ALU.mult, ALU.add,
                                         squares[:, t:t + 1]).then_inc(squared_too, 1)
            dve.wait_ge(squared, HALF)
            dve.wait_ge(squared_too, HALF)
            dve.tensor_scalar(ms[:, :], squares[:, :], 1.0 / D, RMS_EPS, ALU.mult, ALU.add).then_inc(ms_ready, 1)
            dve.wait_ge(loaded, 16)
            dve.tensor_copy(gate_parts[:, :, 0:EXPERTS], gate[:, :, :]).then_inc(gate_split, 1)
            dve.wait_ge(gate_split, 1)
            dve.tensor_tensor(gate_parts[:, :, EXPERTS:2 * EXPERTS], gate[:, :, :],
                              gate_parts[:, :, 0:EXPERTS].bitcast(F32), ALU.subtract).then_inc(gate_split, 1)
            dve.memset(probs[:, :, EXPERTS:EXPERTS + 1], -1.0)
            dve.memset(probs[:, :, EXPERTS + 1:EXPERTS + 2], -2.0)
            dve.memset(cw3[:, :, EXPERTS:E1], 1.0)
            dve.memset(cw3[:, :, E1 + EXPERTS:2 * E1], 0.0)
            dve.memset(cw3[:, :, 2 * E1 + EXPERTS:3 * E1], 0.0).then_inc(vec, 1)
            dve.wait_ge(rms_std_ready, 1)
            dve.reciprocal(rrms[:, :], rms_std[:, :]).then_inc(rrms_ready, 1)
            dve.wait_ge(rrms_ready, 1)
            scaled(0)
            for b in range(SEQS):
                if b + 1 < SEQS:
                    scaled(b + 1)
                for k in range(KT):
                    n = KT * b + k
                    at = slice(SEQ * b, SEQ * b + SEQ)
                    dve.wait_ge(hi_done, n + 1)
                    dve.scalar_tensor_tensor(out=hT_lo[:, k, at], in0=tp[:, n % BANKS, :], scalar=weight[:, k:k + 1],
                                             in1=hT_hi[:, k, at].bitcast(F32), op0=ALU.mult,
                                             op1=ALU.subtract).then_inc(split_done, 1)
            dve.wait_ge(logits_done, SEQS)
            dve.tensor_copy(left1[:, :, :], l_ps[:, :, 0:EXPERTS]).then_inc(copied, 1)
            dve.wait_ge(copied, 1)
            dve.tensor_tensor(logits[:, :, :], l_ps[:, :, EXPERTS:2 * EXPERTS], left1[:, :, :],
                              ALU.add).then_inc(copied, 1)
            dve.wait_ge(copied, 2)
            dve.tensor_reduce(rowmax[:, :], logits[:, :, :], AX.X, ALU.max).then_inc(vec, 1)
            dve.wait_ge(vec, 2)
            dve.tensor_tensor(shifted[:, :, :], logits[:, :, :], spread(rowmax), ALU.subtract).then_inc(shifted_done, 1)
            dve.wait_ge(exp_done, 1)
            dve.tensor_reduce(rowsum[:, :], ex[:, :, :], AX.X, ALU.add).then_inc(vec, 1)
            dve.wait_ge(vec, 3)
            dve.reciprocal(rsum[:, :], rowsum[:, :]).then_inc(vec, 1)
            dve.wait_ge(vec, 4)
            dve.tensor_tensor(probs[:, :, 0:EXPERTS], ex[:, :, :], spread(rsum), ALU.mult).then_inc(vec, 1)
            dve.wait_ge(vec, 5)
            for t in range(TILES):
                last = dve.max(top8[:, t, :], probs[:, t, 0:EXPERTS])
            last.then_inc(vec, 1)
            dve.wait_ge(vec, 6)
            dve.memset(top8[:, :, TOPK:TOPK + 1], -1.0).then_inc(vec, 1)
            dve.memset(top8[:, :, TOPK + 1:TOPK + 2], -2.0).then_inc(vec, 1)
            dve.wait_ge(vec, 8)
            for t in range(TILES):
                last = dve.match_replace(rest[:, t, :], top8[:, t, :], probs[:, t, :], 0.0)
            last.then_inc(vec, 1)
            dve.wait_ge(vec, 9)
            dve.tensor_tensor(sel[:, :, :], probs[:, :, 0:EXPERTS], rest[:, :, 0:EXPERTS],
                              ALU.subtract).then_inc(vec, 1)
            dve.wait_ge(vec, 10)
            dve.tensor_reduce(topsum[:, :], sel[:, :, :], AX.X, ALU.add).then_inc(vec, 1)
            dve.wait_ge(vec, 11)
            dve.reciprocal(rtop[:, :], topsum[:, :]).then_inc(vec, 1)
            dve.wait_ge(vec, 12)
            dve.tensor_tensor(cw[:, :, :], sel[:, :, :], spread(rtop), ALU.mult).then_inc(vec, 1)
            dve.wait_ge(vec, 13)
            parts = [cw3[:, :, E1 * i:E1 * i + EXPERTS] for i in range(3)]
            dve.tensor_copy(parts[0], cw[:, :, :]).then_inc(vec, 1)
            dve.wait_ge(vec, 14)
            dve.tensor_tensor(left1[:, :, :], cw[:, :, :], parts[0], ALU.subtract).then_inc(vec, 1)
            dve.wait_ge(vec, 15)
            dve.tensor_copy(parts[1], left1[:, :, :]).then_inc(vec, 1)
            dve.wait_ge(vec, 16)
            dve.tensor_tensor(left2[:, :, :], left1[:, :, :], parts[1], ALU.subtract).then_inc(vec, 1)
            dve.wait_ge(vec, 17)
            dve.tensor_copy(parts[2], left2[:, :, :]).then_inc(cw_ready, 1)
            dve.wait_ge(turned, 1)
            for i in range(2):
                dve.tensor_copy(cwT[:, 8 * P * i:8 * P * i + 8 * P], cw_ps[0:CW_ROWS, i, :]).then_inc(copied, 1)


def expert_weights(ctx, nc, tag, sel_dram, w_dram):
    up_dram, down_dram = w_dram
    sel_words = sel_dram.bitcast(F32)

    def sb(name, shape, dt=F32):
        return ctx.enter_context(nc.sbuf_tensor(f"{tag}_{name}", shape, dt))

    raw_up = sb("raw_up", [P, CPG, 2, KT, P])
    raw_dn = sb("raw_dn", [P, CPG, D])
    up_hi, up_lo = (sb(f"up_{s}", [P, CPG, 2, KT, P], F32R) for s in ("hi", "lo"))
    dn_hi, dn_lo = (sb(f"dn_{s}", [P, CPG, D], F32R) for s in ("hi", "lo"))
    sel_bf = sb("sel_bf", [CW_ROWS, CPG, P], BF16)

    def loads(g, c):
        up = [(raw_up[:, c, j, :, :], up_dram[j][:, :, bass.ds(g * (CPG * P) + c * P, P)]) for j in range(2)]
        return up + [(raw_dn[:, c, :], down_dram[bass.ds(g * (CPG * P) + c * P, P), :])]

    def sel_load(g, c):
        return (sel_bf[:, c, :].bitcast(F32), sel_words[:, bass.ds(g * (CPG * P // 2) + c * P // 2, P // 2)])

    def views(c):
        return [(raw_up[:, c], up_hi[:, c], up_lo[:, c]), (raw_dn[:, c, :], dn_hi[:, c, :], dn_lo[:, c, :])]

    def first_pieces():
        return [(loads(0, c) + [sel_load(0, c)], views(c)) for c in range(FIRST_CHUNKS)]

    return (up_hi, up_lo, dn_hi, dn_lo, sel_bf), (loads, sel_load, views), first_pieces()


FIRST_CHUNKS = CPG - 1


def experts_phase(nc, tag, tT_hi, tT_lo, cwT, weights, y, x, out_dram):
    (up_hi, up_lo, dn_hi, dn_lo, sel_bf), (w_loads, sel_load, w_views) = weights
    with ExitStack() as ctx:
        new_sem = ctx.enter_context(phase_semaphores(nc))

        def sb(name, shape, dt=F32):
            return ctx.enter_context(nc.sbuf_tensor(f"{tag}_{name}", shape, dt))

        def ps(name, banks):
            return ctx.enter_context(nc.psum_tensor(f"{tag}_{name}", [P, banks, 512], F32))

        def sem(name):
            return new_sem(f"{tag}_{name}")

        silu = sb("silu", [P, 2, SEQ])
        prod = sb("prod", [P, 2, SEQ])
        hh = sb("hh", [P, 2, SEQ])
        hh_hi, hh_lo = (sb(f"hh_{s}", [P, 2, SEQ], F32R) for s in ("hi", "lo"))
        g_ps, u_ps, cw_ps, dn_ps = ps("g_ps", 2), ps("u_ps", 2), ps("cw_ps", 2), ps("dn_ps", 2)

        raw_loaded = [sem(f"raw_{c}") for c in range(CPG)]
        sel_loaded = [sem(f"sel_{c}") for c in range(CPG)]
        w_hi_done = sem("w_hi_done")
        w_split = sem("w_split")
        up_done = sem("up_done")
        silu_done = sem("silu_done")
        prod_done = sem("prod_done")
        gated = sem("gated")
        hh_hi_done = sem("hh_hi_done")
        hh_split = sem("hh_split")
        dn_done = sem("dn_done")
        y_added = sem("y_added")
        x_added = sem("x_added")
        stored = sem("stored")
        block = ctx.enter_context(nc.Block())

        @block.sync
        def _(sp):
            def load(g, c):
                sp.wait_ge(w_split, CPG * g + c + 1)
                for dst, src_dram in w_loads(g, c):
                    sp.dma_start(dst, src_dram).then_inc(raw_loaded[c], 16)

            def load_sel(g, c):
                sp.wait_ge(dn_done, UNITS * g + CPG * (SEQS - 1) + c + 1)
                dst, src_dram = sel_load(g, c)
                sp.dma_start(dst, src_dram).then_inc(sel_loaded[c], 16)

            for c in range(FIRST_CHUNKS):
                sp.sem_inc(raw_loaded[c], 48)
                sp.sem_inc(sel_loaded[c], 16)
            for c in range(FIRST_CHUNKS, CPG):
                load(0, c)
                load_sel(0, c)
            with sp.Fori(1, CHUNK_GROUPS) as g:
                for c in range(CPG):
                    load(g, c)
                for c in range(CPG):
                    load_sel(g, c)
            if out_dram is not None:
                for b in range(SEQS):
                    sp.wait_ge(x_added, b + 1)
                    sp.dma_start(out_dram[:, TPS * b:TPS * b + TPS, :],
                                 x[:, TPS * b:TPS * b + TPS, :]).then_inc(stored, 16)
                sp.wait_ge(stored, 16 * SEQS)

        @block.gpsimd
        def _(pool):
            pool.sem_inc(w_split, CPG + FIRST_CHUNKS)

            def weights_lo(g, c):
                pool.wait_ge(w_hi_done, CPG * g + c + 1)
                for raw, hi, lo in w_views(c):
                    last = pool.tensor_tensor(lo, raw, hi.bitcast(F32), ALU.subtract)
                last.then_inc(w_split, 1)

            for c in range(FIRST_CHUNKS, CPG):
                weights_lo(0, c)
            with pool.Fori(1, CHUNK_GROUPS) as g:
                for c in range(CPG):
                    weights_lo(g, c)

        @block.tensor
        def _(pe):
            pe.sem_inc(dn_done, UNITS)

            def up(g, k):
                b, c = divmod(k % UNITS, CPG)
                if b == 0:
                    pe.wait_ge(w_split, CPG + CPG * (g + k // UNITS) + c + 1)
                    pe.wait_ge(sel_loaded[c], 16 * (g + k // UNITS + 1))
                pe.wait_ge(gated, UNITS * g + k + 1)
                at = slice(SEQ * b, SEQ * b + SEQ)
                for j, bank in enumerate((g_ps, u_ps)):
                    for kt in range(KT):
                        product(pe, bank[:, k % 2, :], up_hi[:, c, j, kt, :], up_lo[:, c, j, kt, :],
                                tT_hi[:, kt, at], tT_lo[:, kt, at], kt == 0, kt == KT - 1)
                pe.matmul(cw_ps[:, k % 2, :], sel_bf[:, c, :], cwT[:, at], start=True, stop=True).then_inc(up_done, 1)

            def down(g, k):
                b, c = divmod(k, CPG)
                pe.wait_ge(hh_split, UNITS * g + k + 1)
                if c == 0:
                    pe.wait_ge(y_added, 2 * SEQS * g + 2 * b + 2)
                for t in range(TPS):
                    at = slice(P * t, P * t + P)
                    last = product(pe, dn_ps[:, t // 2, D * (t % 2):D * (t % 2) + D], hh_hi[:, k % 2, at],
                                   hh_lo[:, k % 2, at], dn_hi[:, c, :], dn_lo[:, c, :],
                                   c == 0 and t % 2 == 0, c == CPG - 1, shared_bank=True)
                last.then_inc(dn_done, 1)

            up(0, 0)
            with pe.Fori(0, CHUNK_GROUPS - 1) as g:
                for k in range(UNITS):
                    up(g, k + 1)
                    down(g, k)
            for k in range(UNITS):
                if k + 1 < UNITS:
                    up(CHUNK_GROUPS - 1, k + 1)
                down(CHUNK_GROUPS - 1, k)

        @block.scalar
        def _(act):
            def weights_hi(g, c):
                act.wait_ge(raw_loaded[c], 48 * (g + 1))
                act.wait_ge(dn_done, UNITS * g + CPG * (SEQS - 1) + c + 1)
                for raw, hi, _ in w_views(c):
                    last = act.activation(hi, raw, ACT.Copy)
                last.then_inc(w_hi_done, 1)

            def unit(g, k, last=False):
                act.wait_ge(up_done, UNITS * g + k + 1)
                act.activation(silu[:, k % 2, :], g_ps[:, k % 2, :], ACT.Silu).then_inc(silu_done, 1)
                act.wait_ge(gated, 2 + UNITS * g + k + 1)
                act.activation(hh_hi[:, k % 2, :], hh[:, k % 2, :], ACT.Copy).then_inc(hh_hi_done, 1)
                if k == 0:
                    weights_hi(g, CPG - 1)
                elif k > UNITS - CPG and not last:
                    weights_hi(g + 1, k - (UNITS - CPG) - 1)

            act.sem_inc(w_hi_done, FIRST_CHUNKS)
            with act.Fori(0, CHUNK_GROUPS - 1) as g:
                for k in range(UNITS):
                    unit(g, k)
            for k in range(UNITS):
                unit(CHUNK_GROUPS - 1, k, last=True)

        @block.vector
        def _(dve):
            dve.sem_inc(gated, 2)
            dve.sem_inc(y_added, 2)

            def add_down(g, b, m):
                t = TPS * b + 2 * m
                dve.tensor_tensor(y[:, t:t + 2, :], dn_ps[:, m, :].rearrange("p (t d) -> p t d", d=D),
                                  y[:, t:t + 2, :], ALU.add).then_inc(y_added, 1)

            def unit(g, k, last=False):
                n, b = UNITS * g + k, k // CPG - 1
                runs = not last or k < UNITS
                adds = k % CPG == 0 and k > 0
                if runs:
                    dve.wait_ge(silu_done, n + 1)
                    dve.tensor_tensor(prod[:, k % 2, :], u_ps[:, k % 2, :], silu[:, k % 2, :],
                                      ALU.mult).then_inc(prod_done, 1)
                    dve.wait_ge(prod_done, n + 1)
                    dve.tensor_tensor(hh[:, k % 2, :], cw_ps[:, k % 2, :], prod[:, k % 2, :],
                                      ALU.mult).then_inc(gated, 1)
                if adds:
                    dve.wait_ge(dn_done, UNITS + n)
                    add_down(g, b, 0)
                if runs:
                    dve.wait_ge(hh_hi_done, n + 1)
                    dve.tensor_tensor(hh_lo[:, k % 2, :], hh[:, k % 2, :], hh_hi[:, k % 2, :].bitcast(F32),
                                      ALU.subtract).then_inc(hh_split, 1)
                if adds:
                    add_down(g, b, 1)
                    if last:
                        at = slice(TPS * b, TPS * b + TPS)
                        dve.wait_ge(y_added, 2 + 2 * SEQS * g + 2 * b + 2)
                        dve.scalar_tensor_tensor(out=x[:, at, :], in0=y[:, at, :], scalar=0.5, in1=x[:, at, :],
                                                 op0=ALU.mult, op1=ALU.add).then_inc(x_added, 1)

            unit(0, 0)
            with dve.Fori(0, CHUNK_GROUPS - 1) as g:
                for k in range(1, UNITS + 1):
                    unit(g, k)
            for k in range(1, UNITS + 1):
                unit(CHUNK_GROUPS - 1, k, last=True)


def macaron_kernel(nc, x_in, Wq, Wk, Wv, phi_in, Wo, bo_in, ln1_in, ln2_in, wq, wk, wv, wo,
                   gate_w, eg_w, eu_w, ed_w, ident_in, ident_bf_in, causal_in, local_in, block_mask_in, sel_in, out):
    with ExitStack() as ctx:
        def sb(name, shape, dt=F32):
            return ctx.enter_context(nc.sbuf_tensor(name, shape, dt))

        ident = sb("ident", [P, P])
        ident_bf = sb("ident_bf", [P, P], BF16)
        causal_bf = sb("causal_bf", [P, 2 * P], BF16)
        ln_w = sb("ln_w", [P, 2, KT])
        x = sb("x", [P, TILES, D])
        hT_hi, hT_lo = (sb(f"hT_{s}", [P, KT, TOKENS], F32R) for s in ("hi", "lo"))

        def by_k(w):
            return w.rearrange("(k p) n -> p k n", p=P)

        def by_token(a):
            return a.rearrange("(t p) d -> p t d", p=P)

        attn_w = (by_k(Wq), by_k(Wk), by_k(Wv), by_k(Wo))
        ffn_w = (by_k(wq), by_k(wk), by_k(wv), by_k(wo))
        up_w = ((by_k(eg_w), by_k(eu_w)), ed_w)
        x_loads = [(x[:, TPS * b:TPS * b + TPS, :], by_token(x_in)[:, TPS * b:TPS * b + TPS, :]) for b in range(SEQS)]
        first_loads = [(ident[:, :], ident_in), (ident_bf[:, :], ident_bf_in),
                       (causal_bf[:, :], causal_in), (ln_w[:, 0, :], ln1_in), (ln_w[:, 1, :], ln2_in)]

        def ffn(tag, x_loads, loads, out_dram):
            with ExitStack() as inner:
                def sbi(name, shape, dt=F32):
                    return inner.enter_context(nc.sbuf_tensor(f"{tag}_{name}", shape, dt))

                y = sbi("y", [P, TILES, D])
                with ExitStack() as attn:
                    *w, first = attention_weights(attn, nc, f"{tag}at", ffn_w, None)
                    norm_phase(nc, f"{tag}n1", x, y, ln_w[:, 0, :], hT_hi, hT_lo, ident, first,
                               x_loads=x_loads, loads=loads)
                    attention_phase(nc, f"{tag}at", False, hT_hi, hT_lo, y, w, (ident, ident_bf, causal_bf, None, None, None))
                cwT = sbi("cwT", [CW_ROWS, TOKENS], BF16)
                *w, first = expert_weights(inner, nc, f"{tag}ex", sel_in, up_w)
                routing_phase(nc, f"{tag}rt", y, ln_w[:, 1, :], hT_hi, hT_lo, by_k(gate_w), ident, ident_bf, cwT, first)
                experts_phase(nc, f"{tag}ex", hT_hi, hT_lo, cwT, w, y, x, out_dram)

        ffn("f1", x_loads, first_loads, None)
        with ExitStack() as inner:
            def sbi(name, shape, dt=F32):
                return inner.enter_context(nc.sbuf_tensor(name, shape, dt))

            local_bf = sbi("local_bf", [P, SEQ], BF16)
            block_mask = sbi("block_mask", [P, SEQ])
            bo = sbi("bo", [P, D])
            *w, first = attention_weights(inner, nc, "aa", attn_w, phi_in)
            norm_phase(nc, "an", x, None, None, hT_hi, hT_lo, ident, first,
                       loads=[(local_bf[:, :], local_in), (block_mask[:, :], block_mask_in),
                              (bo[:, :], bo_in)])
            attention_phase(nc, "aa", True, hT_hi, hT_lo, x, w, (ident, ident_bf, None, local_bf, block_mask, bo))
        ffn("f2", None, None, by_token(out))


def kernel(**inputs):
    import ml_dtypes
    import numpy as np
    import concourse.bacc as bacc
    from concourse.bass_utils import run_bass_kernel_spmd

    def arr(name):
        return np.asarray(inputs[name])

    def experts_side_by_side(routed, shared):
        flat = np.concatenate([routed.reshape(EXPERTS * INNER, D), shared], axis=0)
        return np.concatenate([flat, np.zeros((CHUNKS * P - flat.shape[0], D), flat.dtype)], axis=0)

    bf = ml_dtypes.bfloat16
    below = np.tril(np.ones((P, P), bool))
    hidden = -1e9 / SCALE
    causal = np.tile(np.where(below, 0.0, hidden), (1, 2)).astype(bf)
    same = np.kron(np.eye(P // 64), np.ones((64, 64))).astype(bool)
    local = np.tile(np.where(same, 0.0, hidden), (1, TPS)).astype(bf)
    block_mask = np.ones((P, SEQ), np.float32)
    block_mask[:64, SEQ - 64:] = 0.0
    sel = np.zeros((CW_ROWS, CHUNKS * P), np.float32)
    for c in range(EXPERTS * INNER + SHARED):
        for part in range(3):
            sel[part * (EXPERTS + 1) + min(c // INNER, EXPERTS), c] = 1.0

    arrays = {
        "x_in": arr("L0_attn_x").reshape(TOKENS, D),
        "Wq": arr("L0_attn_Wq"), "Wk": arr("L0_attn_Wk"), "Wv": arr("L0_attn_Wv"),
        "phi_in": np.stack([arr(f"L0_attn_phi_{s}").reshape(HEADS, HD).T for s in ("scale", "bias")],
                           axis=2).reshape(HD, 2 * HEADS),
        "Wo": arr("L0_attn_Wo"),
        "bo_in": np.ascontiguousarray(np.broadcast_to(arr("L0_attn_bo"), (P, D))),
        "ln1_in": np.ascontiguousarray(arr("L0_ffn_ln1_w").reshape(KT, P).T),
        "ln2_in": np.ascontiguousarray(arr("L0_ffn_ln2_w").reshape(KT, P).T),
        "wq": arr("L0_ffn_wq"), "wk": arr("L0_ffn_wk"), "wv": arr("L0_ffn_wv"), "wo": arr("L0_ffn_wo"),
        "gate_w": np.ascontiguousarray(arr("L0_ffn_gate_w").T),
        "eg_w": np.ascontiguousarray(experts_side_by_side(arr("L0_ffn_eg_w"), arr("L0_ffn_sg_w")).T),
        "eu_w": np.ascontiguousarray(experts_side_by_side(arr("L0_ffn_eu_w"), arr("L0_ffn_su_w")).T),
        "ed_w": experts_side_by_side(arr("L0_ffn_ed_w").transpose(0, 2, 1), arr("L0_ffn_sd_w").T),
        "ident_in": np.eye(P, dtype=np.float32), "ident_bf_in": np.eye(P).astype(bf),
        "causal_in": causal, "local_in": local, "block_mask_in": block_mask, "sel_in": sel.astype(bf),
    }
    nc = bacc.Bacc("TRN2", target_bir_lowering=False, num_devices=1)
    args = [nc.dram_tensor(name, a.shape, mybir.dt.from_np(a.dtype), kind="ExternalInput").ap()
            for name, a in arrays.items()]
    args.append(nc.dram_tensor("out", (TOKENS, D), F32, kind="ExternalOutput").ap())
    macaron_kernel(nc, *args)
    r = run_bass_kernel_spmd(nc, [{k: np.ascontiguousarray(a) for k, a in arrays.items()}], core_ids=[0])
    return r.results[0]["out"].reshape(SEQS, SEQ, D)
```
